# Optimizing a Trainium2 kernel written in Bass

```python
import numpy as np
import jax
import jax.numpy as jnp

def _softmax(x, axis=-1):
    return jax.nn.softmax(x, axis=axis)

def _gelu(x):
    return jax.nn.gelu(x, approximate=True)

def _silu(x):
    return jax.nn.silu(x)

def _sigmoid(x):
    return jax.nn.sigmoid(x)

def _layernorm(x, axis=-1, eps=1e-05):
    m = jnp.mean(x, axis=axis, keepdims=True)
    v = jnp.var(x, axis=axis, keepdims=True)
    return (x - m) / jnp.sqrt(v + eps)

def _scatter_add(tgt, idx, src, axis=0):
    return tgt.at[idx].add(src)

def _segment_sum(src, seg, n):
    return jax.ops.segment_sum(src, seg, n)
kernel_name = 'mk_gnn_ffn_d1_gnn_r32_dff2ea'

def setup_inputs(seed: int=0):
    np.random.seed(seed)
    _w = jnp.asarray

    def _rec_inputs():
        import jax
        import jax.numpy as jnp
        _gk = jax.random.key(seed)
        x = -6.415e-05 + 1 * jax.random.normal(jax.random.fold_in(_gk, 1), (625, 512), jnp.float32)
        src = jax.random.randint(jax.random.fold_in(_gk, 2), (10000,), 0, 625, jnp.int32)
        dst = jax.random.randint(jax.random.fold_in(_gk, 3), (10000,), 0, 625, jnp.int32)
        _o = jnp.argsort(dst, stable=True)
        src = src[_o]
        dst = dst[_o]
        edge_type_8 = jax.random.randint(jax.random.fold_in(_gk, 12), (10000,), 0, 8, jnp.int32)
        return (x, src, dst, edge_type_8)
    x, src, dst, edge_type_8 = _rec_inputs()

    def _L0_gnn_setup():
        import jax, jax.numpy as jnp
        import numpy as np
        N = 625
        E = 5000
        D = 512
        R = 8
        key = jax.random.key(seed)
        ks = jax.random.split(key, 8)
        inp = {'input': jax.random.normal(ks[0], (N, D), dtype=jnp.float32), 'heads': jax.random.randint(ks[1], (E,), 0, N), 'tails': jax.random.randint(ks[2], (E,), 0, N), 'rel': jax.random.randint(ks[3], (E,), 0, R), 'W_self': jax.random.normal(ks[4], (D, D), dtype=jnp.float32) * 0.03, 'b_self': jnp.zeros((D,), dtype=jnp.float32), 'W_rel': jax.random.normal(ks[5], (2 * R, D, D), dtype=jnp.float32) * 0.03, 'b_rel': jnp.zeros((2 * R, D), dtype=jnp.float32)}
        return inp
    _L0_gnn_all = _L0_gnn_setup()
    _L0_gnn_in = {k: v for k, v in _L0_gnn_all.items() if k in ('W_self', 'b_self', 'W_rel', 'b_rel')}
    del _L0_gnn_all

    def _L0_ffn_setup():
        import jax, jax.numpy as jnp
        import numpy as np
        G, H, DQK, DV, L, D_IN = (8, 16, 128, 128, 100, 512)
        FF = D_IN
        LSW = 1.0

        def _l2norm(x, d):
            n = jnp.maximum(jnp.linalg.norm(x, axis=-1, keepdims=True), 1e-12)
            return x / n * d ** 0.5
        key = jax.random.key(seed)
        ks = jax.random.split(key, 16)
        s = 0.02
        inp = {'x': jax.random.normal(ks[0], (4, 64, D_IN), dtype=jnp.float32), 'gamma_norm': jnp.ones((D_IN,), jnp.float32), 'Wq_w': jax.random.normal(ks[1], (D_IN, G * H * DQK), jnp.float32) * s, 'Wq_b': jnp.zeros((G * H * DQK,), jnp.float32), 'Wkv_w': jax.random.normal(ks[2], (D_IN, G * (DQK + DV)), jnp.float32) * s, 'Wkv_b': jnp.zeros((G * (DQK + DV),), jnp.float32), 'aw1_w': jax.random.normal(ks[3], (G * DQK, L), jnp.float32) * s, 'aw1_b': jnp.zeros((L,), jnp.float32), 'aw2_w': jax.random.normal(ks[4], (L, L), jnp.float32) * s, 'aw2_b': jnp.zeros((L,), jnp.float32), 'wz_g1': jnp.ones((G * H * DV,), jnp.float32), 'wz_w1': jax.random.normal(ks[5], (G * H * DV, 2 * FF), jnp.float32) * s, 'wz_b1': jnp.zeros((2 * FF,), jnp.float32), 'wz_g2': jnp.ones((2 * FF,), jnp.float32), 'wz_w2': jax.random.normal(ks[6], (2 * FF, FF), jnp.float32) * s, 'wz_b2': jnp.zeros((FF,), jnp.float32)}
        return inp
    _L0_ffn_all = _L0_ffn_setup()
    _L0_ffn_in = {k: v for k, v in _L0_ffn_all.items() if k in ('gamma_norm', 'Wq_w', 'Wq_b', 'Wkv_w', 'Wkv_b', 'aw1_w', 'aw1_b', 'aw2_w', 'aw2_b', 'wz_g1', 'wz_w1', 'wz_b1', 'wz_g2', 'wz_w2', 'wz_b2')}
    del _L0_ffn_all
    return {'x': x, 'src': src, 'dst': dst, 'edge_type_8': edge_type_8, 'L0_gnn_W_self': _L0_gnn_in['W_self'], 'L0_gnn_b_self': _L0_gnn_in['b_self'], 'L0_gnn_W_rel': _L0_gnn_in['W_rel'], 'L0_gnn_b_rel': _L0_gnn_in['b_rel'], 'L0_ffn_gamma_norm': _L0_ffn_in['gamma_norm'], 'L0_ffn_Wq_w': _L0_ffn_in['Wq_w'], 'L0_ffn_Wq_b': _L0_ffn_in['Wq_b'], 'L0_ffn_Wkv_w': _L0_ffn_in['Wkv_w'], 'L0_ffn_Wkv_b': _L0_ffn_in['Wkv_b'], 'L0_ffn_aw1_w': _L0_ffn_in['aw1_w'], 'L0_ffn_aw1_b': _L0_ffn_in['aw1_b'], 'L0_ffn_aw2_w': _L0_ffn_in['aw2_w'], 'L0_ffn_aw2_b': _L0_ffn_in['aw2_b'], 'L0_ffn_wz_g1': _L0_ffn_in['wz_g1'], 'L0_ffn_wz_w1': _L0_ffn_in['wz_w1'], 'L0_ffn_wz_b1': _L0_ffn_in['wz_b1'], 'L0_ffn_wz_g2': _L0_ffn_in['wz_g2'], 'L0_ffn_wz_w2': _L0_ffn_in['wz_w2'], 'L0_ffn_wz_b2': _L0_ffn_in['wz_b2']}

def reference(x, src, dst, edge_type_8, L0_gnn_W_self, L0_gnn_b_self, L0_gnn_W_rel, L0_gnn_b_rel, L0_ffn_gamma_norm, L0_ffn_Wq_w, L0_ffn_Wq_b, L0_ffn_Wkv_w, L0_ffn_Wkv_b, L0_ffn_aw1_w, L0_ffn_aw1_b, L0_ffn_aw2_w, L0_ffn_aw2_b, L0_ffn_wz_g1, L0_ffn_wz_w1, L0_ffn_wz_b1, L0_ffn_wz_g2, L0_ffn_wz_w2, L0_ffn_wz_b2):
    import jax
    import jax.numpy as jnp

    def _L0_gnn_ref(input, heads, tails, rel, W_self, b_self, W_rel, b_rel):
        import jax, jax.numpy as jnp
        import numpy as np
        N = 625
        E = 5000
        D = 512
        R = 8
        h_self = input @ W_self.T + b_self
        H_all = jnp.einsum('rod,nd->rno', W_rel, input) + b_rel[:, None, :]
        msg_to_heads = H_all[rel, tails]
        msg_to_tails = H_all[rel + R, heads]
        agg = jax.ops.segment_sum(msg_to_heads, heads, num_segments=N) + jax.ops.segment_sum(msg_to_tails, tails, num_segments=N)
        return jax.nn.relu(h_self + agg)

    def _L0_ffn_ref(x, gamma_norm, Wq_w, Wq_b, Wkv_w, Wkv_b, aw1_w, aw1_b, aw2_w, aw2_b, wz_g1, wz_w1, wz_b1, wz_g2, wz_w2, wz_b2):
        import jax, jax.numpy as jnp
        import numpy as np
        G, H, DQK, DV, L, D_IN = (8, 16, 128, 128, 100, 512)
        FF = D_IN
        LSW = 1.0

        def _l2norm(x, d):
            n = jnp.maximum(jnp.linalg.norm(x, axis=-1, keepdims=True), 1e-12)
            return x / n * d ** 0.5
        b, s, d = x.shape
        xn = _l2norm(x, d) * gamma_norm
        q = (xn @ Wq_w + Wq_b).reshape(b, s, G, H, DQK)
        kv = xn @ Wkv_w + Wkv_b
        k, v = (kv[..., :G * DQK], kv[..., G * DQK:])
        w = jax.nn.silu(k @ aw1_w + aw1_b) @ aw2_w + aw2_b
        w1 = jax.nn.softmax(w, axis=-1) / s
        w2 = jax.nn.softmax(w, axis=-2) / L * LSW
        w = (w1 + w2) / (1.0 + LSW)
        kc = jnp.einsum('bsd,bsl->bld', k, w).reshape(b, L, G, DQK)
        vc = jnp.einsum('bsd,bsl->bld', v, w).reshape(b, L, G, DV)
        qk = jnp.einsum('bsghd,blgd->bghsl', q, kc) * (1.0 / DQK ** 0.5)
        att = jax.nn.softmax(qk, axis=-1)
        z = jnp.einsum('bghsl,blgd->bsghd', att, vc).reshape(b, s, G * H * DV)
        zn = _l2norm(z, G * H * DV) * wz_g1
        h1 = jax.nn.silu(zn @ wz_w1 + wz_b1)
        h1n = _l2norm(h1, 2 * FF) * wz_g2
        out = jax.nn.silu(h1n @ wz_w2 + wz_b2)
        return out
    x = x + _L0_gnn_ref(_layernorm(x, axis=-1), src, dst, edge_type_8, L0_gnn_W_self, L0_gnn_b_self, L0_gnn_W_rel, L0_gnn_b_rel)
    x = x + _L0_ffn_ref(_layernorm(x, axis=-1)[None], L0_ffn_gamma_norm, L0_ffn_Wq_w, L0_ffn_Wq_b, L0_ffn_Wkv_w, L0_ffn_Wkv_b, L0_ffn_aw1_w, L0_ffn_aw1_b, L0_ffn_aw2_w, L0_ffn_aw2_b, L0_ffn_wz_g1, L0_ffn_wz_w1, L0_ffn_wz_b1, L0_ffn_wz_g2, L0_ffn_wz_w2, L0_ffn_wz_b2)[0]
    return x

_drawn_inputs = setup_inputs


def setup_inputs(seed=0):
    import zlib

    import numpy as np

    out = dict(_drawn_inputs(seed))
    spreads = {'L0_gnn_b_self': (0.0, 0.311),
     'L0_gnn_b_rel': (0.0, 0.1),
     'L0_ffn_gamma_norm': (1.0, 0.6),
     'L0_ffn_Wq_b': (0.0, 2.0),
     'L0_ffn_Wkv_b': (0.0, 0.1),
     'L0_ffn_aw1_b': (0.0, 2.0),
     'L0_ffn_aw2_b': (0.0, 2.0),
     'L0_ffn_wz_g1': (1.0, 0.6),
     'L0_ffn_wz_b1': (0.0, 0.8),
     'L0_ffn_wz_g2': (1.0, 0.6),
     'L0_ffn_wz_b2': (0.0, 0.436)}
    factors = {'L0_ffn_Wq_w': 200.0, 'L0_ffn_aw1_w': 8.0, 'L0_ffn_aw2_w': 26.599}
    for name, (base, spread) in spreads.items():
        noise = np.random.default_rng([zlib.crc32(name.encode()), seed]).standard_normal(out[name].shape)
        drawn = base * np.exp(spread * noise) if base else spread * noise
        out[name] = jnp.asarray(drawn.astype(out[name].dtype))
    for name, factor in factors.items():
        out[name] = (out[name] * factor).astype(out[name].dtype)
    return out
```

```python
from contextlib import ExitStack

import concourse.bass as bass
from concourse import mybir

F32 = mybir.dt.float32
F32R = mybir.dt.float32r
I32 = mybir.dt.int32
ALU = mybir.AluOpType
ACT = mybir.ActivationFunctionType
AX = mybir.AxisListType

N, D = 625, 512
NB, RB = 5, 125
KB = D // 128
E = 10000
R = 8
R2 = 2 * R
EP = 125
ET = E // EP
MT = 2 * ET
MR = 4
G, HG, DK, L = 8, 16, 128, 100
HU = 4
U = G * HG // HU
UG = HG // HU
UC = HU * L
F2 = 1024
FH = F2 // 2
FB = F2 // 128
SPAD = 628
SC = SPAD // 2
SR = 3
HO = 2 * NB
LN_EPS = 1e-5
L2_EPS = 1e-12

C_GAMMA = 0
C_G2 = C_GAMMA + KB
C_BK = C_G2 + FB
C_BQ = C_BK + G
C_G1 = C_BQ + G * HG
C_END = C_G1 + G * HG


def build_layer(nc, x, src, dst, etype, w_rel_t, b_rel, cols, wk_t, w_kv, aw1, aw1_b, aw2, aw2_b, b_v,
                wq_t, wz_w1, b1, w2, b2, out):
    ctx = ExitStack()

    def sem(name):
        return ctx.enter_context(nc.semaphore(name))

    h_table = nc.dram_tensor("h_table", [R2 * N, D], F32, kind="Internal").ap()
    x1_stash = nc.dram_tensor("x1_stash", [N, D], F32, kind="Internal").ap()
    bqk_rows = nc.dram_tensor("bqk_rows", [2, G * HG * L], F32, kind="Internal").ap()

    ps = ctx.enter_context(nc.psum_tensor("ps", [128, 8, 512], F32))

    class Shelf:
        def __init__(self, at):
            self.at = at

        def put(self, name, shape, dt=F32):
            size = 4
            for n in shape[1:]:
                size *= n
            t = nc.alloc_sbuf_tensor_at(name, shape, dt, offset=self.at)
            self.at += (size + 31) // 32 * 32
            return t

    whole = Shelf((nc.sbuf_base + 63) // 64 * 64)
    ident = whole.put("ident", [128, 128])
    ones = whole.put("ones", [128, 128])
    ones2 = whole.put("ones2", [2, RB], F32R)
    colc = whole.put("colc", [128, C_END])
    wq_raw = whole.put("wq_raw", [128, HU, D])
    w1_raw = whole.put("w1_raw", [128, HU, FH])
    kc_h = whole.put("kc_h", [128, G, L], F32R)
    kc_l = whole.put("kc_l", [128, G, L], F32R)
    vc_h = whole.put("vc_h", [L, G, DK], F32R)
    vc_l = whole.put("vc_l", [L, G, DK], F32R)
    xn_at = whole.at
    xn_h = whole.put("xn_h", [128, KB, SPAD], F32R)
    xn_l = whole.put("xn_l", [128, KB, SPAD], F32R)

    graph = Shelf(whole.at)
    xin = graph.put("xin", [RB, NB, D])
    hself = graph.put("hself", [RB, NB, D])
    rows = graph.put("rows", [RB, NB, D])
    x1 = graph.put("x1", [RB, NB, D])
    stat = graph.put("stat", [RB, NB, 6])
    mv = graph.put("mv", [RB, NB, 2])
    col = [graph.put(f"col{i}", [RB, NB]) for i in range(8)]
    var1, sdev1, var2, sdev2 = (c[:, :] for c in col[0:4])
    rdev = col[4]
    l2ss, l2sd, l2rc = col[5], col[6][:, :], col[7]
    idx = graph.put("idx", [EP, MT], I32)
    key = graph.put("key", [EP, MT])
    wkv = graph.put("wkv", [128, KB, 2 * G * DK])
    bvb = graph.put("bvb", [L, G * DK])
    table = Shelf(graph.at)
    wr_raw = table.put("wr_raw", [128, 2, KB, D])
    wr_h = table.put("wr_h", [128, 2, KB, D], F32R)
    wr_l = table.put("wr_l", [128, 2, KB, D], F32R)
    hout = table.put("hout", [RB, NB, D])
    brel = table.put("brel", [RB, 2, D])
    ei = rows
    gat = Shelf(graph.at)
    msg = gat.put("msg", [EP, MR, D])
    msg_h = gat.put("msg_h", [EP, MR, D], F32R)
    msg_l = gat.put("msg_l", [EP, MR, D], F32R)
    hot = gat.put("hot", [EP, MR, N + 1], F32R)
    node = gat.put("node", [EP, N])
    wkt = gat.put("wkt", [128, G, D])
    a1w = gat.put("a1w", [128, G, L])
    a2w = gat.put("a2w", [L, L])
    rowc = gat.put("rowc", [L, 2])
    lm = Shelf(graph.at)
    a1_h = lm.put("a1_h", [128, KB, L], F32R)
    a1_l = lm.put("a1_l", [128, KB, L], F32R)
    c1 = lm.put("c1", [L, 1])
    xg = lm.put("xg", [128, 2, KB, RB])
    hid = lm.put("hid", [L, SPAD])
    wt = lm.put("wt", [L, N])
    wt2 = lm.put("wt2", [L, N])
    wtc = lm.put("wtc", [L, 4])
    w = lm.put("w", [RB, NB, L])
    ct = lm.put("ct", [128, KB, L])
    swb = lm.put("swb", [128, L])
    swc = lm.put("swc", [L, 1])
    kf = lm.put("kf", [128, G, L])
    vf = lm.put("vf", [L, G, DK])
    bq_h = lm.put("bq_h", [HG, G, L], F32R)
    bq_l = lm.put("bq_l", [HG, G, L], F32R)
    assert lm.at <= graph.at + 4 * (3 * MR * D + MR * (N + 1))

    att = Shelf(whole.at)
    wq_h = att.put("wq_h", [128, HU, D], F32R)
    wq_l = att.put("wq_l", [128, HU, D], F32R)
    p_at = att.at
    p_h = att.put("p_h", [128, KB, UC], F32R)
    p_l = att.put("p_l", [128, KB, UC], F32R)
    prob = att.put("prob", [RB, SR, UC])
    at_h = att.put("at_h", [L, HU, SPAD], F32R)
    at_l = att.put("at_l", [L, HU, SPAD], F32R)
    z_h = [att.put(f"z_h{k}", [128, HU, SPAD], F32R) for k in range(2)]
    z_l = [att.put(f"z_l{k}", [128, HU, SPAD], F32R) for k in range(2)]
    zsq = att.put("zsq", [128, SPAD])
    w1_h = [att.put(f"w1_h{f}", [128, HU, FH], F32R) for f in range(2)]
    w1_l = [att.put(f"w1_l{f}", [128, HU, FH], F32R) for f in range(2)]
    brow = att.put("brow", [2, UC], F32R)
    vcu_h = att.put("vcu_h", [L, DK], F32R)
    vcu_l = att.put("vcu_l", [L, DK], F32R)
    g1u = att.put("g1u", [128, HU])
    smax = att.put("smax", [RB, HU])
    ssum = att.put("ssum", [RB, HU])
    srec = att.put("srec", [RB, SR, HU])
    acc = att.put("acc", [RB, NB, F2])
    zacc = att.put("zacc", [128, SPAD])
    assert att.at <= nc.sbuf_usable_end, (att.at, nc.sbuf_usable_end)

    assert p_at - whole.at >= 4 * FB * D
    w2_raw = Shelf(whole.at).put("w2_raw", [128, FB, D])
    fin = Shelf(p_at)
    w2_h = fin.put("w2_h", [128, FB, D], F32R)
    w2_l = fin.put("w2_l", [128, FB, D], F32R)
    tail = Shelf(xn_at)
    b1b = tail.put("b1b", [RB, F2])
    b2b = tail.put("b2b", [RB, D])
    x1r = tail.put("x1r", [RB, NB, D])
    assert tail.at <= whole.at
    last = Shelf(fin.at)
    ht_h = last.put("ht_h", [128, 2, FB, RB], F32R)
    ht_l = last.put("ht_l", [128, 2, FB, RB], F32R)
    junk = last.put("junk", [RB, F2])
    o = last.put("o", [RB, NB, D])
    fcol = [last.put(f"fcol{i}", [RB, NB]) for i in range(6)]

    S = {n: sem(n) for n in (
        "x_in", "edges_in", "cols_in", "consts", "pad_zero",
        "dve", "ln_var", "ln_sd", "rows_ready", "rows_t", "xn_hi", "xn_lo", "xg_ready",
        "wr_hi", "wr_lo", "table_mm", "hout_ready", "hself_ready", "idx_ready",
        "hot_ready", "msg_hi", "msg_lo", "seg_mm", "x1_ready", "x1_saved",
        "lm_in", "lm_in2", "kv_in", "l2_sq", "l2_sd", "l2_in",
        "a1_mm", "a1_hi", "a1_lo", "c1_ready", "hid_mm", "hid_ready", "wt_mm", "wt_ready", "wt2_max", "wt2_exp",
        "wt2_ready", "wt_t", "w_sh", "w_exp", "w_ready", "lm_mm", "lm_ev", "ct_ready", "kc_mm", "kf_ready", "kc_hi",
        "kc_lo", "vc_mm", "vf_ready", "vc_hi", "vc_lo", "bq_mm", "bq_hi", "bq_lo", "bq_saved", "lm_done",
        "wq_in", "wq_hi", "wq_lo", "w1_in", "w1_hi", "w1_lo", "brow_in",
        "p_mm", "p_hi", "p_lo", "score_mm", "max_ready", "shifted", "exp_ready", "sum_ready", "rec_ready", "prob_ready",
        "prob_t", "att_hi", "att_lo", "unit_cols", "z_mm", "z_hi", "z_lo", "z_sq", "z_acc", "h_mm", "h_acc", "acc_zero",
        "w2_in", "w2_hi", "w2_lo", "fin_in", "n_mm", "n_sd", "h_sh", "h1_ready", "h1_sq", "h1_sd", "h1_rec",
        "h1_t", "ht_hi", "ht_lo", "o_mm", "o_sh", "o_act", "o_ready", "out_done",
    )}
    wr_in = [sem(f"wr_in{k}") for k in range(2)]
    brel_in = [sem(f"brel_in{k}") for k in range(2)]
    h_saved = [sem(f"h_saved{b}") for b in range(NB)]
    msg_in = [sem(f"msg_in{k}") for k in range(MR)]

    block = ctx.enter_context(nc.Block())

    def spread(ap, shape):
        return ap.unsqueeze(len(shape) - 1).to_broadcast(shape)

    def over_relations(eng, step):
        step(0, 0, 0)
        step(1, 0, 1)
        with eng.Fori(1, R2 // 2) as i:
            step(2 * i, i, 0)
            step(2 * i + 1, i, 1)
        step(R2, R2 // 2, 0)

    def over_messages(eng, step):
        for k in range(MR):
            step(k, 0, k)
        with eng.Fori(1, MT // MR - 1) as i:
            for k in range(MR):
                step(i * MR + k, i, k)
        for k in range(MR):
            step(MT - MR + k, MT // MR - 1, k)

    def over_units(eng, step):
        step(0, 0)
        step(1, 1)
        with eng.Fori(1, U // 2 - 1) as i:
            step(2 * i, 0)
            step(2 * i + 1, 1)
        step(U - 2, 0)
        step(U - 1, 1)

    def first(v):
        return isinstance(v, int) and v == 0

    def final(v, n):
        return isinstance(v, int) and v == n

    @block.sync
    def _(sp):
        sp.dma_start(xin[:, :, :], x.rearrange("(b p) d -> p b d", p=RB)).then_inc(S["x_in"], 16)
        sp.dma_start(colc[:, :], cols).then_inc(S["cols_in"], 16)

        def load_wr(r, k):
            sp.dma_start(wr_raw[:, k, :, :].rearrange("p b d -> p (b d)"),
                         w_rel_t[bass.ds(r, 1), :, :].rearrange("a p n -> p (a n)")).then_inc(wr_in[k], 16)

        def load_brel(r, k):
            sp.dma_start(brel[:, k, :], b_rel[bass.ds(r, 1), :].to_broadcast([RB, D])).then_inc(brel_in[k], 16)

        for k in range(2):
            load_wr(k, k)
            load_brel(k, k)
        for n, a in enumerate((src, dst, etype)):
            sp.dma_start(ei[0:EP, n, 0:ET].bitcast(I32), a.rearrange("(p t) -> p t", t=ET)).then_inc(S["edges_in"], 16)
        sp.dma_start(wkv[:, :, :], w_kv).then_inc(S["kv_in"], 16)
        sp.dma_start(bvb[:, :], b_v.to_broadcast([L, G * DK])).then_inc(S["kv_in"], 16)
        sp.dma_start(wq_raw[:, :, :].rearrange("p h d -> p (h d)"), wq_t[0]).then_inc(S["wq_in"], 16)
        sp.dma_start(w1_raw[:, :, :].rearrange("p h d -> p (h d)"), wz_w1[0, 0]).then_inc(S["w1_in"], 16)

        def table_step(r, i, k):
            if final(r, R2):
                return
            more = not final(r, R2 - 1)
            if more:
                sp.wait_ge(S["wr_hi"], r + 1)
                sp.wait_ge(S["wr_lo"], r + 1)
                load_wr(r + 2, k)
            for b in range(NB):
                sp.wait_ge(S["hout_ready"], NB * r + b + 1)
                sp.dma_start(h_table[bass.ds(r * N + b * RB, RB), :], hout[:, b, :]).then_inc(h_saved[b], 16)
            if more:
                load_brel(r + 2, k)

        step = table_step
        step(0, 0, 0)
        step(1, 0, 1)
        with sp.Fori(1, R2 // 2 - 1) as i:
            step(2 * i, i, 0)
            step(2 * i + 1, i, 1)
        step(R2 - 2, R2 // 2 - 1, 0)
        step(R2 - 1, R2 // 2 - 1, 1)

        sp.wait_ge(S["table_mm"], NB * (R2 + 1))
        sp.wait_ge(S["hself_ready"], NB)
        for b in range(NB):
            sp.wait_ge(h_saved[b], 16 * R2)
        sp.dma_start(wkt[:, :, :], wk_t).then_inc(S["lm_in"], 16)
        sp.dma_start(a1w[:, :, :], aw1).then_inc(S["lm_in"], 16)
        sp.dma_start(a2w[:, :], aw2).then_inc(S["lm_in"], 16)
        sp.dma_start(rowc[:, 0:1], aw1_b).then_inc(S["lm_in"], 16)
        sp.dma_start(rowc[:, 1:2], aw2_b).then_inc(S["lm_in"], 16)

        sp.wait_ge(S["x1_ready"], NB)
        sp.dma_start(x1_stash.rearrange("(b p) d -> p b d", p=RB), x1[:, :, :]).then_inc(S["x1_saved"], 16)

        sp.wait_ge(S["bq_hi"], 1)
        sp.dma_start(bqk_rows[0:1, :].rearrange("a (g h l) -> h (a g) l", g=G, h=HG), bq_h[:, :, :].bitcast(F32))\
            .then_inc(S["bq_saved"], 16)
        sp.wait_ge(S["bq_lo"], 1)
        sp.dma_start(bqk_rows[1:2, :].rearrange("a (g h l) -> h (a g) l", g=G, h=HG), bq_l[:, :, :].bitcast(F32))\
            .then_inc(S["bq_saved"], 16)
        sp.wait_ge(S["bq_saved"], 32)

        def load_w1(v, f):
            sp.wait_ge(S["w1_lo"], HU * (2 * v + f))
            sp.wait_ge(S["w1_hi"], 2 * v + f)
            sp.dma_start(w1_raw[:, :, :].rearrange("p h d -> p (h d)"),
                         wz_w1[bass.ds(v, 1), f].rearrange("a p n -> p (a n)")).then_inc(S["w1_in"], 16)

        def load_wq(v):
            sp.wait_ge(S["wq_lo"], HU * v)
            sp.wait_ge(S["wq_hi"], v)
            sp.dma_start(wq_raw[:, :, :].rearrange("p h d -> p (h d)"),
                         wq_t[bass.ds(v, 1)].rearrange("a p n -> p (a n)")).then_inc(S["wq_in"], 16)

        def load_brow(v):
            sp.dma_start(brow[:, :].bitcast(F32), bqk_rows[:, bass.ds(v * UC, UC)]).then_inc(S["brow_in"], 16)

        sp.wait_ge(S["lm_done"], 1)
        load_brow(0)
        load_wq(1)

        def unit_step(v, k):
            if not first(v):
                load_w1(v, 0)
            if not (final(v, U - 2) or final(v, U - 1)):
                load_wq(v + 2)
            if not final(v, U - 1):
                sp.wait_ge(S["score_mm"], NB * (v + 1))
                load_brow(v + 1)
            load_w1(v, 1)

        over_units(sp, unit_step)

        sp.wait_ge(S["p_mm"], KB * U)
        sp.dma_start(w2_raw[:, :, :], w2).then_inc(S["w2_in"], 16)
        sp.wait_ge(S["score_mm"], NB * U)
        sp.dma_start(b1b[:, :], b1.to_broadcast([RB, F2])).then_inc(S["fin_in"], 16)
        sp.dma_start(b2b[:, :], b2.to_broadcast([RB, D])).then_inc(S["fin_in"], 16)
        sp.wait_ge(S["x1_saved"], 16)
        sp.dma_start(x1r[:, :, :], x1_stash.rearrange("(b p) d -> p b d", p=RB)).then_inc(S["fin_in"], 16)
        for b in range(NB):
            sp.wait_ge(S["o_ready"], b + 1)
            sp.dma_start(out[b * RB:(b + 1) * RB, :], o[:, b, :]).then_inc(S["out_done"], 16)
        sp.wait_ge(S["out_done"], 16 * NB)

    @block.gpsimd
    def _(pool):
        pool.memset(ident[:, :], 0.0).then_inc(S["consts"], 1)
        pool.wait_ge(S["consts"], 1)
        pool.affine_select(out=ident[:, :], in_=ident[:, :], compare_op=ALU.not_equal, fill=1.0, base=0,
                           pattern=[[-1, 128]], channel_multiplier=1).then_inc(S["consts"], 1)
        pool.memset(ones[:, :], 1.0).then_inc(S["consts"], 1)
        pool.memset(ones2[:, :].bitcast(F32), 1.0).then_inc(S["consts"], 1)
        pool.memset(xn_h[:, :, N:SPAD].bitcast(F32), 0.0).then_inc(S["consts"], 1)
        pool.memset(xn_l[:, :, N:SPAD].bitcast(F32), 0.0).then_inc(S["consts"], 1)

        for b in range(NB):
            pool.wait_ge(h_saved[b], 16 * R2)
        pool.wait_ge(S["table_mm"], NB * (R2 + 1))
        pool.wait_ge(S["hself_ready"], NB)
        pool.iota(node[:, :], [[1, N]], base=0, channel_multiplier=0,
                  allow_small_or_imprecise_dtypes=True).then_inc(S["consts"], 1)
        pool.wait_ge(S["idx_ready"], 2)

        for t in range(MT):
            k = t % MR
            if t >= MR:
                pool.wait_ge(S["msg_hi"], t + 1 - MR)
                pool.wait_ge(S["msg_lo"], t + 1 - MR)
            pool.indirect_dma_start(msg[:, k, :], None, h_table,
                                    bass.IndirectOffsetOnAxis(ap=idx[:, t:t + 1], axis=0)).then_inc(msg_in[k], 16)

        pool.wait_ge(S["lm_done"], 1)
        for a in (at_h, at_l):
            pool.memset(a[:, :, N:SPAD].bitcast(F32), 0.0).then_inc(S["pad_zero"], 1)
        pool.memset(acc[:, :, :], 0.0).then_inc(S["acc_zero"], 1)
        pool.memset(zacc[:, :], 0.0).then_inc(S["z_acc"], 1)

        def split_w1(v, f, heads):
            pool.wait_ge(S["w1_hi"], 2 * v + f + 1)
            for h in heads:
                pool.tensor_tensor(w1_l[f][:, h, :], w1_raw[:, h, :], w1_h[f][:, h, :].bitcast(F32),
                                   ALU.subtract).then_inc(S["w1_lo"], 1)

        def split_wq(v, heads):
            pool.wait_ge(S["wq_hi"], v + 1)
            for h in heads:
                pool.tensor_tensor(wq_l[:, h, :], wq_raw[:, h, :], wq_h[:, h, :].bitcast(F32),
                                   ALU.subtract).then_inc(S["wq_lo"], 1)

        split_wq(0, range(HU))

        def unit_step(v, k):
            g = v // UG
            if not first(v):
                pool.wait_ge(S["z_mm"], HU * v)
                pool.wait_ge(S["z_hi"], HU * v)
                pool.wait_ge(S["z_lo"], HU * v)
            pool.tensor_copy(vcu_h[:, :], vc_h[:, bass.ds(g, 1), :].rearrange("p a d -> p (a d)").bitcast(F32)).then_inc(S["unit_cols"], 1)
            pool.tensor_copy(vcu_l[:, :], vc_l[:, bass.ds(g, 1), :].rearrange("p a d -> p (a d)").bitcast(F32)).then_inc(S["unit_cols"], 1)
            pool.tensor_copy(g1u[:, :], colc[:, bass.ds(C_G1 + v * HU, HU)]).then_inc(S["unit_cols"], 1)

            def normalise(j):
                pool.wait_ge(S["rec_ready"], NB * v + j + 1)
                pj = prob[:, j % SR, :].rearrange("p (h l) -> p h l", h=HU)
                pool.tensor_tensor(pj, pj, spread(srec[:, j % SR, :], [RB, HU, L]), ALU.mult)\
                    .then_inc(S["prob_ready"], 1)

            more = not final(v, U - 1)
            normalise(0)
            if not first(v):
                split_w1(v - 1, 1, range(0, 3))
            normalise(1)
            if not first(v):
                split_w1(v - 1, 1, range(3, 4))
            if more:
                split_wq(v + 1, range(0, 1))
            normalise(2)
            if more:
                split_wq(v + 1, range(1, 3))
            normalise(3)
            if more:
                split_wq(v + 1, range(3, 4))
            normalise(4)
            split_w1(v, 0, range(HU))
            for h in range(HU):
                pool.wait_ge(S["z_sq"], HU * v + h + 1)
                pool.wait_ge(S["z_acc"], HU * v + h + 1)
                pool.tensor_tensor(zacc[:, :], zacc[:, :], zsq[:, :], ALU.add).then_inc(S["z_acc"], 1)

        over_units(pool, unit_step)
        split_w1(U - 1, 1, range(HU))

    @block.scalar
    def _(act):
        def hi(dst, source, done):
            nc.scalar.activation(dst, source, ACT.Copy).then_inc(S[done], 1)

        act.wait_ge(S["ln_var"], 1)
        nc.scalar.activation(sdev1, var1, ACT.Sqrt).then_inc(S["ln_sd"], 1)

        def split_wr(r, i, k):
            act.wait_ge(wr_in[k], 16 * (i + 1))
            if not first(i):
                act.wait_ge(S["table_mm"], NB * (r - 1))
            hi(wr_h[:, k, :, :], wr_raw[:, k, :, :], "wr_hi")

        split_wr(0, 0, 0)
        split_wr(1, 0, 1)
        for b in range(NB):
            act.wait_ge(S["rows_t"], b + 1)
            hi(xn_h[:, :, b * RB:(b + 1) * RB], ps[:, 5 + b % 2, 0:KB * RB].rearrange("p (k n) -> p k n", k=KB), "xn_hi")
        with act.Fori(1, R2 // 2) as i:
            split_wr(2 * i, i, 0)
            split_wr(2 * i + 1, i, 1)
        split_wr(R2, R2 // 2, 0)

        def split_msg(t, i, k):
            act.wait_ge(msg_in[k], 16 * (i + 1))
            if not first(i):
                act.wait_ge(S["seg_mm"], t + 1 - MR)
            hi(msg_h[:, k, :], msg[:, k, :], "msg_hi")

        over_messages(act, split_msg)

        act.wait_ge(S["a1_mm"], 1)
        hi(a1_h[:, :, :], ps[:, 7, 0:KB * L].rearrange("p (k l) -> p k l", k=KB), "a1_hi")
        act.wait_ge(S["ln_var"], 2)
        nc.scalar.activation(sdev2, var2, ACT.Sqrt).then_inc(S["ln_sd"], 1)
        for b in range(NB):
            act.wait_ge(S["l2_in"], b + 1)
            nc.scalar.activation(hself[:, b, :], rows[:, b, :], ACT.Square, accum_out=l2ss[:, b:b + 1])\
                .then_inc(S["l2_sq"], 1)
        act.wait_ge(S["l2_sq"], NB)
        nc.scalar.activation(l2sd, l2ss[:, :], ACT.Sqrt).then_inc(S["l2_sd"], 1)
        for b in range(NB):
            act.wait_ge(S["xg_ready"], b + 1)
            hi(xn_h[:, :, b * RB:(b + 1) * RB], xg[:, b % 2, :, :], "xn_hi")
        act.wait_ge(S["hid_mm"], 1)
        act.wait_ge(S["c1_ready"], 1)
        nc.scalar.activation(hid[:, :].rearrange("p (c n) -> p c n", c=2), ps[0:L, 0:2, 0:SC], ACT.Silu,
                             bias=c1[:, 0:1]).then_inc(S["hid_ready"], 1)
        act.wait_ge(S["wt2_max"], 1)
        nc.scalar.activation(wt2[:, :], wt[:, :], ACT.Exp, bias=wtc[:, 0:1], accum_out=wtc[:, 1:2])\
            .then_inc(S["wt2_exp"], 1)
        act.wait_ge(S["w_sh"], 1)
        nc.scalar.activation(w[:, :, :], w[:, :, :], ACT.Exp).then_inc(S["w_exp"], 1)
        act.wait_ge(S["kf_ready"], 1)
        hi(kc_h[:, :, :], kf[:, :, :], "kc_hi")
        act.wait_ge(S["vf_ready"], 1)
        hi(vc_h[:, :, :], vf[:, :, :], "vc_hi")
        act.wait_ge(S["bq_mm"], 1)
        hi(bq_h[:, :, :].rearrange("p (c g) l -> p c g l", c=2),
           ps[0:HG, 4:6, 0:4 * L].rearrange("p c (g l) -> p c g l", g=4), "bq_hi")

        act.wait_ge(S["lm_done"], 1)

        def split_wq(v):
            act.wait_ge(S["wq_in"], 16 * (v + 1))
            if not first(v):
                act.wait_ge(S["p_mm"], KB * v)
            hi(wq_h[:, :, :], wq_raw[:, :, :], "wq_hi")

        def split_w1(v, f):
            act.wait_ge(S["w1_in"], 16 * (2 * v + f + 1))
            if not first(v):
                act.wait_ge(S["h_mm"], HO * (v - 1) + NB * (f + 1))
            hi(w1_h[f][:, :, :], w1_raw[:, :, :], "w1_hi")

        def hi_p(v, kb):
            act.wait_ge(S["p_mm"], KB * v + kb + 1)
            if kb == 0 and not first(v):
                act.wait_ge(S["score_mm"], NB * v)
            hi(p_h[:, kb, :], ps[:, 7, 0:UC], "p_hi")

        split_wq(0)
        for kb in range(KB):
            hi_p(0, kb)

        def unit_step(v, k):
            def exp(j):
                act.wait_ge(S["shifted"], NB * v + j + 1)
                nc.scalar.activation(prob[:, j % SR, :], prob[:, j % SR, :], ACT.Exp).then_inc(S["exp_ready"], 1)

            def hi_att(j):
                act.wait_ge(S["prob_t"], NB * v + j + 1)
                if j == 0:
                    if first(v):
                        act.wait_ge(S["pad_zero"], 2)
                    else:
                        act.wait_ge(S["z_mm"], HU * v)
                hi(at_h[:, :, j * RB:(j + 1) * RB], ps[0:L, 4, 0:HU * RB].rearrange("p (h n) -> p h n", h=HU), "att_hi")

            def hi_z(h):
                act.wait_ge(S["z_mm"], HU * v + h + 1)
                if h == 0:
                    act.wait_ge(S["unit_cols"], 3 * (v + 1))
                    if not (first(v) or first(v - 1)):
                        act.wait_ge(S["h_mm"], HO * (v - 1))
                zp = ps[:, 5:7, 0:SC]
                nc.scalar.activation(z_h[k][:, h, :].rearrange("p (c n) -> p c n", c=2), zp, ACT.Copy,
                                     scale=g1u[:, h:h + 1]).then_inc(S["z_hi"], 1)
                act.wait_ge(S["z_acc"], HU * v + h + 1)
                nc.scalar.activation(zsq[:, :].rearrange("p (c n) -> p c n", c=2), zp, ACT.Square)\
                    .then_inc(S["z_sq"], 1)

            more = not final(v, U - 1)
            exp(0)
            if not first(v):
                split_w1(v - 1, 1)
            exp(1)
            hi_att(0)
            if more:
                split_wq(v + 1)
            exp(2)
            hi_att(1)
            exp(3)
            hi_att(2)
            exp(4)
            if more:
                hi_p(v + 1, 0)
            hi_att(3)
            if more:
                hi_p(v + 1, 1)
            hi_att(4)
            split_w1(v, 0)
            if more:
                hi_p(v + 1, 2)
            hi_z(0)
            if more:
                hi_p(v + 1, 3)
            hi_z(1)
            hi_z(2)
            hi_z(3)

        over_units(act, unit_step)
        split_w1(U - 1, 1)

        act.wait_ge(S["w2_in"], 16)
        act.wait_ge(S["z_mm"], HU * U)
        for f in range(FB):
            nc.scalar.activation(w2_h[:, f, :], w2_raw[:, f, :], ACT.Copy,
                                 scale=colc[:, C_G2 + f:C_G2 + f + 1]).then_inc(S["w2_hi"], 1)
        act.wait_ge(S["n_mm"], 1)
        nc.scalar.activation(fcol[0][:, :], ps[0:RB, 4, 0:NB], ACT.Sqrt).then_inc(S["n_sd"], 1)
        for b in range(NB):
            act.wait_ge(S["h_sh"], b + 1)
            nc.scalar.activation(acc[:, b, :], acc[:, b, :], ACT.Silu).then_inc(S["h1_ready"], 1)
        for b in range(NB):
            act.wait_ge(S["h1_ready"], b + 1)
            if b > 0:
                act.wait_ge(S["h1_sq"], b)
            nc.scalar.activation(junk[:, :], acc[:, b, :], ACT.Square, accum_out=fcol[2][:, b:b + 1])\
                .then_inc(S["h1_sq"], 1)
            for c in range(2):
                act.wait_ge(S["h1_t"], 2 * b + c + 1)
                if b >= 2:
                    act.wait_ge(S["o_mm"], b - 1)
                hi(ht_h[:, b % 2, 4 * c:4 * c + 4, :], ps[:, c, 0:4 * RB].rearrange("p (k n) -> p k n", k=4), "ht_hi")
        act.wait_ge(S["h1_sq"], NB)
        nc.scalar.activation(fcol[3][:, :], fcol[2][:, :], ACT.Sqrt).then_inc(S["h1_sd"], 1)
        for b in range(NB):
            act.wait_ge(S["o_sh"], b + 1)
            nc.scalar.activation(o[:, b, :], o[:, b, :], ACT.Silu).then_inc(S["o_act"], 1)

    @block.vector
    def _(dve):
        chain = [0]

        def link(ins):
            chain[0] += 1
            ins.then_inc(S["dve"], 1)
            dve.wait_ge(S["dve"], chain[0])

        def lo(dst, source, part, done):
            dve.tensor_tensor(dst, source, part.bitcast(F32), ALU.subtract).then_inc(S[done], 1)

        def normalise(source, dest, v, sd, n, done):
            for b in range(NB):
                ins = dve.bn_stats(stat[:, b, :], source[:, b, :])
            link(ins)
            for b in range(NB):
                ins = dve.bn_aggr(mv[:, b, :], stat[:, b, :])
            link(ins)
            dve.tensor_scalar(v, mv[:, :, 1], LN_EPS, None, ALU.add).then_inc(S["ln_var"], 1)
            dve.wait_ge(S["ln_sd"], n)
            link(dve.reciprocal(rdev[:, :], sd))
            for b in range(NB):
                dve.tensor_scalar(dest[:, b, :], source[:, b, :], mv[:, b, 0:1], rdev[:, b:b + 1],
                                  ALU.subtract, ALU.mult).then_inc(S[done], 1)

        dve.wait_ge(S["edges_in"], 48)
        e = ei[0:EP, 0:3, 0:ET].bitcast(I32)
        link(dve.tensor_copy(key[:, 0:ET], e[:, 0, :]))
        link(dve.tensor_copy(key[:, ET:MT], e[:, 1, :]))
        link(dve.tensor_scalar(x1[0:EP, 0, 0:ET], e[:, 2, :], float(N), None, ALU.mult))
        dve.scalar_tensor_tensor(out=idx[:, 0:ET], in0=x1[0:EP, 0, 0:ET], scalar=0.0, in1=key[:, ET:MT],
                                 op0=ALU.add, op1=ALU.add).then_inc(S["idx_ready"], 1)
        dve.scalar_tensor_tensor(out=idx[:, ET:MT], in0=x1[0:EP, 0, 0:ET], scalar=float(R * N), in1=key[:, 0:ET],
                                 op0=ALU.add, op1=ALU.add).then_inc(S["idx_ready"], 1)

        dve.wait_ge(S["x_in"], 16)
        normalise(xin, rows, var1, sdev1, 1, "rows_ready")

        def split_wr(r, i, k):
            dve.wait_ge(S["wr_hi"], r + 1)
            lo(wr_l[:, k, :, :], wr_raw[:, k, :, :], wr_h[:, k, :, :], "wr_lo")

        split_wr(0, 0, 0)
        for b in range(NB):
            dve.wait_ge(S["xn_hi"], b + 1)
            cut = slice(b * RB, (b + 1) * RB)
            lo(xn_l[:, :, cut], ps[:, 5 + b % 2, 0:KB * RB].rearrange("p (k n) -> p k n", k=KB), xn_h[:, :, cut], "xn_lo")

        def drain_table(r, i, k):
            own = final(r, R2)
            dve.wait_ge(brel_in[k], 16 * (i + 1))
            for b in range(NB):
                dve.wait_ge(S["table_mm"], NB * r + b + 1)
                if not first(r) and not own:
                    dve.wait_ge(h_saved[b], 16 * r)
                dst = hself[:, b, :] if own else hout[:, b, :]
                dve.tensor_tensor(dst, ps[0:RB, b, :], brel[:, k, :], ALU.add)\
                    .then_inc(S["hself_ready" if own else "hout_ready"], 1)

        split_wr(1, 0, 1)
        drain_table(0, 0, 0)
        with dve.Fori(1, R2 // 2) as i:
            split_wr(2 * i, i, 0)
            drain_table(2 * i - 1, i - 1, 1)
            split_wr(2 * i + 1, i, 1)
            drain_table(2 * i, i, 0)
        split_wr(R2, R2 // 2, 0)
        drain_table(R2 - 1, R2 // 2 - 1, 1)
        drain_table(R2, R2 // 2, 0)

        dve.wait_ge(S["consts"], 7)

        def split_msg(t, i, k):
            if not first(i):
                dve.wait_ge(S["seg_mm"], t + 1 - MR)
            dve.tensor_scalar(hot[:, k, 0:N], node[:, :], key[:, bass.ds(t, 1)], None, ALU.is_equal)\
                .then_inc(S["hot_ready"], 1)
            dve.wait_ge(S["msg_hi"], t + 1)
            lo(msg_l[:, k, :], msg[:, k, :], msg_h[:, k, :], "msg_lo")

        over_messages(dve, split_msg)

        dve.wait_ge(S["seg_mm"], MT)
        for b in range(NB):
            link(dve.tensor_tensor(rows[:, b, :], ps[0:RB, b, :], hself[:, b, :], ALU.add))
            dve.scalar_tensor_tensor(out=x1[:, b, :], in0=rows[:, b, :], scalar=0.0, in1=xin[:, b, :],
                                     op0=ALU.max, op1=ALU.add).then_inc(S["x1_ready"], 1)
        dve.wait_ge(S["x1_ready"], NB)
        dve.wait_ge(S["cols_in"], 16)

        normalise(x1, rows, var2, sdev2, 2, "l2_in")
        dve.wait_ge(S["l2_sd"], 1)
        link(dve.tensor_scalar(l2rc[:, :], l2sd, L2_EPS, None, ALU.max))
        link(dve.reciprocal(l2rc[:, :], l2rc[:, :]))
        dve.wait_ge(S["l2_in"], NB)
        for b in range(NB):
            dve.tensor_scalar(rows[:, b, :], rows[:, b, :], l2rc[:, b:b + 1], float(D) ** 0.5,
                              ALU.mult, ALU.mult).then_inc(S["rows_ready"], 1)

        dve.wait_ge(S["a1_hi"], 1)
        lo(a1_l[:, :, :], ps[:, 7, 0:KB * L].rearrange("p (k l) -> p k l", k=KB), a1_h[:, :, :], "a1_lo")
        dve.tensor_tensor(c1[:, :], ps[0:L, 6, 0:1], rowc[:, 0:1], ALU.add).then_inc(S["c1_ready"], 1)
        gam = spread(colc[:, C_GAMMA:C_GAMMA + KB], [128, KB, RB])
        for b in range(NB):
            cut = slice(b * RB, (b + 1) * RB)
            dve.wait_ge(S["rows_t"], NB + b + 1)
            if b >= 2:
                dve.wait_ge(S["xn_hi"], NB + b - 1)
            dve.tensor_tensor(xg[:, b % 2, :, :], ps[:, b % 2, 0:KB * RB].rearrange("p (k n) -> p k n", k=KB), gam,
                              ALU.mult).then_inc(S["xg_ready"], 1)
            dve.wait_ge(S["xn_hi"], NB + b + 1)
            lo(xn_l[:, :, cut], xg[:, b % 2, :, :], xn_h[:, :, cut], "xn_lo")

        dve.wait_ge(S["wt_mm"], 1)
        for c, n in ((0, SC), (1, N - SC)):
            ins = dve.tensor_scalar(wt[:, c * SC:c * SC + n], ps[0:L, 2 + c, 0:n], rowc[:, 1:2], None, ALU.add)
            ins.then_inc(S["wt_ready"], 1)
        dve.wait_ge(S["wt_ready"], 2)
        dve.tensor_reduce(wtc[:, 0:1], wt[:, :], AX.X, ALU.max, negate=True).then_inc(S["wt2_max"], 1)
        dve.wait_ge(S["wt2_exp"], 1)
        link(dve.reciprocal(wtc[:, 2:3], wtc[:, 1:2]))
        dve.tensor_scalar(wt2[:, :], wt2[:, :], wtc[:, 2:3], 0.5 / L, ALU.mult, ALU.mult).then_inc(S["wt2_ready"], 1)
        dve.wait_ge(S["wt_t"], 1)
        wps = ps[0:RB, 4, 0:NB * L].rearrange("p (b l) -> p b l", b=NB)
        link(dve.tensor_reduce(rdev[:, :], wps, AX.X, ALU.max))
        dve.tensor_tensor(w[:, :, :], wps, spread(rdev[:, :], [RB, NB, L]), ALU.subtract).then_inc(S["w_sh"], 1)
        dve.wait_ge(S["w_exp"], 1)
        link(dve.tensor_reduce(l2rc[:, :], w[:, :, :], AX.X, ALU.add))
        link(dve.reciprocal(rdev[:, :], l2rc[:, :]))
        link(dve.tensor_tensor(w[:, :, :], w[:, :, :], spread(rdev[:, :], [RB, NB, L]), ALU.mult))
        dve.wait_ge(S["wt_t"], 2)
        dve.scalar_tensor_tensor(out=w[:, :, :], in0=w[:, :, :], scalar=0.5 / N,
                                 in1=ps[0:RB, 5, 0:NB * L].rearrange("p (b l) -> p b l", b=NB),
                                 op0=ALU.mult, op1=ALU.add).then_inc(S["w_ready"], 1)
        dve.wait_ge(S["lm_mm"], 1)
        dve.tensor_copy(swb[:, :], ps[:, 6, 0:L]).then_inc(S["lm_ev"], 1)
        dve.tensor_copy(swc[:, :], ps[0:L, 6, 128:129]).then_inc(S["lm_ev"], 1)
        dve.tensor_tensor(ct[:, :, :], ps[:, 7, 0:KB * L].rearrange("p (k l) -> p k l", k=KB),
                          spread(colc[:, C_GAMMA:C_GAMMA + KB], [128, KB, L]), ALU.mult).then_inc(S["ct_ready"], 1)
        dve.wait_ge(S["lm_ev"], 2)
        for g in range(G):
            if g % 4 == 0:
                dve.wait_ge(S["kc_mm"], g // 4 + 1)
            ins = dve.scalar_tensor_tensor(out=kf[:, g, :], in0=swb[:, :], scalar=colc[:, C_BK + g:C_BK + g + 1],
                                           in1=ps[:, g // 4, (g % 4) * L:(g % 4 + 1) * L],
                                           op0=ALU.mult, op1=ALU.add)
        link(ins)
        dve.tensor_scalar(kf[:, :, :], kf[:, :, :], float(DK) ** -0.5, None, ALU.mult).then_inc(S["kf_ready"], 1)
        dve.wait_ge(S["vc_mm"], 1)
        dve.scalar_tensor_tensor(out=vf[:, :, :].rearrange("p g d -> p (g d)").rearrange("p (c n) -> p c n", c=2),
                                 in0=bvb[:, :].rearrange("p (c n) -> p c n", c=2), scalar=swc[:, 0:1],
                                 in1=ps[0:L, 2:4, :], op0=ALU.mult, op1=ALU.add).then_inc(S["vf_ready"], 1)
        dve.wait_ge(S["kc_hi"], 1)
        lo(kc_l[:, :, :], kf[:, :, :], kc_h[:, :, :], "kc_lo")
        dve.wait_ge(S["vc_hi"], 1)
        lo(vc_l[:, :, :], vf[:, :, :], vc_h[:, :, :], "vc_lo")
        dve.wait_ge(S["bq_hi"], 1)
        lo(bq_l[:, :, :].rearrange("p (c g) l -> p c g l", c=2),
           ps[0:HG, 4:6, 0:4 * L].rearrange("p c (g l) -> p c g l", g=4),
           bq_h[:, :, :].rearrange("p (c g) l -> p c g l", c=2), "bq_lo")
        for n in ("kc_lo", "vc_lo", "bq_lo"):
            dve.wait_ge(S[n], 1)
        dve.wait_ge(S["bq_saved"], 32)
        dve.wait_ge(S["x1_saved"], 16)
        dve.nop().then_inc(S["lm_done"], 1)

        def lo_p(v, kb):
            dve.wait_ge(S["p_hi"], KB * v + kb + 1)
            lo(p_l[:, kb, :], ps[:, 7, 0:UC], p_h[:, kb, :], "p_lo")

        for kb in range(KB):
            lo_p(0, kb)

        def add_h(v, n):
            f, b = n // NB, n % NB
            dve.wait_ge(S["h_mm"], HO * v + n + 1)
            a = acc[:, b, f * FH:(f + 1) * FH]
            dve.tensor_tensor(a, a, ps[0:RB, 2 + n % 2, :], ALU.add).then_inc(S["h_acc"], 1)

        def unit_step(v, k):
            def softmax(j):
                q = NB * v + j
                sj = ps[0:RB, j % 2, 0:UC].rearrange("p (h l) -> p h l", h=HU)
                pj = prob[:, j % SR, :].rearrange("p (h l) -> p h l", h=HU)
                dve.wait_ge(S["score_mm"], q + 1)
                dve.tensor_reduce(smax[:, :], sj, AX.X, ALU.max).then_inc(S["max_ready"], 1)
                dve.wait_ge(S["max_ready"], q + 1)
                if j >= SR:
                    dve.wait_ge(S["prob_t"], q + 1 - SR)
                elif not first(v):
                    dve.wait_ge(S["prob_t"], NB * v - {0: 1, 1: 0, 2: 2}[j])
                dve.tensor_tensor(pj, sj, spread(smax[:, :], [RB, HU, L]), ALU.subtract).then_inc(S["shifted"], 1)
                dve.wait_ge(S["exp_ready"], q + 1)
                dve.tensor_reduce(ssum[:, :], pj, AX.X, ALU.add).then_inc(S["sum_ready"], 1)
                dve.wait_ge(S["sum_ready"], q + 1)
                dve.reciprocal(srec[:, j % SR, :], ssum[:, :]).then_inc(S["rec_ready"], 1)

            def lo_att(j):
                dve.wait_ge(S["att_hi"], NB * v + j + 1)
                cut = slice(j * RB, (j + 1) * RB)
                lo(at_l[:, :, cut], ps[0:L, 4, 0:HU * RB].rearrange("p (h n) -> p h n", h=HU), at_h[:, :, cut],
                   "att_lo")

            def lo_z(h):
                dve.wait_ge(S["z_sq"], HU * v + h + 1)
                dve.scalar_tensor_tensor(out=z_l[k][:, h, :].rearrange("p (c n) -> p c n", c=2), in0=ps[:, 5:7, 0:SC],
                                         scalar=g1u[:, h:h + 1],
                                         in1=z_h[k][:, h, :].rearrange("p (c n) -> p c n", c=2).bitcast(F32),
                                         op0=ALU.mult, op1=ALU.subtract).then_inc(S["z_lo"], 1)

            def add(n):
                if not first(v):
                    add_h(v - 1, n)

            more = not final(v, U - 1)
            softmax(0)
            add(0)
            softmax(1)
            add(1)
            lo_att(0)
            softmax(2)
            add(2)
            lo_att(1)
            softmax(3)
            add(3)
            lo_att(2)
            softmax(4)
            if more:
                lo_p(v + 1, 0)
            add(4)
            lo_att(3)
            if more:
                lo_p(v + 1, 1)
            add(5)
            lo_att(4)
            if more:
                lo_p(v + 1, 2)
            add(6)
            lo_z(0)
            if more:
                lo_p(v + 1, 3)
            add(7)
            lo_z(1)
            add(8)
            lo_z(2)
            add(9)
            lo_z(3)

        dve.wait_ge(S["acc_zero"], 1)
        over_units(dve, unit_step)
        for n in range(HO):
            add_h(U - 1, n)

        dve.wait_ge(S["w2_hi"], FB)
        for f in range(FB):
            dve.scalar_tensor_tensor(out=w2_l[:, f, :], in0=w2_raw[:, f, :], scalar=colc[:, C_G2 + f:C_G2 + f + 1],
                                     in1=w2_h[:, f, :].bitcast(F32), op0=ALU.mult, op1=ALU.subtract)\
                .then_inc(S["w2_lo"], 1)
        dve.wait_ge(S["n_sd"], 1)
        link(dve.tensor_scalar(fcol[1][:, :], fcol[0][:, :], L2_EPS, None, ALU.max))
        link(dve.reciprocal(fcol[1][:, :], fcol[1][:, :]))
        link(dve.tensor_scalar(fcol[1][:, :], fcol[1][:, :], float(G * HG * DK) ** 0.5, None, ALU.mult))
        dve.wait_ge(S["h_acc"], HO * U)
        dve.wait_ge(S["fin_in"], 48)
        for b in range(NB):
            dve.scalar_tensor_tensor(out=acc[:, b, :], in0=acc[:, b, :], scalar=fcol[1][:, b:b + 1], in1=b1b[:, :],
                                     op0=ALU.mult, op1=ALU.add).then_inc(S["h_sh"], 1)
        for b in range(NB):
            for c in range(2):
                dve.wait_ge(S["ht_hi"], 2 * b + c + 1)
                lo(ht_l[:, b % 2, 4 * c:4 * c + 4, :], ps[:, c, 0:4 * RB].rearrange("p (k n) -> p k n", k=4),
                   ht_h[:, b % 2, 4 * c:4 * c + 4, :], "ht_lo")
        dve.wait_ge(S["h1_sd"], 1)
        link(dve.tensor_scalar(fcol[4][:, :], fcol[3][:, :], L2_EPS, None, ALU.max))
        link(dve.reciprocal(fcol[5][:, :], fcol[4][:, :]))
        link(dve.tensor_scalar(fcol[5][:, :], fcol[5][:, :], float(F2) ** 0.5, None, ALU.mult))
        for b in range(NB):
            dve.wait_ge(S["o_mm"], b + 1)
            dve.scalar_tensor_tensor(out=o[:, b, :], in0=ps[0:RB, 3 + b, :], scalar=fcol[5][:, b:b + 1],
                                     in1=b2b[:, :], op0=ALU.mult, op1=ALU.add).then_inc(S["o_sh"], 1)
        for b in range(NB):
            dve.wait_ge(S["o_act"], b + 1)
            dve.tensor_tensor(o[:, b, :], o[:, b, :], x1r[:, b, :], ALU.add).then_inc(S["o_ready"], 1)

    @block.tensor
    def _(pe):
        def three(dst, lh, ll, rh, rl, start, stop):
            pe.matmul(dst, lh, rh, start=start, stop=False)
            pe.matmul(dst, lh, rl, start=False, stop=False)
            return pe.matmul(dst, ll, rh, start=False, stop=stop)

        def transpose_rows(n, bank, before):
            for b in range(NB):
                pe.wait_ge(S["rows_ready"], n * NB + b + 1)
                if b >= 2:
                    pe.wait_ge(S[before], b - 1)
                for k in range(KB):
                    mm = pe.transpose(ps[:, bank + b % 2, k * RB:(k + 1) * RB], rows[:, b, k * 128:(k + 1) * 128],
                                      ident[0:RB, 0:RB])
                mm.then_inc(S["rows_t"], 1)

        pe.wait_ge(S["consts"], 6)
        transpose_rows(0, 5, "xn_lo")

        def table(r, i, k):
            pe.wait_ge(S["wr_hi"], r + 1)
            pe.wait_ge(S["wr_lo"], r + 1)
            for b in range(NB):
                if first(r):
                    pe.wait_ge(S["xn_lo"], b + 1)
                else:
                    pe.wait_ge(S["hout_ready"], NB * (r - 1) + b + 1)
                cut = slice(b * RB, (b + 1) * RB)
                for kb in range(KB):
                    mm = three(ps[0:RB, b, :], xn_h[:, kb, cut], xn_l[:, kb, cut], wr_h[:, k, kb, :],
                               wr_l[:, k, kb, :], kb == 0, kb == KB - 1)
                mm.then_inc(S["table_mm"], 1)

        over_relations(pe, table)

        pe.wait_ge(S["hself_ready"], NB)

        def segment(t, i, k):
            pe.wait_ge(S["hot_ready"], t + 1)
            pe.wait_ge(S["msg_lo"], t + 1)
            for b in range(NB):
                cut = slice(b * RB, (b + 1) * RB)
                pe.matmul(ps[0:RB, b, :], hot[:, k, cut], msg_h[:, k, :], start=first(t), stop=False)
                mm = pe.matmul(ps[0:RB, b, :], hot[:, k, cut], msg_l[:, k, :], start=False, stop=final(t, MT - 1))
            mm.then_inc(S["seg_mm"], 1)

        over_messages(pe, segment)

        pe.wait_ge(S["lm_in"], 80)
        pe.wait_ge(S["cols_in"], 16)
        for kb in range(KB):
            for g in range(G):
                pe.matmul(ps[:, 7, kb * L:(kb + 1) * L], wkt[:, g, kb * 128:(kb + 1) * 128], a1w[:, g, :],
                          start=(g == 0), stop=(g == G - 1))
        for g in range(G):
            mm = pe.matmul(ps[0:L, 6, 0:1], a1w[:, g, :], colc[:, C_BK + g:C_BK + g + 1], start=(g == 0),
                           stop=(g == G - 1))
        mm.then_inc(S["a1_mm"], 1)

        pe.wait_ge(S["x1_ready"], NB)
        transpose_rows(1, 0, "xg_ready")

        pe.wait_ge(S["a1_lo"], 1)
        pe.wait_ge(S["xn_lo"], 2 * NB)
        for c in range(2):
            for kb in range(KB):
                cut = slice(c * SC, (c + 1) * SC)
                mm = three(ps[0:L, c, 0:SC], a1_h[:, kb, :], a1_l[:, kb, :], xn_h[:, kb, cut], xn_l[:, kb, cut],
                           kb == 0, kb == KB - 1)
        mm.then_inc(S["hid_mm"], 1)
        pe.wait_ge(S["hid_ready"], 1)
        for c in range(2):
            mm = pe.matmul(ps[0:L, 2 + c, 0:SC], a2w[:, :], hid[:, c * SC:(c + 1) * SC], start=True, stop=True)
        mm.then_inc(S["wt_mm"], 1)
        pe.wait_ge(S["wt_ready"], 2)
        for b in range(NB):
            mm = pe.transpose(ps[0:RB, 4, b * L:(b + 1) * L], wt[:, b * RB:(b + 1) * RB], ident[0:L, 0:L])
        mm.then_inc(S["wt_t"], 1)
        pe.wait_ge(S["wt2_ready"], 1)
        for b in range(NB):
            mm = pe.transpose(ps[0:RB, 5, b * L:(b + 1) * L], wt2[:, b * RB:(b + 1) * RB], ident[0:L, 0:L])
        mm.then_inc(S["wt_t"], 1)
        pe.wait_ge(S["w_ready"], 1)
        for b in range(NB):
            pe.matmul(ps[:, 6, 0:L], ones[0:RB, :], w[:, b, :], start=(b == 0), stop=(b == NB - 1))
        for b in range(NB):
            pe.matmul(ps[0:L, 6, 128:129], w[:, b, :], ones[0:RB, 0:1], start=(b == 0), stop=(b == NB - 1))
        for kb in range(KB):
            for b in range(NB):
                mm = pe.matmul(ps[:, 7, kb * L:(kb + 1) * L], rows[:, b, kb * 128:(kb + 1) * 128], w[:, b, :],
                               start=(b == 0), stop=(b == NB - 1))
        mm.then_inc(S["lm_mm"], 1)
        pe.wait_ge(S["ct_ready"], 1)
        pe.wait_ge(S["kv_in"], 32)
        for g in range(G):
            for kb in range(KB):
                mm = pe.matmul(ps[:, g // 4, (g % 4) * L:(g % 4 + 1) * L], wkv[:, kb, g * DK:(g + 1) * DK],
                               ct[:, kb, :], start=(kb == 0), stop=(kb == KB - 1))
            if g % 4 == 3:
                mm.then_inc(S["kc_mm"], 1)
        for c in range(2):
            for kb in range(KB):
                mm = pe.matmul(ps[0:L, 2 + c, :], ct[:, kb, :], wkv[:, kb, G * DK + c * 512:G * DK + (c + 1) * 512],
                               start=(kb == 0), stop=(kb == KB - 1))
        mm.then_inc(S["vc_mm"], 1)
        pe.wait_ge(S["kf_ready"], 1)
        for g in range(G):
            mm = pe.matmul(ps[0:HG, 4 + g // 4, (g % 4) * L:(g % 4 + 1) * L],
                           colc[:, C_BQ + g * HG:C_BQ + (g + 1) * HG], kf[:, g, :], start=True, stop=True)
        mm.then_inc(S["bq_mm"], 1)

        def queries(v, kb):
            if kb == 0:
                pe.wait_ge(S["wq_lo"], HU * (v + 1))
            if kb > 0 or not first(v):
                pe.wait_ge(S["p_lo"], KB * v + kb)
            g = v // UG
            for h in range(HU):
                cut = slice(kb * 128, (kb + 1) * 128)
                rh = kc_h[:, bass.ds(g, 1), :].rearrange("p a l -> p (a l)")
                rl = kc_l[:, bass.ds(g, 1), :].rearrange("p a l -> p (a l)")
                mm = three(ps[:, 7, h * L:(h + 1) * L], wq_h[:, h, cut], wq_l[:, h, cut], rh, rl, True, True)
            mm.then_inc(S["p_mm"], 1)

        pe.wait_ge(S["lm_done"], 1)
        for kb in range(KB):
            queries(0, kb)

        def hidden(v, k, n):
            f, b = n // NB, n % NB
            if n == 0:
                pe.wait_ge(S["z_lo"], HU * (v + 1))
            if b == 0:
                pe.wait_ge(S["w1_lo"], HU * (2 * v + f + 1))
            if n == 0:
                if not first(v):
                    pe.wait_ge(S["h_acc"], HO * v)
            elif n > 1:
                pe.wait_ge(S["h_acc"], HO * v + n - 1)
            cut = slice(b * RB, (b + 1) * RB)
            for h in range(HU):
                mm = three(ps[0:RB, 2 + n % 2, :], z_h[k][:, h, cut], z_l[k][:, h, cut], w1_h[f][:, h, :],
                           w1_l[f][:, h, :], h == 0, h == HU - 1)
            mm.then_inc(S["h_mm"], 1)

        def unit_step(v, k):
            def scores(j):
                q = NB * v + j
                if j == 0:
                    pe.wait_ge(S["p_lo"], KB * (v + 1))
                    pe.wait_ge(S["brow_in"], 16 * (v + 1))
                if j >= 2:
                    pe.wait_ge(S["shifted"], q - 1)
                elif not first(v):
                    pe.wait_ge(S["shifted"], NB * v)
                dst = ps[0:RB, j % 2, 0:UC]
                cut = slice(j * RB, (j + 1) * RB)
                for kb in range(KB):
                    three(dst, xn_h[:, kb, cut], xn_l[:, kb, cut], p_h[:, kb, :], p_l[:, kb, :], kb == 0, False)
                pe.matmul(dst, ones2[:, :], brow[:, :], start=False, stop=True).then_inc(S["score_mm"], 1)

            def turn(j):
                q = NB * v + j
                pe.wait_ge(S["prob_ready"], q + 1)
                if j > 0 or not first(v):
                    pe.wait_ge(S["att_lo"], q)
                for h in range(HU):
                    mm = pe.transpose(ps[0:L, 4, h * RB:(h + 1) * RB], prob[:, j % SR, h * L:(h + 1) * L],
                                      ident[0:RB, 0:RB])
                mm.then_inc(S["prob_t"], 1)

            def values(h):
                q = HU * v + h
                if h == 0:
                    pe.wait_ge(S["att_lo"], NB * (v + 1))
                    pe.wait_ge(S["unit_cols"], 3 * (v + 1))
                if h > 0 or not first(v):
                    pe.wait_ge(S["z_lo"], q)
                    pe.wait_ge(S["z_sq"], q)
                for c in range(2):
                    cut = slice(c * SC, (c + 1) * SC)
                    mm = three(ps[:, 5 + c, 0:SC], vcu_h[:, :], vcu_l[:, :], at_h[:, h, cut], at_l[:, h, cut],
                               True, True)
                mm.then_inc(S["z_mm"], 1)

            def h1(n):
                if not first(v):
                    hidden(v - 1, 1 - k, n)

            def p(kb):
                if not final(v, U - 1):
                    queries(v + 1, kb)

            scores(0)
            h1(0)
            scores(1)
            h1(1)
            turn(0)
            scores(2)
            h1(2)
            turn(1)
            scores(3)
            h1(3)
            turn(2)
            scores(4)
            p(0)
            h1(4)
            turn(3)
            p(1)
            h1(5)
            turn(4)
            p(2)
            h1(6)
            values(0)
            p(3)
            h1(7)
            values(1)
            h1(8)
            values(2)
            h1(9)
            values(3)

        over_units(pe, unit_step)
        for n in range(HO):
            hidden(U - 1, 1, n)
        pe.wait_ge(S["z_acc"], HU * U + 1)
        for b in range(NB):
            mm = pe.matmul(ps[0:RB, 4, b:b + 1], zacc[:, b * RB:(b + 1) * RB], ones[:, 0:1], start=True, stop=True)
        mm.then_inc(S["n_mm"], 1)
        for b in range(NB):
            pe.wait_ge(S["h1_ready"], b + 1)
            for c in range(2):
                if b > 0:
                    pe.wait_ge(S["ht_lo"], 2 * b + c - 1)
                for k in range(4):
                    f = 4 * c + k
                    mm = pe.transpose(ps[:, c, k * RB:(k + 1) * RB], acc[:, b, f * 128:(f + 1) * 128],
                                      ident[0:RB, 0:RB])
                mm.then_inc(S["h1_t"], 1)
            pe.wait_ge(S["ht_lo"], 2 * b + 2)
            pe.wait_ge(S["w2_lo"], FB)
            if b == 1:
                pe.wait_ge(S["n_sd"], 1)
            for f in range(FB):
                mm = three(ps[0:RB, 3 + b, :], ht_h[:, b % 2, f, :], ht_l[:, b % 2, f, :], w2_h[:, f, :],
                           w2_l[:, f, :], f == 0, f == FB - 1)
            mm.then_inc(S["o_mm"], 1)

    ctx.close()


def kernel(**inputs):
    import numpy as np
    import concourse.bacc as bacc
    from concourse.bass_utils import run_bass_kernel_spmd

    a = {k: np.asarray(v) for k, v in inputs.items()}
    f = "L0_ffn_"

    def by_partition(m):
        return m.reshape(-1, 128, m.shape[-1]).transpose(1, 0, 2)

    def col(v):
        return v.reshape(-1, 128).T

    w_rel = np.concatenate([a["L0_gnn_W_rel"], a["L0_gnn_W_self"][None]], 0).transpose(0, 2, 1)
    data = {
        "x": a["x"], "src": a["src"], "dst": a["dst"], "etype": a["edge_type_8"],
        "w_rel_t": w_rel.reshape(R2 + 1, KB, 128, D).transpose(0, 2, 1, 3).reshape(R2 + 1, 128, KB * D),
        "b_rel": np.concatenate([a["L0_gnn_b_rel"], a["L0_gnn_b_self"][None]], 0),
        "cols": np.concatenate([col(a[f + "gamma_norm"]), col(a[f + "wz_g2"]), col(a[f + "Wkv_b"][:G * DK]),
                                col(a[f + "Wq_b"]), col(a[f + "wz_g1"])], 1),
        "wk_t": by_partition(a[f + "Wkv_w"][:, :G * DK].T),
        "w_kv": by_partition(a[f + "Wkv_w"]),
        "aw1": by_partition(a[f + "aw1_w"]), "aw1_b": a[f + "aw1_b"][:, None],
        "aw2": a[f + "aw2_w"], "aw2_b": a[f + "aw2_b"][:, None],
        "b_v": a[f + "Wkv_b"][None, G * DK:],
        "wq_t": a[f + "Wq_w"].T.reshape(U, HU, 128, D).transpose(0, 2, 1, 3).reshape(U, 128, HU * D),
        "wz_w1": a[f + "wz_w1"].reshape(U, HU, 128, 2, FH).transpose(0, 3, 2, 1, 4).reshape(U, 2, 128, HU * FH),
        "b1": a[f + "wz_b1"][None], "w2": by_partition(a[f + "wz_w2"]), "b2": a[f + "wz_b2"][None],
    }
    nc = bacc.Bacc("TRN2", target_bir_lowering=False, num_devices=1)
    arrays, args = {}, []
    for name, v in data.items():
        v = np.ascontiguousarray(v)
        arrays[f"in_{name}"] = v
        args.append(nc.dram_tensor(f"in_{name}", v.shape, mybir.dt.from_np(v.dtype), kind="ExternalInput").ap())
    args.append(nc.dram_tensor("out", (N, D), F32, kind="ExternalOutput").ap())
    build_layer(nc, *args)
    r = run_bass_kernel_spmd(nc, [arrays], core_ids=[0])
    return r.results[0]["out"]
```

```python
from contextlib import ExitStack

import concourse.bass as bass
from concourse import mybir

F32 = mybir.dt.float32
F32R = mybir.dt.float32r
I32 = mybir.dt.int32
ALU = mybir.AluOpType
ACT = mybir.ActivationFunctionType
AX = mybir.AxisListType

N, D = 625, 512
NB, RB = 5, 125
KB = D // 128
E = 10000
R = 8
R2 = 2 * R
EP = 125
ET = E // EP
MT = 2 * ET
MP = 128
MS = MT * EP // MP + NB
MR = 4
G, HG, DK, L = 8, 16, 128, 100
HU = 4
U = G * HG // HU
UG = HG // HU
UC = HU * L
F2 = 1024
FH = F2 // 2
FB = F2 // 128
SPAD = 628
SC = SPAD // 2
SR = 3
HO = 2 * NB
LN_EPS = 1e-5
L2_EPS = 1e-12

C_GAMMA = 0
C_G2 = C_GAMMA + KB
C_BK = C_G2 + FB
C_BQ = C_BK + G
C_G1 = C_BQ + G * HG
C_END = C_G1 + G * HG


def build_layer(nc, x, src, dst, etype, w_rel_t, b_rel, cols, wk_t, w_kv, aw1, aw1_b, aw2, aw2_b, b_v,
                wq_t, wz_w1, b1, w2, b2, out):
    ctx = ExitStack()

    def sem(name):
        return ctx.enter_context(nc.semaphore(name))

    h_table = nc.dram_tensor("h_table", [R2 * N, D], F32, kind="Internal").ap()
    x1_stash = nc.dram_tensor("x1_stash", [N, D], F32, kind="Internal").ap()
    slots = nc.dram_tensor("slots", [MP * MS, 2], F32, kind="Internal").ap()
    bqk_rows = nc.dram_tensor("bqk_rows", [2, G * HG * L], F32, kind="Internal").ap()

    ps = ctx.enter_context(nc.psum_tensor("ps", [128, 8, 512], F32))

    class Shelf:
        def __init__(self, at):
            self.at = at

        def put(self, name, shape, dt=F32):
            size = 4
            for n in shape[1:]:
                size *= n
            t = nc.alloc_sbuf_tensor_at(name, shape, dt, offset=self.at)
            self.at += (size + 31) // 32 * 32
            return t

    whole = Shelf((nc.sbuf_base + 63) // 64 * 64)
    ident = whole.put("ident", [128, 128])
    ones = whole.put("ones", [128, 128])
    ones2 = whole.put("ones2", [2, RB], F32R)
    colc = whole.put("colc", [128, C_END])
    wq_raw = whole.put("wq_raw", [128, HU, D])
    w1_raw = whole.put("w1_raw", [128, HU, FH])
    kc_h = whole.put("kc_h", [128, G, L], F32R)
    kc_l = whole.put("kc_l", [128, G, L], F32R)
    vc_h = whole.put("vc_h", [L, G, DK], F32R)
    vc_l = whole.put("vc_l", [L, G, DK], F32R)
    xn_at = whole.at
    xn_h = whole.put("xn_h", [128, KB, SPAD], F32R)
    xn_l = whole.put("xn_l", [128, KB, SPAD], F32R)

    graph = Shelf(whole.at)
    xin = graph.put("xin", [RB, NB, D])
    hself_at = graph.at
    junk2 = graph.put("junk2", [RB, NB, D])
    rows = graph.put("rows", [RB, NB, D])
    x1_at = graph.at
    x1 = graph.put("x1", [RB, NB, D])
    stat = graph.put("stat", [RB, NB, 6])
    mv = graph.put("mv", [RB, NB, 2])
    col = [graph.put(f"col{i}", [RB, NB]) for i in range(8)]
    var1, sdev1, var2, sdev2 = (c[:, :] for c in col[0:4])
    rdev = col[4]
    l2ss, l2sd, l2rc = col[5], col[6][:, :], col[7]
    rows2_at = graph.at
    wkv = graph.put("wkv", [128, KB, 2 * G * DK])
    bvb = graph.put("bvb", [L, G * DK])
    table = Shelf(graph.at)
    wr_raw = table.put("wr_raw", [128, 2, KB, D])
    wr_h = table.put("wr_h", [128, 2, KB, D], F32R)
    wr_l = table.put("wr_l", [128, 2, KB, D], F32R)
    hout = table.put("hout", [RB, NB, D])
    brel_at = table.at
    brel = table.put("brel", [RB, 2, D])
    side = Shelf(table.at)
    srt = side.put("srt", [MP, MS, 2])
    msg = side.put("msg", [MP, MR, D])
    hot = side.put("hot", [MP, MR, 128], F32R)
    node = side.put("node", [MP, RB])
    tile_no = side.put("tile_no", [1, MS])
    tile_block = side.put("tile_block", [1, MS], I32)
    zero = side.put("zero", [1, D], F32R)
    assert side.at <= nc.sbuf_usable_end
    early = Shelf(hself_at)
    above = early.put("above", [EP, NB + 1, MT])
    inb = early.put("inb", [EP, NB, MT])
    rank = early.put("rank", [EP, NB, MT])
    assert early.at <= hself_at + 4 * NB * D
    early = Shelf(x1_at)
    cs = early.put("cs", [ET, 2, NB, EP])
    later_t = early.put("later_t", [ET, 2, MT + 1])
    later_p = early.put("later_p", [EP, EP])
    pk = early.put("pk", [EP, MT, 2])
    ei = early.put("ei", [EP, 3, ET], I32)
    assert early.at <= x1_at + 4 * NB * D
    early = Shelf(rows2_at)
    recv = early.put("recv", [EP, MT])
    send = early.put("send", [EP, MT])
    relrow = early.put("relrow", [EP, MT])
    nabove = early.put("nabove", [EP, MT])
    pos = early.put("pos", [EP, MT])
    pos_i = early.put("pos_i", [EP, MT], I32)
    pos_lane = early.put("pos_lane", [EP, MT], I32)
    pos_tile = early.put("pos_tile", [EP, MT], I32)
    slot = early.put("slot", [EP, MT], I32)
    count_i = early.put("count_i", [EP, NB], I32)
    tiles_i = early.put("tiles_i", [EP, NB], I32)
    tiles = early.put("tiles", [EP, NB])
    base = early.put("base", [EP, NB])
    base_m = early.put("base_m", [EP, NB])
    tb = [early.put(f"tb{i}", [1, MS]) for i in range(2)]
    assert early.at <= rows2_at + 4 * 2 * G * DK * KB
    gat = Shelf(graph.at)
    msg_h = gat.put("msg_h", [MP, MR, D], F32R)
    msg_l = gat.put("msg_l", [MP, MR, D], F32R)
    LM_BYTES = 34816
    gat = Shelf(graph.at + LM_BYTES)
    wkt = gat.put("wkt", [128, G, D])
    a1w = gat.put("a1w", [128, G, L])
    a2w = gat.put("a2w", [L, L])
    rowc = gat.put("rowc", [L, 2])
    assert gat.at <= brel_at
    lm = Shelf(graph.at)
    a1_h = lm.put("a1_h", [128, KB, L], F32R)
    a1_l = lm.put("a1_l", [128, KB, L], F32R)
    c1 = lm.put("c1", [L, 1])
    xg = lm.put("xg", [128, 2, KB, RB])
    hid = lm.put("hid", [L, SPAD])
    wt = lm.put("wt", [L, N])
    wt2 = lm.put("wt2", [L, N])
    wtc = lm.put("wtc", [L, 4])
    w = lm.put("w", [RB, NB, L])
    ct = lm.put("ct", [128, KB, L])
    swb = lm.put("swb", [128, L])
    swc = lm.put("swc", [L, 1])
    kf = lm.put("kf", [128, G, L])
    vf = lm.put("vf", [L, G, DK])
    bq_h = lm.put("bq_h", [HG, G, L], F32R)
    bq_l = lm.put("bq_l", [HG, G, L], F32R)
    assert lm.at <= graph.at + LM_BYTES

    att = Shelf(whole.at)
    wq_h = att.put("wq_h", [128, HU, D], F32R)
    wq_l = att.put("wq_l", [128, HU, D], F32R)
    p_at = att.at
    p_h = att.put("p_h", [128, KB, UC], F32R)
    p_l = att.put("p_l", [128, KB, UC], F32R)
    prob = att.put("prob", [RB, SR, UC])
    at_h = att.put("at_h", [L, HU, SPAD], F32R)
    at_l = att.put("at_l", [L, HU, SPAD], F32R)
    z_h = [att.put(f"z_h{k}", [128, HU, SPAD], F32R) for k in range(2)]
    z_l = [att.put(f"z_l{k}", [128, HU, SPAD], F32R) for k in range(2)]
    zsq = att.put("zsq", [128, SPAD])
    w1_h = [att.put(f"w1_h{f}", [128, HU, FH], F32R) for f in range(2)]
    w1_l = [att.put(f"w1_l{f}", [128, HU, FH], F32R) for f in range(2)]
    brow = att.put("brow", [2, UC], F32R)
    vcu_h = att.put("vcu_h", [L, DK], F32R)
    vcu_l = att.put("vcu_l", [L, DK], F32R)
    g1u = att.put("g1u", [128, HU])
    smax = att.put("smax", [RB, HU])
    ssum = att.put("ssum", [RB, HU])
    srec = att.put("srec", [RB, SR, HU])
    acc = att.put("acc", [RB, NB, F2])
    zacc = att.put("zacc", [128, SPAD])
    assert att.at <= nc.sbuf_usable_end, (att.at, nc.sbuf_usable_end)

    assert p_at - whole.at >= 4 * FB * D
    w2_raw = Shelf(whole.at).put("w2_raw", [128, FB, D])
    fin = Shelf(p_at)
    w2_h = fin.put("w2_h", [128, FB, D], F32R)
    w2_l = fin.put("w2_l", [128, FB, D], F32R)
    tail = Shelf(xn_at)
    b1b = tail.put("b1b", [RB, F2])
    b2b = tail.put("b2b", [RB, D])
    x1r = tail.put("x1r", [RB, NB, D])
    assert tail.at <= whole.at
    last = Shelf(fin.at)
    ht_h = last.put("ht_h", [128, 2, FB, RB], F32R)
    ht_l = last.put("ht_l", [128, 2, FB, RB], F32R)
    junk = last.put("junk", [RB, F2])
    o = last.put("o", [RB, NB, D])
    fcol = [last.put(f"fcol{i}", [RB, NB]) for i in range(6)]

    S = {n: sem(n) for n in (
        "x_in", "edges_in", "cols_in", "consts", "pad_zero",
        "dve", "ln_var", "ln_sd", "rows_ready", "rows_t", "xn_hi", "xn_lo", "xg_ready",
        "wr_hi", "wr_lo", "table_mm", "hout_ready", "edge_cols", "blocks_ready", "pk_step", "pk_ready", "cs_mm", "cs_ready", "rank_mm", "slot_ready", "srt_pad", "slots_pad", "scattered", "srt_in",
        "hot_ready", "msg_hi", "msg_lo", "seg_mm", "x1_ready", "x1_saved",
        "lm_in", "lm_in2", "kv_in", "l2_sq", "l2_sd", "l2_in",
        "a1_mm", "a1_hi", "a1_lo", "c1_ready", "hid_mm", "hid_ready", "wt_mm", "wt_ready", "wt2_max", "wt2_exp",
        "wt2_ready", "wt_t", "w_sh", "w_exp", "w_ready", "lm_mm", "lm_ev", "ct_ready", "kc_mm", "kf_ready", "kc_hi",
        "kc_lo", "vc_mm", "vf_ready", "vc_hi", "vc_lo", "bq_mm", "bq_hi", "bq_lo", "bq_saved", "lm_done",
        "wq_in", "wq_hi", "wq_lo", "w1_in", "w1_hi", "w1_lo", "brow_in",
        "p_mm", "p_hi", "p_lo", "score_mm", "max_ready", "shifted", "exp_ready", "sum_ready", "rec_ready", "prob_ready",
        "prob_t", "att_hi", "att_lo", "unit_cols", "z_mm", "z_hi", "z_lo", "z_sq", "z_acc", "h_mm", "h_acc", "acc_zero",
        "w2_in", "w2_hi", "w2_lo", "fin_in", "n_mm", "n_sd", "h_sh", "h1_ready", "h1_sq", "h1_sd", "h1_rec",
        "h1_t", "ht_hi", "ht_lo", "o_mm", "o_sh", "o_act", "o_ready", "out_done",
    )}
    wr_in = [sem(f"wr_in{k}") for k in range(2)]
    brel_in = [sem(f"brel_in{k}") for k in range(2)]
    h_saved = [sem(f"h_saved{b}") for b in range(NB)]
    msg_in = [sem(f"msg_in{k}") for k in range(MR)]

    block = ctx.enter_context(nc.Block())

    def spread(ap, shape):
        return ap.unsqueeze(len(shape) - 1).to_broadcast(shape)

    def over_relations(eng, step):
        step(0, 0, 0)
        step(1, 0, 1)
        with eng.Fori(1, R2 // 2) as i:
            step(2 * i, i, 0)
            step(2 * i + 1, i, 1)
        step(R2, R2 // 2, 0)

    def over_messages(eng, step):
        for k in range(MR):
            step(k, 0, k)
        with eng.Fori(1, MS // MR) as i:
            for k in range(MR):
                step(i * MR + k, i, k)
        for k in range(MS % MR):
            step(MS - MS % MR + k, MS // MR, k)

    def over_units(eng, step):
        step(0, 0)
        step(1, 1)
        with eng.Fori(1, U // 2 - 1) as i:
            step(2 * i, 0)
            step(2 * i + 1, 1)
        step(U - 2, 0)
        step(U - 1, 1)

    def first(v):
        return isinstance(v, int) and v == 0

    def final(v, n):
        return isinstance(v, int) and v == n

    @block.sync
    def _(sp):
        for n, a in enumerate((src, dst, etype)):
            sp.dma_start(ei[:, n, :], a.rearrange("(p t) -> p t", t=ET)).then_inc(S["edges_in"], 16)
        sp.dma_start(xin[:, :, :], x.rearrange("(b p) d -> p b d", p=RB)).then_inc(S["x_in"], 16)
        sp.dma_start(colc[:, :], cols).then_inc(S["cols_in"], 16)

        def load_wr(r, k):
            sp.dma_start(wr_raw[:, k, :, :].rearrange("p b d -> p (b d)"),
                         w_rel_t[bass.ds(r, 1), :, :].rearrange("a p n -> p (a n)")).then_inc(wr_in[k], 16)

        def load_brel(r, k):
            sp.dma_start(brel[:, k, :], b_rel[bass.ds(r, 1), :].to_broadcast([RB, D])).then_inc(brel_in[k], 16)

        for k in range(2):
            load_wr(k, k)
            load_brel(k, k)
        sp.wait_ge(S["srt_pad"], 2)
        sp.dma_start(slots.rearrange("(p t) c -> p t c", t=MS), srt[:, :, :]).then_inc(S["slots_pad"], 16)
        sp.dma_start(bvb[:, :], b_v.to_broadcast([L, G * DK])).then_inc(S["kv_in"], 16)
        sp.dma_start(wq_raw[:, :, :].rearrange("p h d -> p (h d)"), wq_t[0]).then_inc(S["wq_in"], 16)
        sp.dma_start(w1_raw[:, :, :].rearrange("p h d -> p (h d)"), wz_w1[0, 0]).then_inc(S["w1_in"], 16)

        def table_step(r, i, k):
            if final(r, R2):
                return
            more = not final(r, R2 - 1)
            if more:
                sp.wait_ge(S["wr_hi"], r + 1)
                sp.wait_ge(S["wr_lo"], r + 1)
                load_wr(r + 2, k)
            for b in range(NB):
                sp.wait_ge(S["hout_ready"], NB * r + b + 1)
                sp.dma_start(h_table[bass.ds(r * N + b * RB, RB), :], hout[:, b, :]).then_inc(h_saved[b], 16)
            if more:
                load_brel(r + 2, k)

        step = table_step
        step(0, 0, 0)
        step(1, 0, 1)
        with sp.Fori(1, R2 // 2 - 1) as i:
            step(2 * i, i, 0)
            step(2 * i + 1, i, 1)
        step(R2 - 2, R2 // 2 - 1, 0)
        step(R2 - 1, R2 // 2 - 1, 1)

        sp.wait_ge(S["scattered"], 16 * MT)
        sp.dma_start(srt[:, :, :], slots.rearrange("(p t) c -> p t c", t=MS)).then_inc(S["srt_in"], 16)
        sp.dma_start(wkv[:, :, :], w_kv).then_inc(S["kv_in"], 16)
        sp.wait_ge(S["table_mm"], NB * (R2 + 1))
        for b in range(NB):
            sp.wait_ge(h_saved[b], 16 * R2)
        sp.dma_start(wkt[:, :, :], wk_t).then_inc(S["lm_in"], 16)
        sp.dma_start(a1w[:, :, :], aw1).then_inc(S["lm_in"], 16)
        sp.dma_start(a2w[:, :], aw2).then_inc(S["lm_in"], 16)
        sp.dma_start(rowc[:, 0:1], aw1_b).then_inc(S["lm_in"], 16)
        sp.dma_start(rowc[:, 1:2], aw2_b).then_inc(S["lm_in"], 16)

        sp.wait_ge(S["x1_ready"], NB)
        sp.dma_start(x1_stash.rearrange("(b p) d -> p b d", p=RB), x1[:, :, :]).then_inc(S["x1_saved"], 16)

        sp.wait_ge(S["bq_hi"], 1)
        sp.dma_start(bqk_rows[0:1, :].rearrange("a (g h l) -> h (a g) l", g=G, h=HG), bq_h[:, :, :].bitcast(F32))\
            .then_inc(S["bq_saved"], 16)
        sp.wait_ge(S["bq_lo"], 1)
        sp.dma_start(bqk_rows[1:2, :].rearrange("a (g h l) -> h (a g) l", g=G, h=HG), bq_l[:, :, :].bitcast(F32))\
            .then_inc(S["bq_saved"], 16)
        sp.wait_ge(S["bq_saved"], 32)

        def load_w1(v, f):
            sp.wait_ge(S["w1_lo"], HU * (2 * v + f))
            sp.wait_ge(S["w1_hi"], 2 * v + f)
            sp.dma_start(w1_raw[:, :, :].rearrange("p h d -> p (h d)"),
                         wz_w1[bass.ds(v, 1), f].rearrange("a p n -> p (a n)")).then_inc(S["w1_in"], 16)

        def load_wq(v):
            sp.wait_ge(S["wq_lo"], HU * v)
            sp.wait_ge(S["wq_hi"], v)
            sp.dma_start(wq_raw[:, :, :].rearrange("p h d -> p (h d)"),
                         wq_t[bass.ds(v, 1)].rearrange("a p n -> p (a n)")).then_inc(S["wq_in"], 16)

        def load_brow(v):
            sp.dma_start(brow[:, :].bitcast(F32), bqk_rows[:, bass.ds(v * UC, UC)]).then_inc(S["brow_in"], 16)

        sp.wait_ge(S["lm_done"], 1)
        load_brow(0)
        load_wq(1)

        def unit_step(v, k):
            if not first(v):
                load_w1(v, 0)
            if not (final(v, U - 2) or final(v, U - 1)):
                load_wq(v + 2)
            if not final(v, U - 1):
                sp.wait_ge(S["score_mm"], NB * (v + 1))
                load_brow(v + 1)
            load_w1(v, 1)

        over_units(sp, unit_step)

        sp.wait_ge(S["p_mm"], KB * U)
        sp.dma_start(w2_raw[:, :, :], w2).then_inc(S["w2_in"], 16)
        sp.wait_ge(S["score_mm"], NB * U)
        sp.dma_start(b1b[:, :], b1.to_broadcast([RB, F2])).then_inc(S["fin_in"], 16)
        sp.dma_start(b2b[:, :], b2.to_broadcast([RB, D])).then_inc(S["fin_in"], 16)
        sp.wait_ge(S["x1_saved"], 16)
        sp.dma_start(x1r[:, :, :], x1_stash.rearrange("(b p) d -> p b d", p=RB)).then_inc(S["fin_in"], 16)
        for b in range(NB):
            sp.wait_ge(S["o_ready"], b + 1)
            sp.dma_start(out[b * RB:(b + 1) * RB, :], o[:, b, :]).then_inc(S["out_done"], 16)
        sp.wait_ge(S["out_done"], 16 * NB)

    @block.gpsimd
    def _(pool):
        pool.memset(ident[:, :], 0.0).then_inc(S["consts"], 1)
        pool.wait_ge(S["consts"], 1)
        pool.affine_select(out=ident[:, :], in_=ident[:, :], compare_op=ALU.not_equal, fill=1.0, base=0,
                           pattern=[[-1, 128]], channel_multiplier=1).then_inc(S["consts"], 1)
        pool.memset(ones[:, :], 1.0).then_inc(S["consts"], 1)
        pool.memset(ones2[:, :].bitcast(F32), 1.0).then_inc(S["consts"], 1)
        pool.memset(xn_h[:, :, N:SPAD].bitcast(F32), 0.0).then_inc(S["consts"], 1)
        pool.memset(xn_l[:, :, N:SPAD].bitcast(F32), 0.0).then_inc(S["consts"], 1)

        pool.memset(srt[:, :, 0], 0.0).then_inc(S["srt_pad"], 1)
        pool.memset(srt[:, :, 1], -1.0).then_inc(S["srt_pad"], 1)
        pool.iota(node[:, :], [[1, RB]], base=0, channel_multiplier=0,
                  allow_small_or_imprecise_dtypes=True).then_inc(S["consts"], 1)
        pool.iota(tile_no[:, :], [[1, MS]], base=0, channel_multiplier=0,
                  allow_small_or_imprecise_dtypes=True).then_inc(S["consts"], 1)
        pool.memset(later_t[:, :, :], 1.0).then_inc(S["consts"], 1)
        pool.memset(later_p[:, :], 1.0).then_inc(S["consts"], 1)
        pool.memset(zero[:, :].bitcast(F32), 0.0).then_inc(S["consts"], 1)
        pool.wait_ge(S["consts"], 11)
        for h in range(2):
            pool.affine_select(out=later_t[:, h, :], in_=later_t[:, h, :], compare_op=ALU.is_ge, fill=0.0,
                               base=-h * ET - 1, pattern=[[1, MT + 1]], channel_multiplier=-1).then_inc(S["consts"], 1)
        pool.affine_select(out=later_p[:, :], in_=later_p[:, :], compare_op=ALU.is_ge, fill=0.0,
                           base=-1, pattern=[[1, EP]], channel_multiplier=-1).then_inc(S["consts"], 1)

        pool.wait_ge(S["edges_in"], 48)
        for n, part in ((0, slice(0, ET)), (1, slice(ET, MT))):
            pool.tensor_copy(recv[:, part], ei[:, n, :]).then_inc(S["edge_cols"], 1)
            pool.tensor_copy(send[:, part], ei[:, 1 - n, :]).then_inc(S["edge_cols"], 1)
        pool.tensor_scalar(relrow[:, 0:ET], ei[:, 2, :], float(N), None, ALU.mult).then_inc(S["edge_cols"], 1)
        pool.tensor_scalar(relrow[:, ET:MT], ei[:, 2, :], float(N), float(R * N), ALU.mult, ALU.add)\
            .then_inc(S["edge_cols"], 1)
        pool.memset(above[:, 0, :], 1.0).then_inc(S["edge_cols"], 1)
        pool.memset(above[:, NB, :], 0.0).then_inc(S["edge_cols"], 1)
        pool.wait_ge(S["edge_cols"], 8)
        for b in range(1, NB):
            pool.tensor_scalar(above[:, b, :], recv[:, :], float(b * RB), None, ALU.is_ge).then_inc(S["edge_cols"], 1)
        pool.wait_ge(S["edge_cols"], 8 + NB - 1)
        pool.tensor_tensor(inb[:, :, :], above[:, 0:NB, :], above[:, 1:NB + 1, :], ALU.subtract)\
            .then_inc(S["blocks_ready"], 1)
        pool.tensor_tensor(relrow[:, :], relrow[:, :], send[:, :], ALU.add).then_inc(S["pk_step"], 1)
        pool.tensor_tensor(nabove[:, :], above[:, 1, :], above[:, 2, :], ALU.add).then_inc(S["pk_step"], 1)
        for b in range(3, NB):
            pool.wait_ge(S["pk_step"], b - 1)
            pool.tensor_tensor(nabove[:, :], nabove[:, :], above[:, b, :], ALU.add).then_inc(S["pk_step"], 1)
        pool.wait_ge(S["pk_step"], NB - 1)
        pool.tensor_scalar(nabove[:, :], nabove[:, :], float(RB), None, ALU.mult).then_inc(S["pk_step"], 1)
        pool.wait_ge(S["pk_step"], NB)
        pool.tensor_copy(pk[:, :, 0].bitcast(I32), relrow[:, :]).then_inc(S["pk_ready"], 1)
        pool.tensor_tensor(pk[:, :, 1], recv[:, :], nabove[:, :], ALU.subtract).then_inc(S["pk_ready"], 1)

        pool.wait_ge(S["pk_ready"], 2)
        pool.wait_ge(S["slots_pad"], 16)
        pool.wait_ge(S["slot_ready"], 1)
        for t in range(MT):
            pool.indirect_dma_start(slots, bass.IndirectOffsetOnAxis(ap=slot[:, t:t + 1], axis=0), pk[:, t, :], None)\
                .then_inc(S["scattered"], 16)

        for b in range(NB):
            pool.wait_ge(h_saved[b], 16 * R2)
        pool.wait_ge(S["srt_in"], 16)

        for t in range(MS):
            k = t % MR
            if t >= MR:
                pool.wait_ge(S["msg_hi"], t + 1 - MR)
                pool.wait_ge(S["msg_lo"], t + 1 - MR)
            pool.indirect_dma_start(msg[:, k, :], None, h_table,
                                    bass.IndirectOffsetOnAxis(ap=srt[:, t, 0:1].bitcast(I32), axis=0))\
                .then_inc(msg_in[k], 16)

        pool.wait_ge(S["lm_done"], 1)
        for a in (at_h, at_l):
            pool.memset(a[:, :, N:SPAD].bitcast(F32), 0.0).then_inc(S["pad_zero"], 1)
        pool.memset(acc[:, :, :], 0.0).then_inc(S["acc_zero"], 1)
        pool.memset(zacc[:, :], 0.0).then_inc(S["z_acc"], 1)

        def split_w1(v, f, heads):
            pool.wait_ge(S["w1_hi"], 2 * v + f + 1)
            for h in heads:
                pool.tensor_tensor(w1_l[f][:, h, :], w1_raw[:, h, :], w1_h[f][:, h, :].bitcast(F32),
                                   ALU.subtract).then_inc(S["w1_lo"], 1)

        def split_wq(v, heads):
            pool.wait_ge(S["wq_hi"], v + 1)
            for h in heads:
                pool.tensor_tensor(wq_l[:, h, :], wq_raw[:, h, :], wq_h[:, h, :].bitcast(F32),
                                   ALU.subtract).then_inc(S["wq_lo"], 1)

        split_wq(0, range(HU))

        def unit_step(v, k):
            g = v // UG
            if not first(v):
                pool.wait_ge(S["z_mm"], HU * v)
                pool.wait_ge(S["z_hi"], HU * v)
                pool.wait_ge(S["z_lo"], HU * v)
            pool.tensor_copy(vcu_h[:, :], vc_h[:, bass.ds(g, 1), :].rearrange("p a d -> p (a d)").bitcast(F32)).then_inc(S["unit_cols"], 1)
            pool.tensor_copy(vcu_l[:, :], vc_l[:, bass.ds(g, 1), :].rearrange("p a d -> p (a d)").bitcast(F32)).then_inc(S["unit_cols"], 1)
            pool.tensor_copy(g1u[:, :], colc[:, bass.ds(C_G1 + v * HU, HU)]).then_inc(S["unit_cols"], 1)

            def normalise(j):
                pool.wait_ge(S["rec_ready"], NB * v + j + 1)
                pj = prob[:, j % SR, :].rearrange("p (h l) -> p h l", h=HU)
                pool.tensor_tensor(pj, pj, spread(srec[:, j % SR, :], [RB, HU, L]), ALU.mult)\
                    .then_inc(S["prob_ready"], 1)

            more = not final(v, U - 1)
            normalise(0)
            if not first(v):
                split_w1(v - 1, 1, range(0, 3))
            normalise(1)
            if not first(v):
                split_w1(v - 1, 1, range(3, 4))
            if more:
                split_wq(v + 1, range(0, 1))
            normalise(2)
            if more:
                split_wq(v + 1, range(1, 3))
            normalise(3)
            if more:
                split_wq(v + 1, range(3, 4))
            normalise(4)
            split_w1(v, 0, range(HU))
            for h in range(HU):
                pool.wait_ge(S["z_sq"], HU * v + h + 1)
                pool.wait_ge(S["z_acc"], HU * v + h + 1)
                pool.tensor_tensor(zacc[:, :], zacc[:, :], zsq[:, :], ALU.add).then_inc(S["z_acc"], 1)

        over_units(pool, unit_step)
        split_w1(U - 1, 1, range(HU))

    @block.scalar
    def _(act):
        def hi(dst, source, done):
            nc.scalar.activation(dst, source, ACT.Copy).then_inc(S[done], 1)

        act.wait_ge(S["ln_var"], 1)
        nc.scalar.activation(sdev1, var1, ACT.Sqrt).then_inc(S["ln_sd"], 1)

        def split_wr(r, i, k):
            act.wait_ge(wr_in[k], 16 * (i + 1))
            if not first(i):
                act.wait_ge(S["table_mm"], NB * (r - 1))
            hi(wr_h[:, k, :, :], wr_raw[:, k, :, :], "wr_hi")

        split_wr(0, 0, 0)
        act.wait_ge(S["cs_mm"], 1)
        for c in range(2):
            nc.scalar.activation(cs[:, c, 0:4, :], ps[0:ET, c, 0:4 * EP].rearrange("p (b n) -> p b n", b=4), ACT.Copy)\
                .then_inc(S["cs_ready"], 1)
        nc.scalar.activation(cs[:, :, 4, :], ps[0:ET, 2, 0:2 * EP].rearrange("p (c n) -> p c n", c=2), ACT.Copy)\
            .then_inc(S["cs_ready"], 1)
        split_wr(1, 0, 1)
        for b in range(NB):
            act.wait_ge(S["rows_t"], b + 1)
            hi(xn_h[:, :, b * RB:(b + 1) * RB], ps[:, 5 + b % 2, 0:KB * RB].rearrange("p (k n) -> p k n", k=KB), "xn_hi")
        with act.Fori(1, R2 // 2) as i:
            split_wr(2 * i, i, 0)
            split_wr(2 * i + 1, i, 1)
        split_wr(R2, R2 // 2, 0)

        act.wait_ge(S["table_mm"], NB * (R2 + 1))

        def split_msg(t, i, k):
            act.wait_ge(msg_in[k], 16 * (i + 1))
            if not first(i):
                act.wait_ge(S["seg_mm"], t + 1 - MR)
            hi(msg_h[:, k, :], msg[:, k, :], "msg_hi")

        over_messages(act, split_msg)

        act.wait_ge(S["a1_mm"], 1)
        hi(a1_h[:, :, :], ps[:, 7, 0:KB * L].rearrange("p (k l) -> p k l", k=KB), "a1_hi")
        act.wait_ge(S["ln_var"], 2)
        nc.scalar.activation(sdev2, var2, ACT.Sqrt).then_inc(S["ln_sd"], 1)
        for b in range(NB):
            act.wait_ge(S["l2_in"], b + 1)
            nc.scalar.activation(junk2[:, b, :], rows[:, b, :], ACT.Square, accum_out=l2ss[:, b:b + 1])\
                .then_inc(S["l2_sq"], 1)
        act.wait_ge(S["l2_sq"], NB)
        nc.scalar.activation(l2sd, l2ss[:, :], ACT.Sqrt).then_inc(S["l2_sd"], 1)
        for b in range(NB):
            act.wait_ge(S["xg_ready"], b + 1)
            hi(xn_h[:, :, b * RB:(b + 1) * RB], xg[:, b % 2, :, :], "xn_hi")
        act.wait_ge(S["hid_mm"], 1)
        act.wait_ge(S["c1_ready"], 1)
        nc.scalar.activation(hid[:, :].rearrange("p (c n) -> p c n", c=2), ps[0:L, 0:2, 0:SC], ACT.Silu,
                             bias=c1[:, 0:1]).then_inc(S["hid_ready"], 1)
        act.wait_ge(S["wt2_max"], 1)
        nc.scalar.activation(wt2[:, :], wt[:, :], ACT.Exp, bias=wtc[:, 0:1], accum_out=wtc[:, 1:2])\
            .then_inc(S["wt2_exp"], 1)
        act.wait_ge(S["w_sh"], 1)
        nc.scalar.activation(w[:, :, :], w[:, :, :], ACT.Exp).then_inc(S["w_exp"], 1)
        act.wait_ge(S["kf_ready"], 1)
        hi(kc_h[:, :, :], kf[:, :, :], "kc_hi")
        act.wait_ge(S["vf_ready"], 1)
        hi(vc_h[:, :, :], vf[:, :, :], "vc_hi")
        act.wait_ge(S["bq_mm"], 1)
        hi(bq_h[:, :, :].rearrange("p (c g) l -> p c g l", c=2),
           ps[0:HG, 4:6, 0:4 * L].rearrange("p c (g l) -> p c g l", g=4), "bq_hi")

        act.wait_ge(S["lm_done"], 1)

        def split_wq(v):
            act.wait_ge(S["wq_in"], 16 * (v + 1))
            if not first(v):
                act.wait_ge(S["p_mm"], KB * v)
            hi(wq_h[:, :, :], wq_raw[:, :, :], "wq_hi")

        def split_w1(v, f):
            act.wait_ge(S["w1_in"], 16 * (2 * v + f + 1))
            if not first(v):
                act.wait_ge(S["h_mm"], HO * (v - 1) + NB * (f + 1))
            hi(w1_h[f][:, :, :], w1_raw[:, :, :], "w1_hi")

        def hi_p(v, kb):
            act.wait_ge(S["p_mm"], KB * v + kb + 1)
            if kb == 0 and not first(v):
                act.wait_ge(S["score_mm"], NB * v)
            hi(p_h[:, kb, :], ps[:, 7, 0:UC], "p_hi")

        split_wq(0)
        for kb in range(KB):
            hi_p(0, kb)

        def unit_step(v, k):
            def exp(j):
                act.wait_ge(S["shifted"], NB * v + j + 1)
                nc.scalar.activation(prob[:, j % SR, :], prob[:, j % SR, :], ACT.Exp).then_inc(S["exp_ready"], 1)

            def hi_att(j):
                act.wait_ge(S["prob_t"], NB * v + j + 1)
                if j == 0:
                    if first(v):
                        act.wait_ge(S["pad_zero"], 2)
                    else:
                        act.wait_ge(S["z_mm"], HU * v)
                hi(at_h[:, :, j * RB:(j + 1) * RB], ps[0:L, 4, 0:HU * RB].rearrange("p (h n) -> p h n", h=HU), "att_hi")

            def hi_z(h):
                act.wait_ge(S["z_mm"], HU * v + h + 1)
                if h == 0:
                    act.wait_ge(S["unit_cols"], 3 * (v + 1))
                    if not (first(v) or first(v - 1)):
                        act.wait_ge(S["h_mm"], HO * (v - 1))
                zp = ps[:, 5:7, 0:SC]
                nc.scalar.activation(z_h[k][:, h, :].rearrange("p (c n) -> p c n", c=2), zp, ACT.Copy,
                                     scale=g1u[:, h:h + 1]).then_inc(S["z_hi"], 1)
                act.wait_ge(S["z_acc"], HU * v + h + 1)
                nc.scalar.activation(zsq[:, :].rearrange("p (c n) -> p c n", c=2), zp, ACT.Square)\
                    .then_inc(S["z_sq"], 1)

            more = not final(v, U - 1)
            exp(0)
            if not first(v):
                split_w1(v - 1, 1)
            exp(1)
            hi_att(0)
            if more:
                split_wq(v + 1)
            exp(2)
            hi_att(1)
            exp(3)
            hi_att(2)
            exp(4)
            if more:
                hi_p(v + 1, 0)
            hi_att(3)
            if more:
                hi_p(v + 1, 1)
            hi_att(4)
            split_w1(v, 0)
            if more:
                hi_p(v + 1, 2)
            hi_z(0)
            if more:
                hi_p(v + 1, 3)
            hi_z(1)
            hi_z(2)
            hi_z(3)

        over_units(act, unit_step)
        split_w1(U - 1, 1)

        act.wait_ge(S["w2_in"], 16)
        act.wait_ge(S["z_mm"], HU * U)
        for f in range(FB):
            nc.scalar.activation(w2_h[:, f, :], w2_raw[:, f, :], ACT.Copy,
                                 scale=colc[:, C_G2 + f:C_G2 + f + 1]).then_inc(S["w2_hi"], 1)
        act.wait_ge(S["n_mm"], 1)
        nc.scalar.activation(fcol[0][:, :], ps[0:RB, 4, 0:NB], ACT.Sqrt).then_inc(S["n_sd"], 1)
        for b in range(NB):
            act.wait_ge(S["h_sh"], b + 1)
            nc.scalar.activation(acc[:, b, :], acc[:, b, :], ACT.Silu).then_inc(S["h1_ready"], 1)
        for b in range(NB):
            act.wait_ge(S["h1_ready"], b + 1)
            if b > 0:
                act.wait_ge(S["h1_sq"], b)
            nc.scalar.activation(junk[:, :], acc[:, b, :], ACT.Square, accum_out=fcol[2][:, b:b + 1])\
                .then_inc(S["h1_sq"], 1)
            for c in range(2):
                act.wait_ge(S["h1_t"], 2 * b + c + 1)
                if b >= 2:
                    act.wait_ge(S["o_mm"], b - 1)
                hi(ht_h[:, b % 2, 4 * c:4 * c + 4, :], ps[:, c, 0:4 * RB].rearrange("p (k n) -> p k n", k=4), "ht_hi")
        act.wait_ge(S["h1_sq"], NB)
        nc.scalar.activation(fcol[3][:, :], fcol[2][:, :], ACT.Sqrt).then_inc(S["h1_sd"], 1)
        for b in range(NB):
            act.wait_ge(S["o_sh"], b + 1)
            nc.scalar.activation(o[:, b, :], o[:, b, :], ACT.Silu).then_inc(S["o_act"], 1)

    @block.vector
    def _(dve):
        chain = [0]

        def link(ins):
            chain[0] += 1
            ins.then_inc(S["dve"], 1)
            dve.wait_ge(S["dve"], chain[0])

        def lo(dst, source, part, done):
            dve.tensor_tensor(dst, source, part.bitcast(F32), ALU.subtract).then_inc(S[done], 1)

        def normalise(source, dest, v, sd, n, done):
            for b in range(NB):
                ins = dve.bn_stats(stat[:, b, :], source[:, b, :])
            link(ins)
            for b in range(NB):
                ins = dve.bn_aggr(mv[:, b, :], stat[:, b, :])
            link(ins)
            dve.tensor_scalar(v, mv[:, :, 1], LN_EPS, None, ALU.add).then_inc(S["ln_var"], 1)
            dve.wait_ge(S["ln_sd"], n)
            link(dve.reciprocal(rdev[:, :], sd))
            for b in range(NB):
                dve.tensor_scalar(dest[:, b, :], source[:, b, :], mv[:, b, 0:1], rdev[:, b:b + 1],
                                  ALU.subtract, ALU.mult).then_inc(S[done], 1)

        dve.wait_ge(S["x_in"], 16)
        normalise(xin, rows, var1, sdev1, 1, "rows_ready")

        def split_wr(r, i, k):
            dve.wait_ge(S["wr_hi"], r + 1)
            lo(wr_l[:, k, :, :], wr_raw[:, k, :, :], wr_h[:, k, :, :], "wr_lo")

        split_wr(0, 0, 0)
        for b in range(NB):
            dve.wait_ge(S["xn_hi"], b + 1)
            cut = slice(b * RB, (b + 1) * RB)
            lo(xn_l[:, :, cut], ps[:, 5 + b % 2, 0:KB * RB].rearrange("p (k n) -> p k n", k=KB), xn_h[:, :, cut], "xn_lo")

        def drain_table(r, i, k):
            dve.wait_ge(brel_in[k], 16 * (i + 1))
            for b in range(NB):
                dve.wait_ge(S["table_mm"], NB * r + b + 1)
                if not first(r):
                    dve.wait_ge(h_saved[b], 16 * r)
                dve.tensor_tensor(hout[:, b, :], ps[0:RB, b, :], brel[:, k, :], ALU.add)\
                    .then_inc(S["hout_ready"], 1)

        split_wr(1, 0, 1)
        drain_table(0, 0, 0)

        dve.wait_ge(S["rank_mm"], 1)
        ranks = ((5, 0, 3), (6, 3, NB))
        psr = {q: ps[0:EP, q, 0:(b1 - b0) * (MT + 1)].rearrange("p (b t) -> p b t", b=b1 - b0) for q, b0, b1 in ranks}
        for q, b0, b1 in ranks:
            ins = dve.tensor_scalar(count_i[:, b0:b1], psr[q][:, :, MT], float(MP - 1), None, ALU.add)
        link(ins)
        link(dve.tensor_scalar(tiles_i[:, :], count_i[:, :], MP.bit_length() - 1, None, ALU.arith_shift_right))
        dve.memset(base[:, 0:1], 0.0)
        link(dve.tensor_copy(tiles[:, :], tiles_i[:, :]))
        for b in range(1, NB):
            link(dve.tensor_tensor(base[:, b:b + 1], base[:, b - 1:b], tiles[:, b - 1:b], ALU.add))
        link(dve.tensor_scalar(base_m[:, :], base[:, :], float(MP), None, ALU.mult))
        for q, b0, b1 in ranks:
            ins = dve.tensor_tensor(rank[:, b0:b1, :], psr[q][:, :, 0:MT], spread(base_m[:, b0:b1], [EP, b1 - b0, MT]),
                                    ALU.add)
        link(ins)
        link(dve.tensor_tensor(rank[:, :, :], rank[:, :, :], inb[:, :, :], ALU.mult))
        link(dve.tensor_reduce(pos[:, :], rank[:, :, :].rearrange("p b t -> p t b"), AX.X, ALU.add))
        link(dve.tensor_copy(pos_i[:, :], pos[:, :]))
        dve.tensor_scalar(pos_lane[:, :], pos_i[:, :], MP - 1, None, ALU.bitwise_and)
        link(dve.tensor_scalar(pos_tile[:, :], pos_i[:, :], MP.bit_length() - 1, None, ALU.arith_shift_right))
        dve.scalar_tensor_tensor(out=slot[:, :], in0=pos_lane[:, :], scalar=float(MS), in1=pos_tile[:, :],
                                 op0=ALU.mult, op1=ALU.add).then_inc(S["slot_ready"], 1)
        dve.wait_ge(S["consts"], 8)
        link(dve.tensor_scalar(tb[1][:, :], tile_no[:, :], base[0:1, 1:2], None, ALU.is_ge))
        for b in range(2, NB):
            to = tile_block if b == NB - 1 else tb[b % 2]
            ins = dve.scalar_tensor_tensor(out=to[:, :], in0=tile_no[:, :], scalar=base[0:1, b:b + 1],
                                           in1=tb[(b - 1) % 2][:, :], op0=ALU.is_ge, op1=ALU.add)
            if b < NB - 1:
                link(ins)
        ins.then_inc(S["slot_ready"], 1)

        with dve.Fori(1, R2 // 2) as i:
            split_wr(2 * i, i, 0)
            drain_table(2 * i - 1, i - 1, 1)
            split_wr(2 * i + 1, i, 1)
            drain_table(2 * i, i, 0)
        split_wr(R2, R2 // 2, 0)
        drain_table(R2 - 1, R2 // 2 - 1, 1)
        dve.wait_ge(S["srt_in"], 16)
        dve.wait_ge(S["table_mm"], NB * (R2 + 1))

        def split_msg(t, i, k):
            if not first(i):
                dve.wait_ge(S["seg_mm"], t + 1 - MR)
            dve.tensor_scalar(hot[:, k, 0:RB], node[:, :], srt[:, bass.ds(t, 1), 1], None, ALU.is_equal)\
                .then_inc(S["hot_ready"], 1)
            dve.wait_ge(S["msg_hi"], t + 1)
            lo(msg_l[:, k, :], msg[:, k, :], msg_h[:, k, :], "msg_lo")

        over_messages(dve, split_msg)

        dve.wait_ge(S["seg_mm"], MS + 1)
        dve.wait_ge(brel_in[0], 16 * (R2 // 2 + 1))
        for b in range(NB):
            link(dve.tensor_tensor(rows[:, b, :], ps[0:RB, b, :], brel[:, 0, :], ALU.add))
            dve.scalar_tensor_tensor(out=x1[:, b, :], in0=rows[:, b, :], scalar=0.0, in1=xin[:, b, :],
                                     op0=ALU.max, op1=ALU.add).then_inc(S["x1_ready"], 1)
        dve.wait_ge(S["x1_ready"], NB)
        dve.wait_ge(S["cols_in"], 16)

        normalise(x1, rows, var2, sdev2, 2, "l2_in")
        dve.wait_ge(S["l2_sd"], 1)
        link(dve.tensor_scalar(l2rc[:, :], l2sd, L2_EPS, None, ALU.max))
        link(dve.reciprocal(l2rc[:, :], l2rc[:, :]))
        dve.wait_ge(S["l2_in"], NB)
        for b in range(NB):
            dve.tensor_scalar(rows[:, b, :], rows[:, b, :], l2rc[:, b:b + 1], float(D) ** 0.5,
                              ALU.mult, ALU.mult).then_inc(S["rows_ready"], 1)

        dve.wait_ge(S["a1_hi"], 1)
        lo(a1_l[:, :, :], ps[:, 7, 0:KB * L].rearrange("p (k l) -> p k l", k=KB), a1_h[:, :, :], "a1_lo")
        dve.tensor_tensor(c1[:, :], ps[0:L, 6, 0:1], rowc[:, 0:1], ALU.add).then_inc(S["c1_ready"], 1)
        gam = spread(colc[:, C_GAMMA:C_GAMMA + KB], [128, KB, RB])
        for b in range(NB):
            cut = slice(b * RB, (b + 1) * RB)
            dve.wait_ge(S["rows_t"], NB + b + 1)
            if b >= 2:
                dve.wait_ge(S["xn_hi"], NB + b - 1)
            dve.tensor_tensor(xg[:, b % 2, :, :], ps[:, b % 2, 0:KB * RB].rearrange("p (k n) -> p k n", k=KB), gam,
                              ALU.mult).then_inc(S["xg_ready"], 1)
            dve.wait_ge(S["xn_hi"], NB + b + 1)
            lo(xn_l[:, :, cut], xg[:, b % 2, :, :], xn_h[:, :, cut], "xn_lo")

        dve.wait_ge(S["wt_mm"], 1)
        for c, n in ((0, SC), (1, N - SC)):
            ins = dve.tensor_scalar(wt[:, c * SC:c * SC + n], ps[0:L, 2 + c, 0:n], rowc[:, 1:2], None, ALU.add)
            ins.then_inc(S["wt_ready"], 1)
        dve.wait_ge(S["wt_ready"], 2)
        dve.tensor_reduce(wtc[:, 0:1], wt[:, :], AX.X, ALU.max, negate=True).then_inc(S["wt2_max"], 1)
        dve.wait_ge(S["wt2_exp"], 1)
        link(dve.reciprocal(wtc[:, 2:3], wtc[:, 1:2]))
        dve.tensor_scalar(wt2[:, :], wt2[:, :], wtc[:, 2:3], 0.5 / L, ALU.mult, ALU.mult).then_inc(S["wt2_ready"], 1)
        dve.wait_ge(S["wt_t"], 1)
        wps = ps[0:RB, 4, 0:NB * L].rearrange("p (b l) -> p b l", b=NB)
        link(dve.tensor_reduce(rdev[:, :], wps, AX.X, ALU.max))
        dve.tensor_tensor(w[:, :, :], wps, spread(rdev[:, :], [RB, NB, L]), ALU.subtract).then_inc(S["w_sh"], 1)
        dve.wait_ge(S["w_exp"], 1)
        link(dve.tensor_reduce(l2rc[:, :], w[:, :, :], AX.X, ALU.add))
        link(dve.reciprocal(rdev[:, :], l2rc[:, :]))
        link(dve.tensor_tensor(w[:, :, :], w[:, :, :], spread(rdev[:, :], [RB, NB, L]), ALU.mult))
        dve.wait_ge(S["wt_t"], 2)
        dve.scalar_tensor_tensor(out=w[:, :, :], in0=w[:, :, :], scalar=0.5 / N,
                                 in1=ps[0:RB, 5, 0:NB * L].rearrange("p (b l) -> p b l", b=NB),
                                 op0=ALU.mult, op1=ALU.add).then_inc(S["w_ready"], 1)
        dve.wait_ge(S["lm_mm"], 1)
        dve.tensor_copy(swb[:, :], ps[:, 6, 0:L]).then_inc(S["lm_ev"], 1)
        dve.tensor_copy(swc[:, :], ps[0:L, 6, 128:129]).then_inc(S["lm_ev"], 1)
        dve.tensor_tensor(ct[:, :, :], ps[:, 7, 0:KB * L].rearrange("p (k l) -> p k l", k=KB),
                          spread(colc[:, C_GAMMA:C_GAMMA + KB], [128, KB, L]), ALU.mult).then_inc(S["ct_ready"], 1)
        dve.wait_ge(S["lm_ev"], 2)
        for g in range(G):
            if g % 4 == 0:
                dve.wait_ge(S["kc_mm"], g // 4 + 1)
            ins = dve.scalar_tensor_tensor(out=kf[:, g, :], in0=swb[:, :], scalar=colc[:, C_BK + g:C_BK + g + 1],
                                           in1=ps[:, g // 4, (g % 4) * L:(g % 4 + 1) * L],
                                           op0=ALU.mult, op1=ALU.add)
        link(ins)
        dve.tensor_scalar(kf[:, :, :], kf[:, :, :], float(DK) ** -0.5, None, ALU.mult).then_inc(S["kf_ready"], 1)
        dve.wait_ge(S["vc_mm"], 1)
        dve.scalar_tensor_tensor(out=vf[:, :, :].rearrange("p g d -> p (g d)").rearrange("p (c n) -> p c n", c=2),
                                 in0=bvb[:, :].rearrange("p (c n) -> p c n", c=2), scalar=swc[:, 0:1],
                                 in1=ps[0:L, 2:4, :], op0=ALU.mult, op1=ALU.add).then_inc(S["vf_ready"], 1)
        dve.wait_ge(S["kc_hi"], 1)
        lo(kc_l[:, :, :], kf[:, :, :], kc_h[:, :, :], "kc_lo")
        dve.wait_ge(S["vc_hi"], 1)
        lo(vc_l[:, :, :], vf[:, :, :], vc_h[:, :, :], "vc_lo")
        dve.wait_ge(S["bq_hi"], 1)
        lo(bq_l[:, :, :].rearrange("p (c g) l -> p c g l", c=2),
           ps[0:HG, 4:6, 0:4 * L].rearrange("p c (g l) -> p c g l", g=4),
           bq_h[:, :, :].rearrange("p (c g) l -> p c g l", c=2), "bq_lo")
        for n in ("kc_lo", "vc_lo", "bq_lo"):
            dve.wait_ge(S[n], 1)
        dve.wait_ge(S["bq_saved"], 32)
        dve.wait_ge(S["x1_saved"], 16)
        dve.nop().then_inc(S["lm_done"], 1)

        def lo_p(v, kb):
            dve.wait_ge(S["p_hi"], KB * v + kb + 1)
            lo(p_l[:, kb, :], ps[:, 7, 0:UC], p_h[:, kb, :], "p_lo")

        for kb in range(KB):
            lo_p(0, kb)

        def add_h(v, n):
            f, b = n // NB, n % NB
            dve.wait_ge(S["h_mm"], HO * v + n + 1)
            a = acc[:, b, f * FH:(f + 1) * FH]
            dve.tensor_tensor(a, a, ps[0:RB, 2 + n % 2, :], ALU.add).then_inc(S["h_acc"], 1)

        def unit_step(v, k):
            def softmax(j):
                q = NB * v + j
                sj = ps[0:RB, j % 2, 0:UC].rearrange("p (h l) -> p h l", h=HU)
                pj = prob[:, j % SR, :].rearrange("p (h l) -> p h l", h=HU)
                dve.wait_ge(S["score_mm"], q + 1)
                dve.tensor_reduce(smax[:, :], sj, AX.X, ALU.max).then_inc(S["max_ready"], 1)
                dve.wait_ge(S["max_ready"], q + 1)
                if j >= SR:
                    dve.wait_ge(S["prob_t"], q + 1 - SR)
                elif not first(v):
                    dve.wait_ge(S["prob_t"], NB * v - {0: 1, 1: 0, 2: 2}[j])
                dve.tensor_tensor(pj, sj, spread(smax[:, :], [RB, HU, L]), ALU.subtract).then_inc(S["shifted"], 1)
                dve.wait_ge(S["exp_ready"], q + 1)
                dve.tensor_reduce(ssum[:, :], pj, AX.X, ALU.add).then_inc(S["sum_ready"], 1)
                dve.wait_ge(S["sum_ready"], q + 1)
                dve.reciprocal(srec[:, j % SR, :], ssum[:, :]).then_inc(S["rec_ready"], 1)

            def lo_att(j):
                dve.wait_ge(S["att_hi"], NB * v + j + 1)
                cut = slice(j * RB, (j + 1) * RB)
                lo(at_l[:, :, cut], ps[0:L, 4, 0:HU * RB].rearrange("p (h n) -> p h n", h=HU), at_h[:, :, cut],
                   "att_lo")

            def lo_z(h):
                dve.wait_ge(S["z_sq"], HU * v + h + 1)
                dve.scalar_tensor_tensor(out=z_l[k][:, h, :].rearrange("p (c n) -> p c n", c=2), in0=ps[:, 5:7, 0:SC],
                                         scalar=g1u[:, h:h + 1],
                                         in1=z_h[k][:, h, :].rearrange("p (c n) -> p c n", c=2).bitcast(F32),
                                         op0=ALU.mult, op1=ALU.subtract).then_inc(S["z_lo"], 1)

            def add(n):
                if not first(v):
                    add_h(v - 1, n)

            more = not final(v, U - 1)
            softmax(0)
            add(0)
            softmax(1)
            add(1)
            lo_att(0)
            softmax(2)
            add(2)
            lo_att(1)
            softmax(3)
            add(3)
            lo_att(2)
            softmax(4)
            if more:
                lo_p(v + 1, 0)
            add(4)
            lo_att(3)
            if more:
                lo_p(v + 1, 1)
            add(5)
            lo_att(4)
            if more:
                lo_p(v + 1, 2)
            add(6)
            lo_z(0)
            if more:
                lo_p(v + 1, 3)
            add(7)
            lo_z(1)
            add(8)
            lo_z(2)
            add(9)
            lo_z(3)

        dve.wait_ge(S["acc_zero"], 1)
        over_units(dve, unit_step)
        for n in range(HO):
            add_h(U - 1, n)

        dve.wait_ge(S["w2_hi"], FB)
        for f in range(FB):
            dve.scalar_tensor_tensor(out=w2_l[:, f, :], in0=w2_raw[:, f, :], scalar=colc[:, C_G2 + f:C_G2 + f + 1],
                                     in1=w2_h[:, f, :].bitcast(F32), op0=ALU.mult, op1=ALU.subtract)\
                .then_inc(S["w2_lo"], 1)
        dve.wait_ge(S["n_sd"], 1)
        link(dve.tensor_scalar(fcol[1][:, :], fcol[0][:, :], L2_EPS, None, ALU.max))
        link(dve.reciprocal(fcol[1][:, :], fcol[1][:, :]))
        link(dve.tensor_scalar(fcol[1][:, :], fcol[1][:, :], float(G * HG * DK) ** 0.5, None, ALU.mult))
        dve.wait_ge(S["h_acc"], HO * U)
        dve.wait_ge(S["fin_in"], 48)
        for b in range(NB):
            dve.scalar_tensor_tensor(out=acc[:, b, :], in0=acc[:, b, :], scalar=fcol[1][:, b:b + 1], in1=b1b[:, :],
                                     op0=ALU.mult, op1=ALU.add).then_inc(S["h_sh"], 1)
        for b in range(NB):
            for c in range(2):
                dve.wait_ge(S["ht_hi"], 2 * b + c + 1)
                lo(ht_l[:, b % 2, 4 * c:4 * c + 4, :], ps[:, c, 0:4 * RB].rearrange("p (k n) -> p k n", k=4),
                   ht_h[:, b % 2, 4 * c:4 * c + 4, :], "ht_lo")
        dve.wait_ge(S["h1_sd"], 1)
        link(dve.tensor_scalar(fcol[4][:, :], fcol[3][:, :], L2_EPS, None, ALU.max))
        link(dve.reciprocal(fcol[5][:, :], fcol[4][:, :]))
        link(dve.tensor_scalar(fcol[5][:, :], fcol[5][:, :], float(F2) ** 0.5, None, ALU.mult))
        for b in range(NB):
            dve.wait_ge(S["o_mm"], b + 1)
            dve.scalar_tensor_tensor(out=o[:, b, :], in0=ps[0:RB, 3 + b, :], scalar=fcol[5][:, b:b + 1],
                                     in1=b2b[:, :], op0=ALU.mult, op1=ALU.add).then_inc(S["o_sh"], 1)
        for b in range(NB):
            dve.wait_ge(S["o_act"], b + 1)
            dve.tensor_tensor(o[:, b, :], o[:, b, :], x1r[:, b, :], ALU.add).then_inc(S["o_ready"], 1)

    @block.tensor
    def _(pe):
        def three(dst, lh, ll, rh, rl, start, stop):
            pe.matmul(dst, lh, rh, start=start, stop=False)
            pe.matmul(dst, lh, rl, start=False, stop=False)
            return pe.matmul(dst, ll, rh, start=False, stop=stop)

        def transpose_rows(n, bank, before):
            for b in range(NB):
                pe.wait_ge(S["rows_ready"], n * NB + b + 1)
                if b >= 2:
                    pe.wait_ge(S[before], b - 1)
                for k in range(KB):
                    mm = pe.transpose(ps[:, bank + b % 2, k * RB:(k + 1) * RB], rows[:, b, k * 128:(k + 1) * 128],
                                      ident[0:RB, 0:RB])
                mm.then_inc(S["rows_t"], 1)

        pe.wait_ge(S["consts"], 14)
        pe.wait_ge(S["blocks_ready"], 1)
        for b in range(NB):
            for c in range(2):
                dst = ps[0:ET, c, b * EP:(b + 1) * EP] if b < 4 else ps[0:ET, 2, c * EP:(c + 1) * EP]
                mm = pe.matmul(dst, inb[:, b, c * ET:(c + 1) * ET], ones[0:EP, 0:EP], start=True, stop=True)
        mm.then_inc(S["cs_mm"], 1)
        transpose_rows(0, 5, "xn_lo")

        def table(r, i, k):
            pe.wait_ge(S["wr_hi"], r + 1)
            pe.wait_ge(S["wr_lo"], r + 1)
            for b in range(NB):
                if first(r):
                    pe.wait_ge(S["xn_lo"], b + 1)
                else:
                    pe.wait_ge(S["hout_ready"], NB * (r - 1) + b + 1)
                cut = slice(b * RB, (b + 1) * RB)
                for kb in range(KB):
                    mm = three(ps[0:RB, b, :], xn_h[:, kb, cut], xn_l[:, kb, cut], wr_h[:, k, kb, :],
                               wr_l[:, k, kb, :], kb == 0, kb == KB - 1 and not final(r, R2))
                mm.then_inc(S["table_mm"], 1)

        table(0, 0, 0)
        pe.wait_ge(S["cs_ready"], 3)
        for b in range(NB):
            q, at = (5, b) if b < 3 else (6, b - 3)
            dst = ps[0:EP, q, at * (MT + 1):(at + 1) * (MT + 1)]
            for c in range(2):
                pe.matmul(dst, cs[:, c, b, :], later_t[:, c, :], start=(c == 0), stop=False)
            mm = pe.matmul(dst[:, 0:MT], later_p[:, :], inb[:, b, :], start=False, stop=True)
        mm.then_inc(S["rank_mm"], 1)
        table(1, 0, 1)
        with pe.Fori(1, R2 // 2) as i:
            table(2 * i, i, 0)
            table(2 * i + 1, i, 1)
        table(R2, R2 // 2, 0)

        pe.wait_ge(S["slot_ready"], 2)

        def tile_blocks(t, n):
            return nc.values_load_multi_w_load_instructions(
                tile_block[0:1, bass.ds(t, n)], engines=[mybir.EngineType.PE], min_val=0, max_val=NB - 1,
                skip_runtime_bounds_check_because="the block is a sum of NB - 1 comparisons")[1]

        def segment(t, i, k, block_of):
            pe.wait_ge(S["hot_ready"], t + 1)
            pe.wait_ge(S["msg_lo"], t + 1)
            dst = ps[0:RB, bass.ds(block_of, 1), :].rearrange("p b d -> p (b d)")
            pe.matmul(dst, hot[:, k, 0:RB], msg_h[:, k, :], start=False, stop=False)
            pe.matmul(dst, hot[:, k, 0:RB], msg_l[:, k, :], start=False, stop=False).then_inc(S["seg_mm"], 1)

        blocks = tile_blocks(0, MR)
        for k in range(MR):
            segment(k, 0, k, blocks[k])
        with pe.Fori(1, MS // MR) as i:
            blocks = tile_blocks(i * MR, MR)
            for k in range(MR):
                segment(i * MR + k, i, k, blocks[k])
        blocks = tile_blocks(MS - MS % MR, MS % MR)
        for k in range(MS % MR):
            segment(MS - MS % MR + k, MS // MR, k, blocks[k])
        for b in range(NB):
            mm = pe.matmul(ps[0:RB, b, :], zero[:, 0:RB], zero[:, :], start=False, stop=True)
        mm.then_inc(S["seg_mm"], 1)

        pe.wait_ge(S["lm_in"], 80)
        pe.wait_ge(S["cols_in"], 16)
        for kb in range(KB):
            for g in range(G):
                pe.matmul(ps[:, 7, kb * L:(kb + 1) * L], wkt[:, g, kb * 128:(kb + 1) * 128], a1w[:, g, :],
                          start=(g == 0), stop=(g == G - 1))
        for g in range(G):
            mm = pe.matmul(ps[0:L, 6, 0:1], a1w[:, g, :], colc[:, C_BK + g:C_BK + g + 1], start=(g == 0),
                           stop=(g == G - 1))
        mm.then_inc(S["a1_mm"], 1)

        pe.wait_ge(S["x1_ready"], NB)
        transpose_rows(1, 0, "xg_ready")

        pe.wait_ge(S["a1_lo"], 1)
        pe.wait_ge(S["xn_lo"], 2 * NB)
        for c in range(2):
            for kb in range(KB):
                cut = slice(c * SC, (c + 1) * SC)
                mm = three(ps[0:L, c, 0:SC], a1_h[:, kb, :], a1_l[:, kb, :], xn_h[:, kb, cut], xn_l[:, kb, cut],
                           kb == 0, kb == KB - 1)
        mm.then_inc(S["hid_mm"], 1)
        pe.wait_ge(S["hid_ready"], 1)
        for c in range(2):
            mm = pe.matmul(ps[0:L, 2 + c, 0:SC], a2w[:, :], hid[:, c * SC:(c + 1) * SC], start=True, stop=True)
        mm.then_inc(S["wt_mm"], 1)
        pe.wait_ge(S["wt_ready"], 2)
        for b in range(NB):
            mm = pe.transpose(ps[0:RB, 4, b * L:(b + 1) * L], wt[:, b * RB:(b + 1) * RB], ident[0:L, 0:L])
        mm.then_inc(S["wt_t"], 1)
        pe.wait_ge(S["wt2_ready"], 1)
        for b in range(NB):
            mm = pe.transpose(ps[0:RB, 5, b * L:(b + 1) * L], wt2[:, b * RB:(b + 1) * RB], ident[0:L, 0:L])
        mm.then_inc(S["wt_t"], 1)
        pe.wait_ge(S["w_ready"], 1)
        for b in range(NB):
            pe.matmul(ps[:, 6, 0:L], ones[0:RB, :], w[:, b, :], start=(b == 0), stop=(b == NB - 1))
        for b in range(NB):
            pe.matmul(ps[0:L, 6, 128:129], w[:, b, :], ones[0:RB, 0:1], start=(b == 0), stop=(b == NB - 1))
        for kb in range(KB):
            for b in range(NB):
                mm = pe.matmul(ps[:, 7, kb * L:(kb + 1) * L], rows[:, b, kb * 128:(kb + 1) * 128], w[:, b, :],
                               start=(b == 0), stop=(b == NB - 1))
        mm.then_inc(S["lm_mm"], 1)
        pe.wait_ge(S["ct_ready"], 1)
        pe.wait_ge(S["kv_in"], 32)
        for g in range(G):
            for kb in range(KB):
                mm = pe.matmul(ps[:, g // 4, (g % 4) * L:(g % 4 + 1) * L], wkv[:, kb, g * DK:(g + 1) * DK],
                               ct[:, kb, :], start=(kb == 0), stop=(kb == KB - 1))
            if g % 4 == 3:
                mm.then_inc(S["kc_mm"], 1)
        for c in range(2):
            for kb in range(KB):
                mm = pe.matmul(ps[0:L, 2 + c, :], ct[:, kb, :], wkv[:, kb, G * DK + c * 512:G * DK + (c + 1) * 512],
                               start=(kb == 0), stop=(kb == KB - 1))
        mm.then_inc(S["vc_mm"], 1)
        pe.wait_ge(S["kf_ready"], 1)
        for g in range(G):
            mm = pe.matmul(ps[0:HG, 4 + g // 4, (g % 4) * L:(g % 4 + 1) * L],
                           colc[:, C_BQ + g * HG:C_BQ + (g + 1) * HG], kf[:, g, :], start=True, stop=True)
        mm.then_inc(S["bq_mm"], 1)

        def queries(v, kb):
            if kb == 0:
                pe.wait_ge(S["wq_lo"], HU * (v + 1))
            if kb > 0 or not first(v):
                pe.wait_ge(S["p_lo"], KB * v + kb)
            g = v // UG
            for h in range(HU):
                cut = slice(kb * 128, (kb + 1) * 128)
                rh = kc_h[:, bass.ds(g, 1), :].rearrange("p a l -> p (a l)")
                rl = kc_l[:, bass.ds(g, 1), :].rearrange("p a l -> p (a l)")
                mm = three(ps[:, 7, h * L:(h + 1) * L], wq_h[:, h, cut], wq_l[:, h, cut], rh, rl, True, True)
            mm.then_inc(S["p_mm"], 1)

        pe.wait_ge(S["lm_done"], 1)
        for kb in range(KB):
            queries(0, kb)

        def hidden(v, k, n):
            f, b = n // NB, n % NB
            if n == 0:
                pe.wait_ge(S["z_lo"], HU * (v + 1))
            if b == 0:
                pe.wait_ge(S["w1_lo"], HU * (2 * v + f + 1))
            if n == 0:
                if not first(v):
                    pe.wait_ge(S["h_acc"], HO * v)
            elif n > 1:
                pe.wait_ge(S["h_acc"], HO * v + n - 1)
            cut = slice(b * RB, (b + 1) * RB)
            for h in range(HU):
                mm = three(ps[0:RB, 2 + n % 2, :], z_h[k][:, h, cut], z_l[k][:, h, cut], w1_h[f][:, h, :],
                           w1_l[f][:, h, :], h == 0, h == HU - 1)
            mm.then_inc(S["h_mm"], 1)

        def unit_step(v, k):
            def scores(j):
                q = NB * v + j
                if j == 0:
                    pe.wait_ge(S["p_lo"], KB * (v + 1))
                    pe.wait_ge(S["brow_in"], 16 * (v + 1))
                if j >= 2:
                    pe.wait_ge(S["shifted"], q - 1)
                elif not first(v):
                    pe.wait_ge(S["shifted"], NB * v)
                dst = ps[0:RB, j % 2, 0:UC]
                cut = slice(j * RB, (j + 1) * RB)
                for kb in range(KB):
                    three(dst, xn_h[:, kb, cut], xn_l[:, kb, cut], p_h[:, kb, :], p_l[:, kb, :], kb == 0, False)
                pe.matmul(dst, ones2[:, :], brow[:, :], start=False, stop=True).then_inc(S["score_mm"], 1)

            def turn(j):
                q = NB * v + j
                pe.wait_ge(S["prob_ready"], q + 1)
                if j > 0 or not first(v):
                    pe.wait_ge(S["att_lo"], q)
                for h in range(HU):
                    mm = pe.transpose(ps[0:L, 4, h * RB:(h + 1) * RB], prob[:, j % SR, h * L:(h + 1) * L],
                                      ident[0:RB, 0:RB])
                mm.then_inc(S["prob_t"], 1)

            def values(h):
                q = HU * v + h
                if h == 0:
                    pe.wait_ge(S["att_lo"], NB * (v + 1))
                    pe.wait_ge(S["unit_cols"], 3 * (v + 1))
                if h > 0 or not first(v):
                    pe.wait_ge(S["z_lo"], q)
                    pe.wait_ge(S["z_sq"], q)
                for c in range(2):
                    cut = slice(c * SC, (c + 1) * SC)
                    mm = three(ps[:, 5 + c, 0:SC], vcu_h[:, :], vcu_l[:, :], at_h[:, h, cut], at_l[:, h, cut],
                               True, True)
                mm.then_inc(S["z_mm"], 1)

            def h1(n):
                if not first(v):
                    hidden(v - 1, 1 - k, n)

            def p(kb):
                if not final(v, U - 1):
                    queries(v + 1, kb)

            scores(0)
            h1(0)
            scores(1)
            h1(1)
            turn(0)
            scores(2)
            h1(2)
            turn(1)
            scores(3)
            h1(3)
            turn(2)
            scores(4)
            p(0)
            h1(4)
            turn(3)
            p(1)
            h1(5)
            turn(4)
            p(2)
            h1(6)
            values(0)
            p(3)
            h1(7)
            values(1)
            h1(8)
            values(2)
            h1(9)
            values(3)

        over_units(pe, unit_step)
        for n in range(HO):
            hidden(U - 1, 1, n)
        pe.wait_ge(S["z_acc"], HU * U + 1)
        for b in range(NB):
            mm = pe.matmul(ps[0:RB, 4, b:b + 1], zacc[:, b * RB:(b + 1) * RB], ones[:, 0:1], start=True, stop=True)
        mm.then_inc(S["n_mm"], 1)
        for b in range(NB):
            pe.wait_ge(S["h1_ready"], b + 1)
            for c in range(2):
                if b > 0:
                    pe.wait_ge(S["ht_lo"], 2 * b + c - 1)
                for k in range(4):
                    f = 4 * c + k
                    mm = pe.transpose(ps[:, c, k * RB:(k + 1) * RB], acc[:, b, f * 128:(f + 1) * 128],
                                      ident[0:RB, 0:RB])
                mm.then_inc(S["h1_t"], 1)
            pe.wait_ge(S["ht_lo"], 2 * b + 2)
            pe.wait_ge(S["w2_lo"], FB)
            if b == 1:
                pe.wait_ge(S["n_sd"], 1)
            for f in range(FB):
                mm = three(ps[0:RB, 3 + b, :], ht_h[:, b % 2, f, :], ht_l[:, b % 2, f, :], w2_h[:, f, :],
                           w2_l[:, f, :], f == 0, f == FB - 1)
            mm.then_inc(S["o_mm"], 1)

    ctx.close()


def kernel(**inputs):
    import numpy as np
    import concourse.bacc as bacc
    from concourse.bass_utils import run_bass_kernel_spmd

    a = {k: np.asarray(v) for k, v in inputs.items()}
    f = "L0_ffn_"

    def by_partition(m):
        return m.reshape(-1, 128, m.shape[-1]).transpose(1, 0, 2)

    def col(v):
        return v.reshape(-1, 128).T

    w_rel = np.concatenate([a["L0_gnn_W_rel"], a["L0_gnn_W_self"][None]], 0).transpose(0, 2, 1)
    data = {
        "x": a["x"], "src": a["src"], "dst": a["dst"], "etype": a["edge_type_8"],
        "w_rel_t": w_rel.reshape(R2 + 1, KB, 128, D).transpose(0, 2, 1, 3).reshape(R2 + 1, 128, KB * D),
        "b_rel": np.concatenate([a["L0_gnn_b_rel"], a["L0_gnn_b_self"][None]], 0),
        "cols": np.concatenate([col(a[f + "gamma_norm"]), col(a[f + "wz_g2"]), col(a[f + "Wkv_b"][:G * DK]),
                                col(a[f + "Wq_b"]), col(a[f + "wz_g1"])], 1),
        "wk_t": by_partition(a[f + "Wkv_w"][:, :G * DK].T),
        "w_kv": by_partition(a[f + "Wkv_w"]),
        "aw1": by_partition(a[f + "aw1_w"]), "aw1_b": a[f + "aw1_b"][:, None],
        "aw2": a[f + "aw2_w"], "aw2_b": a[f + "aw2_b"][:, None],
        "b_v": a[f + "Wkv_b"][None, G * DK:],
        "wq_t": a[f + "Wq_w"].T.reshape(U, HU, 128, D).transpose(0, 2, 1, 3).reshape(U, 128, HU * D),
        "wz_w1": a[f + "wz_w1"].reshape(U, HU, 128, 2, FH).transpose(0, 3, 2, 1, 4).reshape(U, 2, 128, HU * FH),
        "b1": a[f + "wz_b1"][None], "w2": by_partition(a[f + "wz_w2"]), "b2": a[f + "wz_b2"][None],
    }
    nc = bacc.Bacc("TRN2", target_bir_lowering=False, num_devices=1)
    arrays, args = {}, []
    for name, v in data.items():
        v = np.ascontiguousarray(v)
        arrays[f"in_{name}"] = v
        args.append(nc.dram_tensor(f"in_{name}", v.shape, mybir.dt.from_np(v.dtype), kind="ExternalInput").ap())
    args.append(nc.dram_tensor("out", (N, D), F32, kind="ExternalOutput").ap())
    build_layer(nc, *args)
    r = run_bass_kernel_spmd(nc, [arrays], core_ids=[0])
    return r.results[0]["out"]
```

```python
from contextlib import ExitStack

import concourse.bass as bass
from concourse import mybir

F32 = mybir.dt.float32
F32R = mybir.dt.float32r
I32 = mybir.dt.int32
ALU = mybir.AluOpType
ACT = mybir.ActivationFunctionType
AX = mybir.AxisListType

N, D = 625, 512
NB, RB = 5, 125
KB = D // 128
E = 10000
R = 8
R2 = 2 * R
EP = 125
ET = E // EP
MT = 2 * ET
MP = 128
MS = MT * EP // MP + NB
MR = 8
G, HG, DK, L = 8, 16, 128, 100
HU = 4
U = G * HG // HU
UG = HG // HU
UC = HU * L
F2 = 1024
FH = F2 // 2
FB = F2 // 128
SPAD = 628
SC = SPAD // 2
SR = 3
HO = FB * 2
HH = HO // 2
LN_EPS = 1e-5
L2_EPS = 1e-12

C_GAMMA = 0
C_G2 = C_GAMMA + KB
C_BK = C_G2 + FB
C_BQ = C_BK + G
C_G1 = C_BQ + G * HG
C_B1 = C_G1 + G * HG
C_END = C_B1 + FB


def build_layer(nc, x, src, dst, etype, w_rel_t, b_rel, cols, wk_t, w_kv, aw1, aw1_b, aw2, aw2_b, b_v,
                wq_t, wz_w1, w2, b2, out):
    ctx = ExitStack()

    def sem(name):
        return ctx.enter_context(nc.semaphore(name))

    h_table = nc.dram_tensor("h_table", [R2 * N, D], F32, kind="Internal").ap()
    x1_stash = nc.dram_tensor("x1_stash", [N, D], F32, kind="Internal").ap()
    slots = nc.dram_tensor("slots", [MP * MS, 2], F32, kind="Internal").ap()
    bqk_rows = nc.dram_tensor("bqk_rows", [1, G * HG * L], F32, kind="Internal").ap()

    ps = ctx.enter_context(nc.psum_tensor("ps", [128, 8, 512], F32))

    class Shelf:
        def __init__(self, at):
            self.at = at

        def put(self, name, shape, dt=F32):
            size = 4
            for n in shape[1:]:
                size *= n
            t = nc.alloc_sbuf_tensor_at(name, shape, dt, offset=self.at)
            self.at += (size + 31) // 32 * 32
            return t

    whole = Shelf((nc.sbuf_base + 63) // 64 * 64)
    ident = whole.put("ident", [128, 128])
    ones = whole.put("ones", [128, 128])
    ones_r = whole.put("ones_r", [1, RB], F32R)
    colc = whole.put("colc", [128, C_END])
    wq_raw = whole.put("wq_raw", [128, HU, D])
    w1_raw = whole.put("w1_raw", [128, HU, FH])
    kc = whole.put("kc", [128, G, 2, L], F32R)
    vc_h = whole.put("vc_h", [L, G, DK], F32R)
    vc_l = whole.put("vc_l", [L, G, DK], F32R)
    xn_at = whole.at
    xn_h = whole.put("xn_h", [128, KB, SPAD], F32R)
    xn_l = whole.put("xn_l", [128, KB, SPAD], F32R)

    graph = Shelf(whole.at)
    xin = graph.put("xin", [RB, NB, D])
    early_at = graph.at
    graph.at += 4 * NB * D
    rows = graph.put("rows", [RB, NB, D])
    x1_at = graph.at
    x1 = graph.put("x1", [RB, NB, D])
    stat = graph.put("stat", [RB, NB, 6])
    mv = graph.put("mv", [RB, NB, 2])
    var1, sdev1, rdev, rsum = (graph.put(n, [RB, NB]) for n in ("var1", "sdev1", "rdev", "rsum"))
    vn = graph.put("vn", [RB, 2, NB])
    wkv_at = graph.at
    wkv = graph.put("wkv", [128, KB, 2 * G * DK])
    bvb = graph.put("bvb", [L, G * DK])
    table = Shelf(graph.at)
    wr_raw = table.put("wr_raw", [128, 2, KB, D])
    wr_h = table.put("wr_h", [128, 2, KB, D], F32R)
    wr_l = table.put("wr_l", [128, 2, KB, D], F32R)
    hout = table.put("hout", [RB, NB, D])
    brel_at = table.at
    brel = table.put("brel", [RB, 2, D])
    side = Shelf(table.at)
    srt = side.put("srt", [MP, MS, 2])
    msg = Shelf(early_at).put("msg", [MP, MR, D])
    assert early_at + 4 * MR * D <= x1_at
    hot = side.put("hot", [MP, MR, 128], F32R)
    node = side.put("node", [MP, RB])
    tile_no = side.put("tile_no", [1, MS])
    tile_block = side.put("tile_block", [1, MS], I32)
    bself_h = side.put("bself_h", [1, D], F32R)
    bself_l = side.put("bself_l", [1, D], F32R)
    a1_h = side.put("a1_h", [128, KB, L], F32R)
    a1_l = side.put("a1_l", [128, KB, L], F32R)
    c1 = side.put("c1", [L, 1])
    assert side.at <= nc.sbuf_usable_end
    early = Shelf(early_at)
    above = early.put("above", [EP, NB + 1, MT])
    inb = early.put("inb", [EP, NB, MT])
    rank = early.put("rank", [EP, NB, MT])
    assert early.at <= early_at + 4 * NB * D
    early = Shelf(x1_at)
    cs = early.put("cs", [ET, 2, NB, EP])
    later_t = early.put("later_t", [ET, 2, MT + 1])
    later_p = early.put("later_p", [EP, EP])
    pk = early.put("pk", [EP, MT, 2])
    ei = early.put("ei", [EP, 3, ET], I32)
    assert early.at <= x1_at + 4 * NB * D
    early = Shelf(wkv_at)
    recv = early.put("recv", [EP, MT])
    send = early.put("send", [EP, MT])
    relrow = early.put("relrow", [EP, MT])
    nabove = early.put("nabove", [EP, MT])
    pos = early.put("pos", [EP, MT])
    pos_i = early.put("pos_i", [EP, MT], I32)
    pos_lane = early.put("pos_lane", [EP, MT], I32)
    pos_tile = early.put("pos_tile", [EP, MT], I32)
    slot = early.put("slot", [EP, MT], I32)
    count_i = early.put("count_i", [EP, NB], I32)
    tiles_i = early.put("tiles_i", [EP, NB], I32)
    tiles = early.put("tiles", [EP, NB])
    base = early.put("base", [EP, NB])
    base_m = early.put("base_m", [EP, NB])
    tb = [early.put(f"tb{i}", [1, MS]) for i in range(2)]
    assert early.at <= wkv_at + 4 * 2 * G * DK
    gat = Shelf(graph.at)
    msg_h = gat.put("msg_h", [MP, MR, D], F32R)
    msg_l = gat.put("msg_l", [MP, MR, D], F32R)
    LM_BYTES = 34816
    gat = Shelf(graph.at + LM_BYTES)
    wkt = gat.put("wkt", [128, G, D])
    a1w = gat.put("a1w", [128, G, L])
    a2w = gat.put("a2w", [L, L])
    rowc = gat.put("rowc", [L, 2])
    assert gat.at <= brel_at
    lm = Shelf(graph.at)
    xg = lm.put("xg", [128, 2, KB, RB])
    hid = lm.put("hid", [L, SPAD])
    wt = lm.put("wt", [L, N])
    wt2 = lm.put("wt2", [L, N])
    wtc = lm.put("wtc", [L, 4])
    w = lm.put("w", [RB, NB, L])
    ct = lm.put("ct", [128, KB, L])
    swb = lm.put("swb", [128, L])
    swc = lm.put("swc", [L, 1])
    kf = lm.put("kf", [128, G, L])
    vf = lm.put("vf", [L, G, DK])
    bq = lm.put("bq", [HG, G, L])
    assert lm.at <= graph.at + LM_BYTES

    att = Shelf(whole.at)
    wq_h = att.put("wq_h", [128, HU, D], F32R)
    wq_l = att.put("wq_l", [128, HU, D], F32R)
    p_at = att.at
    p_h = att.put("p_h", [128, KB, UC], F32R)
    p_l = att.put("p_l", [128, KB, UC], F32R)
    prob = att.put("prob", [RB, SR, UC])
    at_h = att.put("at_h", [L, HU, SPAD], F32R)
    at_l = att.put("at_l", [L, HU, SPAD], F32R)
    z_at = att.at
    z_h, z_l = zip(*((att.put(f"z_h{k}", [128, HU, SPAD], F32R), att.put(f"z_l{k}", [128, HU, SPAD], F32R))
                     for k in range(2)))
    zsq = att.put("zsq", [128, SPAD])
    w1_at = att.at
    w1_h, w1_l = zip(*((att.put(f"w1_h{f}", [128, HU, FH], F32R), att.put(f"w1_l{f}", [128, HU, FH], F32R))
                       for f in range(2)))
    brow_at = att.at
    brow = att.put("brow", [RB, UC])
    p_second = att.put("p_second", [128, UC])
    p_sum = att.put("p_sum", [128, UC])
    vcu_h = att.put("vcu_h", [L, DK], F32R)
    vcu_l = att.put("vcu_l", [L, DK], F32R)
    g1u = att.put("g1u", [128, HU])
    smax = att.put("smax", [RB, HU])
    ssum = att.put("ssum", [RB, HU])
    srec = att.put("srec", [RB, SR, HU])
    acc = att.put("acc", [128, FB, SPAD])
    zacc = att.put("zacc", [128, SPAD])
    assert att.at <= nc.sbuf_usable_end, (att.at, nc.sbuf_usable_end)

    assert p_at - whole.at >= 4 * FB * D and z_at - p_at >= 2 * 4 * FB * D
    w2_raw = Shelf(whole.at).put("w2_raw", [128, FB, D])
    o = Shelf(whole.at).put("o", [RB, NB, D])
    fin = Shelf(p_at)
    w2_h = fin.put("w2_h", [128, FB, D], F32R)
    w2_l = fin.put("w2_l", [128, FB, D], F32R)
    ht_h = Shelf(z_at).put("ht_h", [128, FB, SPAD], F32R)
    ht_l = Shelf(xn_at).put("ht_l", [128, FB, SPAD], F32R)
    assert FB <= 2 * HU and FB <= 2 * KB
    znorm = Shelf(brow_at).put("znorm", [128, SPAD])
    assert SPAD <= 2 * UC
    tail = Shelf(w1_at)
    x1r = tail.put("x1r", [RB, NB, D])
    b2b = tail.put("b2b", [RB, D])
    hss, hsd, hrn = (tail.put(n, [RB, NB]) for n in ("hss", "hsd", "hrn"))
    assert tail.at <= w1_at + 2 * 4 * HU * FH

    S = {n: sem(n) for n in (
        "edges_in", "cols_in", "consts", "pad_zero", "dve", "ln_var", "ln_sd", "rows_ready", "rows_t", "xn_hi",
        "xn_lo", "xg_ready", "wr_hi", "wr_lo", "table_mm", "hout_ready", "edge_cols", "blocks_ready", "pk_step",
        "pk_ready", "cs_mm", "cs_ready", "rank_mm", "slot_ready", "srt_pad", "slots_pad", "scattered", "srt_in",
        "hot_ready", "msg_hi", "msg_lo", "seg_mm", "bself_hi", "bself_lo", "agg_mm", "x1_ready", "x1_saved",
        "lm_in", "kv_in", "a1_mm", "a1_hi", "a1_lo", "c1_ready", "hid_mm", "hid_ready", "wt_mm", "wt_ready",
        "wt2_max", "wt2_exp", "wt2_ready", "wt_t", "w_sh", "w_exp", "w_ready", "lm_mm", "lm_ev", "ct_ready",
        "kc_mm", "kf_ready", "kc_hi", "kc_lo", "vc_mm", "vf_ready", "vc_hi", "vc_lo", "bq_mm", "bq_ready",
        "bq_saved", "lm_done", "wq_in", "wq_hi", "wq_lo", "w1_in", "w1_hi", "w1_lo", "brow_in", "p_mm", "p_second", "p_sum", "p_hi",
        "p_lo", "score_mm", "biased", "max_ready", "shifted", "exp_ready", "sum_ready", "rec_ready", "prob_ready",
        "prob_t", "att_hi", "att_lo", "unit_cols", "z_mm", "z_hi", "z_lo", "z_sq", "z_acc", "h_mm", "h_acc",
        "acc_zero", "w2_in", "w2_hi", "w2_lo", "fin_in", "n_mm", "n_sd", "h_sh", "h1_ready", "h1_sq", "h1_sum",
        "ss_mm", "h1_sd", "ht_hi", "ht_lo", "o_mm", "o_sh", "o_act", "o_ready", "out_done",
    )}
    x_in = [sem(f"x_in{b}") for b in range(NB)]
    wr_in = [sem(f"wr_in{k}") for k in range(2)]
    brel_in = [sem(f"brel_in{k}") for k in range(2)]
    h_saved = [sem(f"h_saved{b}") for b in range(NB)]
    msg_in = [sem(f"msg_in{k}") for k in range(MR)]

    block = ctx.enter_context(nc.Block())

    def spread(ap, shape):
        return ap.unsqueeze(len(shape) - 1).to_broadcast(shape)

    def over_relations(eng, step):
        step(0, 0, 0)
        step(1, 0, 1)
        with eng.Fori(1, R2 // 2) as i:
            step(2 * i, i, 0)
            step(2 * i + 1, i, 1)
        step(R2, R2 // 2, 0)

    def over_messages(eng, step, pause, meanwhile):
        for k in range(MR):
            step(k, 0, k)
        with eng.Fori(1, pause) as i:
            for k in range(MR):
                step(i * MR + k, i, k)
        meanwhile()
        with eng.Fori(pause, MS // MR) as i:
            for k in range(MR):
                step(i * MR + k, i, k)
        for k in range(MS % MR):
            step(MS - MS % MR + k, MS // MR, k)

    def over_units(eng, step):
        step(0, 0)
        step(1, 1)
        with eng.Fori(1, U // 2 - 1) as i:
            step(2 * i, 0)
            step(2 * i + 1, 1)
        step(U - 2, 0)
        step(U - 1, 1)

    PAUSE = MS // MR // 2

    OB = (4, 5, 6, 7, 0)

    def p_banks(v, kb, part):
        at = 2 * (kb % 2) if first(v) else 4
        return ps[:, at:at + 2, 0:4 * L].rearrange("p c (h a l) -> p c h a l", h=2, a=2)[:, :, :, part, :]

    def by_head(t):
        return t.rearrange("p (c h l) -> p c h l", c=2, h=2)

    def z_banks(h):
        return ps[:, 6:8, 0:SC] if h % 2 == 0 else ps[:, 4:6, 0:SC]

    def first(v):
        return isinstance(v, int) and v == 0

    def final(v, n):
        return isinstance(v, int) and v == n

    @block.sync
    def _(sp):
        for b in range(NB):
            sp.dma_start(xin[:, b, :], x[b * RB:(b + 1) * RB, :]).then_inc(x_in[b], 16)
        sp.dma_start(colc[:, :], cols).then_inc(S["cols_in"], 16)

        def load_wr(r, k):
            sp.dma_start(wr_raw[:, k, :, :].rearrange("p b d -> p (b d)"),
                         w_rel_t[bass.ds(r, 1), :, :].rearrange("a p n -> p (a n)")).then_inc(wr_in[k], 16)

        def load_brel(r, k):
            sp.dma_start(brel[:, k, :], b_rel[bass.ds(r, 1), :].to_broadcast([RB, D])).then_inc(brel_in[k], 16)

        load_wr(0, 0)
        for n, a in enumerate((src, dst, etype)):
            sp.dma_start(ei[:, n, :], a.rearrange("(p t) -> p t", t=ET)).then_inc(S["edges_in"], 16)
        load_brel(0, 0)
        load_wr(1, 1)
        load_brel(1, 1)
        sp.wait_ge(S["srt_pad"], 2)
        sp.dma_start(slots.rearrange("(p t) c -> p t c", t=MS), srt[:, :, :]).then_inc(S["slots_pad"], 16)
        sp.dma_start(bvb[:, :], b_v.to_broadcast([L, G * DK])).then_inc(S["kv_in"], 16)
        sp.dma_start(wq_raw[:, :, :].rearrange("p h d -> p (h d)"), wq_t[0]).then_inc(S["wq_in"], 16)
        sp.dma_start(w1_raw[:, :, :].rearrange("p h d -> p (h d)"), wz_w1[0, 0]).then_inc(S["w1_in"], 16)

        def load_wkv(kb):
            sp.dma_start(wkv[:, kb, :], w_kv[:, kb, :]).then_inc(S["kv_in"], 16)

        def table_step(r, i, k):
            if final(r, R2):
                return
            more = not final(r, R2 - 1)
            if more:
                sp.wait_ge(S["wr_hi"], r + 1)
                sp.wait_ge(S["wr_lo"], r + 1)
                load_wr(r + 2, k)
            for b in range(NB):
                sp.wait_ge(S["hout_ready"], NB * r + b + 1)
                sp.dma_start(h_table[bass.ds(r * N + b * RB, RB), :], hout[:, b, :]).then_inc(h_saved[b], 16)
            if more:
                load_brel(r + 2, k)

        step = table_step
        step(0, 0, 0)
        load_wkv(1)
        step(1, 0, 1)
        for kb in range(2, KB):
            load_wkv(kb)
        with sp.Fori(1, R2 // 2 - 1) as i:
            step(2 * i, i, 0)
            step(2 * i + 1, i, 1)
        step(R2 - 2, R2 // 2 - 1, 0)
        step(R2 - 1, R2 // 2 - 1, 1)

        sp.wait_ge(S["scattered"], 16 * MT)
        sp.dma_start(srt[:, :, :], slots.rearrange("(p t) c -> p t c", t=MS)).then_inc(S["srt_in"], 16)
        load_wkv(0)
        sp.wait_ge(S["table_mm"], NB * (R2 + 1))
        for b in range(NB):
            sp.wait_ge(h_saved[b], 16 * R2)
        sp.dma_start(a1w[:, :, :], aw1).then_inc(S["lm_in"], 16)
        sp.dma_start(a2w[:, :], aw2).then_inc(S["lm_in"], 16)
        sp.dma_start(rowc[:, 0:1], aw1_b).then_inc(S["lm_in"], 16)
        sp.dma_start(rowc[:, 1:2], aw2_b).then_inc(S["lm_in"], 16)
        for g in range(G):
            sp.wait_ge(S["seg_mm"], 4 * (g + 1))
            sp.dma_start(wkt[:, g, :], wk_t[:, g, :]).then_inc(S["lm_in"], 16)

        sp.wait_ge(S["x1_ready"], NB)
        sp.dma_start(x1_stash.rearrange("(b p) d -> p b d", p=RB), x1[:, :, :]).then_inc(S["x1_saved"], 16)

        sp.wait_ge(S["bq_ready"], 1)
        sp.dma_start(bqk_rows.rearrange("a (g h l) -> h (a g) l", g=G, h=HG), bq[:, :, :]).then_inc(S["bq_saved"], 16)
        sp.wait_ge(S["bq_saved"], 16)

        def load_w1(v, f):
            sp.wait_ge(S["w1_lo"], HU * (2 * v + f))
            sp.wait_ge(S["w1_hi"], 2 * v + f)
            sp.dma_start(w1_raw[:, :, :].rearrange("p h d -> p (h d)"),
                         wz_w1[bass.ds(v, 1), f].rearrange("a p n -> p (a n)")).then_inc(S["w1_in"], 16)

        def load_wq(v):
            sp.wait_ge(S["wq_lo"], HU * v)
            sp.wait_ge(S["wq_hi"], v)
            sp.dma_start(wq_raw[:, :, :].rearrange("p h d -> p (h d)"),
                         wq_t[bass.ds(v, 1)].rearrange("a p n -> p (a n)")).then_inc(S["wq_in"], 16)

        def load_brow(v):
            sp.dma_start(brow[:, :], bqk_rows[:, bass.ds(v * UC, UC)].to_broadcast([RB, UC]))\
                .then_inc(S["brow_in"], 16)

        sp.wait_ge(S["lm_done"], 1)
        load_brow(0)
        load_wq(1)

        def unit_step(v, k):
            if not first(v):
                load_w1(v, 0)
            if not (final(v, U - 2) or final(v, U - 1)):
                load_wq(v + 2)
            if not final(v, U - 1):
                sp.wait_ge(S["biased"], NB * (v + 1))
                load_brow(v + 1)
            load_w1(v, 1)

        over_units(sp, unit_step)

        sp.wait_ge(S["p_mm"], KB * U)
        sp.dma_start(w2_raw[:, :, :], w2).then_inc(S["w2_in"], 16)
        sp.wait_ge(S["h_mm"], HO * (U - 1) + HH)
        sp.dma_start(b2b[:, :], b2.to_broadcast([RB, D])).then_inc(S["fin_in"], 16)
        sp.wait_ge(S["x1_saved"], 16)
        sp.dma_start(x1r[:, :, :], x1_stash.rearrange("(b p) d -> p b d", p=RB)).then_inc(S["fin_in"], 16)
        for b in range(NB):
            sp.wait_ge(S["o_ready"], b + 1)
            sp.dma_start(out[b * RB:(b + 1) * RB, :], o[:, b, :]).then_inc(S["out_done"], 16)
        sp.wait_ge(S["out_done"], 16 * NB)

    @block.gpsimd
    def _(pool):
        pool.memset(ident[:, :], 0.0).then_inc(S["consts"], 1)
        pool.wait_ge(S["consts"], 1)
        pool.affine_select(out=ident[:, :], in_=ident[:, :], compare_op=ALU.not_equal, fill=1.0, base=0,
                           pattern=[[-1, 128]], channel_multiplier=1).then_inc(S["consts"], 1)
        pool.memset(ones[:, :], 1.0).then_inc(S["consts"], 1)
        pool.memset(ones_r[:, :].bitcast(F32), 1.0).then_inc(S["consts"], 1)
        pool.memset(xn_h[:, :, N:SPAD].bitcast(F32), 0.0).then_inc(S["consts"], 1)
        pool.memset(xn_l[:, :, N:SPAD].bitcast(F32), 0.0).then_inc(S["consts"], 1)

        pool.memset(srt[:, :, 0], 0.0).then_inc(S["srt_pad"], 1)
        pool.memset(srt[:, :, 1], -1.0).then_inc(S["srt_pad"], 1)
        pool.iota(node[:, :], [[1, RB]], base=0, channel_multiplier=0,
                  allow_small_or_imprecise_dtypes=True).then_inc(S["consts"], 1)
        pool.iota(tile_no[:, :], [[1, MS]], base=0, channel_multiplier=0,
                  allow_small_or_imprecise_dtypes=True).then_inc(S["consts"], 1)
        pool.memset(later_t[:, :, :], 1.0).then_inc(S["consts"], 1)
        pool.memset(later_p[:, :], 1.0).then_inc(S["consts"], 1)
        pool.wait_ge(S["consts"], 10)
        for h in range(2):
            pool.affine_select(out=later_t[:, h, :], in_=later_t[:, h, :], compare_op=ALU.is_ge, fill=0.0,
                               base=-h * ET - 1, pattern=[[1, MT + 1]], channel_multiplier=-1).then_inc(S["consts"], 1)
        pool.affine_select(out=later_p[:, :], in_=later_p[:, :], compare_op=ALU.is_ge, fill=0.0,
                           base=-1, pattern=[[1, EP]], channel_multiplier=-1).then_inc(S["consts"], 1)

        pool.wait_ge(S["edges_in"], 48)
        for n, part in ((0, slice(0, ET)), (1, slice(ET, MT))):
            pool.tensor_copy(recv[:, part], ei[:, n, :]).then_inc(S["edge_cols"], 1)
            pool.tensor_copy(send[:, part], ei[:, 1 - n, :]).then_inc(S["edge_cols"], 1)
        pool.tensor_scalar(relrow[:, 0:ET], ei[:, 2, :], float(N), None, ALU.mult).then_inc(S["edge_cols"], 1)
        pool.tensor_scalar(relrow[:, ET:MT], ei[:, 2, :], float(N), float(R * N), ALU.mult, ALU.add)\
            .then_inc(S["edge_cols"], 1)
        pool.memset(above[:, 0, :], 1.0).then_inc(S["edge_cols"], 1)
        pool.memset(above[:, NB, :], 0.0).then_inc(S["edge_cols"], 1)
        pool.wait_ge(S["edge_cols"], 8)
        for b in range(1, NB):
            pool.tensor_scalar(above[:, b, :], recv[:, :], float(b * RB), None, ALU.is_ge).then_inc(S["edge_cols"], 1)
        pool.wait_ge(S["edge_cols"], 8 + NB - 1)
        pool.tensor_tensor(inb[:, :, :], above[:, 0:NB, :], above[:, 1:NB + 1, :], ALU.subtract)\
            .then_inc(S["blocks_ready"], 1)
        pool.tensor_tensor(relrow[:, :], relrow[:, :], send[:, :], ALU.add).then_inc(S["pk_step"], 1)
        pool.tensor_tensor(nabove[:, :], above[:, 1, :], above[:, 2, :], ALU.add).then_inc(S["pk_step"], 1)
        for b in range(3, NB):
            pool.wait_ge(S["pk_step"], b - 1)
            pool.tensor_tensor(nabove[:, :], nabove[:, :], above[:, b, :], ALU.add).then_inc(S["pk_step"], 1)
        pool.wait_ge(S["pk_step"], NB - 1)
        pool.tensor_scalar(nabove[:, :], nabove[:, :], float(RB), None, ALU.mult).then_inc(S["pk_step"], 1)
        pool.wait_ge(S["pk_step"], NB)
        pool.tensor_copy(pk[:, :, 0].bitcast(I32), relrow[:, :]).then_inc(S["pk_ready"], 1)
        pool.tensor_tensor(pk[:, :, 1], recv[:, :], nabove[:, :], ALU.subtract).then_inc(S["pk_ready"], 1)

        pool.wait_ge(S["pk_ready"], 2)
        pool.wait_ge(S["slots_pad"], 16)
        pool.wait_ge(S["slot_ready"], 1)
        for t in range(MT):
            pool.indirect_dma_start(slots, bass.IndirectOffsetOnAxis(ap=slot[:, t:t + 1], axis=0), pk[:, t, :], None)\
                .then_inc(S["scattered"], 16)

        for b in range(NB):
            pool.wait_ge(h_saved[b], 16 * R2)
        pool.wait_ge(S["srt_in"], 16)

        for t in range(MS):
            k = t % MR
            if t >= MR:
                pool.wait_ge(S["msg_hi"], t + 1 - MR)
                pool.wait_ge(S["msg_lo"], t + 1 - MR)
            pool.indirect_dma_start(msg[:, k, :], None, h_table,
                                    bass.IndirectOffsetOnAxis(ap=srt[:, t, 0:1].bitcast(I32), axis=0))\
                .then_inc(msg_in[k], 16)

        def split_w1(v, f, heads):
            pool.wait_ge(S["w1_hi"], 2 * v + f + 1)
            for h in heads:
                pool.tensor_tensor(w1_l[f][:, h, :], w1_raw[:, h, :], w1_h[f][:, h, :].bitcast(F32),
                                   ALU.subtract).then_inc(S["w1_lo"], 1)

        def split_wq(v, heads):
            pool.wait_ge(S["wq_hi"], v + 1)
            for h in heads:
                pool.tensor_tensor(wq_l[:, h, :], wq_raw[:, h, :], wq_h[:, h, :].bitcast(F32),
                                   ALU.subtract).then_inc(S["wq_lo"], 1)

        split_wq(0, range(HU))

        pool.wait_ge(S["lm_done"], 1)
        pool.wait_ge(S["bq_saved"], 16)
        pool.wait_ge(S["x1_saved"], 16)
        for a in (at_h, at_l):
            pool.memset(a[:, :, N:SPAD].bitcast(F32), 0.0).then_inc(S["pad_zero"], 1)
        pool.memset(acc[:, :, :], 0.0).then_inc(S["acc_zero"], 1)
        pool.memset(zacc[:, :], 0.0).then_inc(S["z_acc"], 1)

        def unit_step(v, k):
            g = v // UG
            if not first(v):
                pool.wait_ge(S["z_mm"], HU * v)
                pool.wait_ge(S["z_hi"], HU * v)
                pool.wait_ge(S["z_lo"], HU * v)
            pool.tensor_copy(vcu_h[:, :], vc_h[:, bass.ds(g, 1), :].rearrange("p a d -> p (a d)").bitcast(F32))\
                .then_inc(S["unit_cols"], 1)
            pool.tensor_copy(vcu_l[:, :], vc_l[:, bass.ds(g, 1), :].rearrange("p a d -> p (a d)").bitcast(F32))\
                .then_inc(S["unit_cols"], 1)
            pool.tensor_copy(g1u[:, :], colc[:, bass.ds(C_G1 + v * HU, HU)]).then_inc(S["unit_cols"], 1)

            def normalise(j):
                pool.wait_ge(S["rec_ready"], NB * v + j + 1)
                pj = prob[:, j % SR, :].rearrange("p (h l) -> p h l", h=HU)
                pool.tensor_tensor(pj, pj, spread(srec[:, j % SR, :], [RB, HU, L]), ALU.mult)\
                    .then_inc(S["prob_ready"], 1)

            more = not final(v, U - 1)
            normalise(0)
            if not first(v):
                split_w1(v - 1, 1, range(0, 3))
            normalise(1)
            if not first(v):
                split_w1(v - 1, 1, range(3, 4))
            if more:
                split_wq(v + 1, range(0, 1))
            normalise(2)
            if more:
                split_wq(v + 1, range(1, 3))
            normalise(3)
            if more:
                split_wq(v + 1, range(3, 4))
            normalise(4)
            split_w1(v, 0, range(HU))
            for h in range(HU):
                pool.wait_ge(S["z_sq"], HU * v + h + 1)
                pool.wait_ge(S["z_acc"], HU * v + h + 1)
                pool.tensor_tensor(zacc[:, :], zacc[:, :], zsq[:, :], ALU.add).then_inc(S["z_acc"], 1)

        over_units(pool, unit_step)
        split_w1(U - 1, 1, range(HU))

        pool.wait_ge(S["n_mm"], 1)
        for f in range(FB):
            pool.wait_ge(S["h1_ready"], f + 1)
            if f == 0:
                pool.tensor_tensor(zacc[:, :], acc[:, f, :], acc[:, f, :], ALU.mult).then_inc(S["h1_sum"], 1)
            else:
                pool.wait_ge(S["h1_sum"], f)
                pool.tensor_tensor(zsq[:, :], acc[:, f, :], acc[:, f, :], ALU.mult).then_inc(S["h1_sq"], 1)
                pool.wait_ge(S["h1_sq"], f)
                pool.tensor_tensor(zacc[:, :], zacc[:, :], zsq[:, :], ALU.add).then_inc(S["h1_sum"], 1)

    @block.scalar
    def _(act):
        def hi(dst, source, done):
            nc.scalar.activation(dst, source, ACT.Copy).then_inc(S[done], 1)

        act.wait_ge(S["ln_var"], 1)
        nc.scalar.activation(sdev1[:, :], var1[:, :], ACT.Sqrt).then_inc(S["ln_sd"], 1)

        def split_wr(r, i, k):
            act.wait_ge(wr_in[k], 16 * (i + 1))
            if not first(i):
                act.wait_ge(S["table_mm"], NB * (r - 1))
            hi(wr_h[:, k, :, :], wr_raw[:, k, :, :], "wr_hi")

        split_wr(0, 0, 0)
        for b in range(NB):
            act.wait_ge(S["rows_t"], b + 1)
            hi(xn_h[:, :, b * RB:(b + 1) * RB], ps[:, b, 0:KB * RB].rearrange("p (k n) -> p k n", k=KB), "xn_hi")
        split_wr(1, 0, 1)
        act.wait_ge(S["cs_mm"], 1)
        for c in range(2):
            nc.scalar.activation(cs[:, c, 0:4, :], ps[0:ET, 5 + c, 0:4 * EP].rearrange("p (b n) -> p b n", b=4),
                                 ACT.Copy).then_inc(S["cs_ready"], 1)
        nc.scalar.activation(cs[:, :, 4, :], ps[0:ET, 7, 0:2 * EP].rearrange("p (c n) -> p c n", c=2), ACT.Copy)\
            .then_inc(S["cs_ready"], 1)
        with act.Fori(1, R2 // 2) as i:
            split_wr(2 * i, i, 0)
            split_wr(2 * i + 1, i, 1)
        split_wr(R2, R2 // 2, 0)

        act.wait_ge(brel_in[0], 16 * (R2 // 2 + 1))
        hi(bself_h[:, :], brel[0:1, 0, :], "bself_hi")
        act.wait_ge(S["table_mm"], NB * (R2 + 1))

        def split_msg(t, i, k):
            act.wait_ge(msg_in[k], 16 * (i + 1))
            if not first(i):
                act.wait_ge(S["seg_mm"], t + 1 - MR)
            hi(msg_h[:, k, :], msg[:, k, :], "msg_hi")

        def hi_a1():
            act.wait_ge(S["a1_mm"], 1)
            hi(a1_h[:, :, :], ps[:, 7, 0:KB * L].rearrange("p (k l) -> p k l", k=KB), "a1_hi")

        over_messages(act, split_msg, PAUSE + 3, hi_a1)

        def split_wq(v):
            act.wait_ge(S["wq_in"], 16 * (v + 1))
            if not first(v):
                act.wait_ge(S["p_mm"], KB * v)
            hi(wq_h[:, :, :], wq_raw[:, :, :], "wq_hi")

        act.wait_ge(S["ln_var"], 2)
        nc.scalar.activation(vn[:, :, :], vn[:, :, :], ACT.Sqrt).then_inc(S["ln_sd"], 1)
        for b in range(NB):
            act.wait_ge(S["xg_ready"], b + 1)
            hi(xn_h[:, :, b * RB:(b + 1) * RB], xg[:, b % 2, :, :], "xn_hi")
        split_wq(0)
        act.wait_ge(S["hid_mm"], 1)
        act.wait_ge(S["c1_ready"], 1)
        nc.scalar.activation(hid[:, :].rearrange("p (c n) -> p c n", c=2), ps[0:L, 0:2, 0:SC], ACT.Silu,
                             bias=c1[:, 0:1]).then_inc(S["hid_ready"], 1)
        act.wait_ge(S["wt2_max"], 1)
        nc.scalar.activation(wt2[:, :], wt[:, :], ACT.Exp, bias=wtc[:, 0:1], accum_out=wtc[:, 1:2])\
            .then_inc(S["wt2_exp"], 1)
        act.wait_ge(S["w_sh"], 1)
        nc.scalar.activation(w[:, :, :], w[:, :, :], ACT.Exp).then_inc(S["w_exp"], 1)
        act.wait_ge(S["kf_ready"], 1)
        hi(kc[:, :, 0, :], kf[:, :, :], "kc_hi")
        act.wait_ge(S["vf_ready"], 1)
        hi(vc_h[:, :, :], vf[:, :, :], "vc_hi")

        def split_w1(v, f):
            act.wait_ge(S["w1_in"], 16 * (2 * v + f + 1))
            if not first(v):
                act.wait_ge(S["h_mm"], HO * (v - 1) + HH * (f + 1))
            hi(w1_h[f][:, :, :], w1_raw[:, :, :], "w1_hi")

        def second_p(v, kb):
            act.wait_ge(S["p_mm"], KB * v + kb + 1)
            nc.scalar.activation(by_head(p_second[:, :]), p_banks(v, kb, 1), ACT.Copy).then_inc(S["p_second"], 1)

        def hi_p(v, kb):
            act.wait_ge(S["p_sum"], KB * v + kb + 1)
            if kb == 0 and not first(v):
                act.wait_ge(S["score_mm"], NB * v)
            hi(p_h[:, kb, :], p_sum[:, :], "p_hi")

        act.wait_ge(S["lm_done"], 1)
        for kb in range(KB):
            second_p(0, kb)
            hi_p(0, kb)
        act.wait_ge(S["bq_saved"], 16)
        act.wait_ge(S["x1_saved"], 16)

        def unit_step(v, k):
            def exp(j):
                act.wait_ge(S["shifted"], NB * v + j + 1)
                nc.scalar.activation(prob[:, j % SR, :], prob[:, j % SR, :], ACT.Exp).then_inc(S["exp_ready"], 1)

            def hi_att(j):
                act.wait_ge(S["prob_t"], NB * v + j + 1)
                if j == 0:
                    if first(v):
                        act.wait_ge(S["pad_zero"], 2)
                    else:
                        act.wait_ge(S["z_mm"], HU * v)
                hi(at_h[:, :, j * RB:(j + 1) * RB], ps[0:L, 6, 0:HU * RB].rearrange("p (h n) -> p h n", h=HU),
                   "att_hi")

            def hi_z(h):
                act.wait_ge(S["z_mm"], HU * v + h + 1)
                if h == 0:
                    act.wait_ge(S["unit_cols"], 3 * (v + 1))
                    if not (first(v) or first(v - 1)):
                        act.wait_ge(S["h_mm"], HO * (v - 1))
                zp = z_banks(h)
                nc.scalar.activation(z_h[k][:, h, :].rearrange("p (c n) -> p c n", c=2), zp, ACT.Copy,
                                     scale=g1u[:, h:h + 1]).then_inc(S["z_hi"], 1)
                act.wait_ge(S["z_acc"], HU * v + h + 1)
                nc.scalar.activation(zsq[:, :].rearrange("p (c n) -> p c n", c=2), zp, ACT.Square)\
                    .then_inc(S["z_sq"], 1)

            more = not final(v, U - 1)
            exp(0)
            if not first(v):
                split_w1(v - 1, 1)
            exp(1)
            hi_att(0)
            if more:
                split_wq(v + 1)
            exp(2)
            hi_att(1)
            exp(3)
            hi_att(2)
            exp(4)
            if more:
                second_p(v + 1, 0)
            hi_att(3)
            if more:
                hi_p(v + 1, 0)
                second_p(v + 1, 1)
            hi_att(4)
            if more:
                hi_p(v + 1, 1)
            split_w1(v, 0)
            if more:
                second_p(v + 1, 2)
            hi_z(0)
            if more:
                hi_p(v + 1, 2)
                second_p(v + 1, 3)
            hi_z(1)
            if more:
                hi_p(v + 1, 3)
            hi_z(2)
            hi_z(3)

        over_units(act, unit_step)
        split_w1(U - 1, 1)

        act.wait_ge(S["w2_in"], 16)
        act.wait_ge(S["z_mm"], HU * U)
        for f in range(FB):
            nc.scalar.activation(w2_h[:, f, :], w2_raw[:, f, :], ACT.Copy,
                                 scale=colc[:, C_G2 + f:C_G2 + f + 1]).then_inc(S["w2_hi"], 1)
        act.wait_ge(S["n_mm"], 1)
        nc.scalar.activation(znorm[:, :].rearrange("p (c n) -> p c n", c=2), ps[:, 0:2, 0:SC], ACT.Sqrt)\
            .then_inc(S["n_sd"], 1)
        for f in range(FB):
            act.wait_ge(S["h_sh"], f + 1)
            nc.scalar.activation(acc[:, f, :], acc[:, f, :], ACT.Silu, bias=colc[:, C_B1 + f:C_B1 + f + 1])\
                .then_inc(S["h1_ready"], 1)
            act.wait_ge(S["h1_ready"], f + 1)
            hi(ht_h[:, f, :], acc[:, f, :], "ht_hi")
        act.wait_ge(S["ss_mm"], 1)
        nc.scalar.activation(hsd[:, :], ps[0:RB, 1, 0:NB], ACT.Sqrt).then_inc(S["h1_sd"], 1)
        for b in range(NB):
            act.wait_ge(S["o_sh"], b + 1)
            nc.scalar.activation(o[:, b, :], o[:, b, :], ACT.Silu).then_inc(S["o_act"], 1)

    @block.vector
    def _(dve):
        chain = [0]

        def link(ins):
            chain[0] += 1
            ins.then_inc(S["dve"], 1)
            dve.wait_ge(S["dve"], chain[0])

        def lo(dst, source, part, done):
            dve.tensor_tensor(dst, source, part.bitcast(F32), ALU.subtract).then_inc(S[done], 1)

        for b in range(NB):
            dve.wait_ge(x_in[b], 16)
            ins = dve.bn_stats(stat[:, b, :], xin[:, b, :])
        link(ins)
        for b in range(NB):
            ins = dve.bn_aggr(mv[:, b, :], stat[:, b, :])
        link(ins)
        dve.tensor_scalar(var1[:, :], mv[:, :, 1], LN_EPS, None, ALU.add).then_inc(S["ln_var"], 1)
        dve.wait_ge(S["ln_sd"], 1)
        link(dve.reciprocal(rdev[:, :], sdev1[:, :]))
        for b in range(NB):
            dve.tensor_scalar(rows[:, b, :], xin[:, b, :], mv[:, b, 0:1], rdev[:, b:b + 1],
                              ALU.subtract, ALU.mult).then_inc(S["rows_ready"], 1)

        def split_wr(r, i, k):
            dve.wait_ge(S["wr_hi"], r + 1)
            lo(wr_l[:, k, :, :], wr_raw[:, k, :, :], wr_h[:, k, :, :], "wr_lo")

        split_wr(0, 0, 0)
        for b in range(NB):
            dve.wait_ge(S["xn_hi"], b + 1)
            cut = slice(b * RB, (b + 1) * RB)
            lo(xn_l[:, :, cut], ps[:, b, 0:KB * RB].rearrange("p (k n) -> p k n", k=KB), xn_h[:, :, cut], "xn_lo")

        def drain_table(r, i, k):
            dve.wait_ge(brel_in[k], 16 * (i + 1))
            for b in range(NB):
                dve.wait_ge(S["table_mm"], NB * r + b + 1)
                if not first(r):
                    dve.wait_ge(h_saved[b], 16 * r)
                dve.tensor_tensor(hout[:, b, :], ps[0:RB, b, :], brel[:, k, :], ALU.add)\
                    .then_inc(S["hout_ready"], 1)

        split_wr(1, 0, 1)
        drain_table(0, 0, 0)

        dve.wait_ge(S["rank_mm"], 1)
        ranks = ((5, 0, 3), (6, 3, NB))
        psr = {q: ps[0:EP, q, 0:(b1 - b0) * (MT + 1)].rearrange("p (b t) -> p b t", b=b1 - b0) for q, b0, b1 in ranks}
        for q, b0, b1 in ranks:
            ins = dve.tensor_scalar(count_i[:, b0:b1], psr[q][:, :, MT], float(MP - 1), None, ALU.add)
        link(ins)
        link(dve.tensor_scalar(tiles_i[:, :], count_i[:, :], MP.bit_length() - 1, None, ALU.arith_shift_right))
        dve.memset(base[:, 0:1], 0.0)
        link(dve.tensor_copy(tiles[:, :], tiles_i[:, :]))
        for b in range(1, NB):
            link(dve.tensor_tensor(base[:, b:b + 1], base[:, b - 1:b], tiles[:, b - 1:b], ALU.add))
        link(dve.tensor_scalar(base_m[:, :], base[:, :], float(MP), None, ALU.mult))
        for q, b0, b1 in ranks:
            ins = dve.tensor_tensor(rank[:, b0:b1, :], psr[q][:, :, 0:MT], spread(base_m[:, b0:b1], [EP, b1 - b0, MT]),
                                    ALU.add)
        link(ins)
        link(dve.tensor_tensor(rank[:, :, :], rank[:, :, :], inb[:, :, :], ALU.mult))
        link(dve.tensor_reduce(pos[:, :], rank[:, :, :].rearrange("p b t -> p t b"), AX.X, ALU.add))
        link(dve.tensor_copy(pos_i[:, :], pos[:, :]))
        dve.tensor_scalar(pos_lane[:, :], pos_i[:, :], MP - 1, None, ALU.bitwise_and)
        link(dve.tensor_scalar(pos_tile[:, :], pos_i[:, :], MP.bit_length() - 1, None, ALU.arith_shift_right))
        dve.scalar_tensor_tensor(out=slot[:, :], in0=pos_lane[:, :], scalar=float(MS), in1=pos_tile[:, :],
                                 op0=ALU.mult, op1=ALU.add).then_inc(S["slot_ready"], 1)
        dve.wait_ge(S["consts"], 8)
        link(dve.tensor_scalar(tb[1][:, :], tile_no[:, :], base[0:1, 1:2], None, ALU.is_ge))
        for b in range(2, NB):
            to = tile_block if b == NB - 1 else tb[b % 2]
            ins = dve.scalar_tensor_tensor(out=to[:, :], in0=tile_no[:, :], scalar=base[0:1, b:b + 1],
                                           in1=tb[(b - 1) % 2][:, :], op0=ALU.is_ge, op1=ALU.add)
            if b < NB - 1:
                link(ins)
        ins.then_inc(S["slot_ready"], 1)

        with dve.Fori(1, R2 // 2) as i:
            split_wr(2 * i, i, 0)
            drain_table(2 * i - 1, i - 1, 1)
            split_wr(2 * i + 1, i, 1)
            drain_table(2 * i, i, 0)
        split_wr(R2, R2 // 2, 0)
        drain_table(R2 - 1, R2 // 2 - 1, 1)
        dve.wait_ge(S["bself_hi"], 1)
        lo(bself_l[:, :], brel[0:1, 0, :], bself_h[:, :], "bself_lo")
        dve.wait_ge(S["srt_in"], 16)
        dve.wait_ge(S["table_mm"], NB * (R2 + 1))

        def split_msg(t, i, k):
            if not first(i):
                dve.wait_ge(S["seg_mm"], t + 1 - MR)
            dve.tensor_scalar(hot[:, k, 0:RB], node[:, :], srt[:, bass.ds(t, 1), 1], None, ALU.is_equal)\
                .then_inc(S["hot_ready"], 1)
            dve.wait_ge(S["msg_hi"], t + 1)
            lo(msg_l[:, k, :], msg[:, k, :], msg_h[:, k, :], "msg_lo")

        def lo_a1():
            dve.wait_ge(S["a1_hi"], 1)
            lo(a1_l[:, :, :], ps[:, 7, 0:KB * L].rearrange("p (k l) -> p k l", k=KB), a1_h[:, :, :], "a1_lo")
            dve.tensor_tensor(c1[:, :], ps[0:L, 6, 0:1], rowc[:, 0:1], ALU.add).then_inc(S["c1_ready"], 1)

        over_messages(dve, split_msg, PAUSE + 3, lo_a1)

        for b in range(NB):
            dve.wait_ge(S["agg_mm"], b + 1)
            dve.scalar_tensor_tensor(out=x1[:, b, :], in0=ps[0:RB, b, :], scalar=0.0, in1=xin[:, b, :],
                                     op0=ALU.max, op1=ALU.add).then_inc(S["x1_ready"], 1)
        dve.wait_ge(S["x1_ready"], NB)
        dve.wait_ge(S["cols_in"], 16)

        for b in range(NB):
            ins = dve.bn_stats(stat[:, b, :], x1[:, b, :])
        link(ins)
        for b in range(NB):
            ins = dve.bn_aggr(mv[:, b, :], stat[:, b, :])
        link(ins)
        link(dve.tensor_scalar(vn[:, 0, :], mv[:, :, 1], LN_EPS, None, ALU.add))
        link(dve.reciprocal(rdev[:, :], vn[:, 0, :]))
        dve.scalar_tensor_tensor(out=vn[:, 1, :], in0=mv[:, :, 1], scalar=float(D), in1=rdev[:, :],
                                 op0=ALU.mult, op1=ALU.mult).then_inc(S["ln_var"], 1)
        dve.wait_ge(S["ln_sd"], 2)
        link(dve.tensor_scalar(vn[:, 1, :], vn[:, 1, :], L2_EPS, None, ALU.max))
        link(dve.reciprocal(vn[:, :, :], vn[:, :, :]))
        link(dve.scalar_tensor_tensor(out=rdev[:, :], in0=vn[:, 0, :], scalar=float(D) ** 0.5, in1=vn[:, 1, :],
                                      op0=ALU.mult, op1=ALU.mult))
        for b in range(NB):
            dve.tensor_scalar(rows[:, b, :], x1[:, b, :], mv[:, b, 0:1], rdev[:, b:b + 1],
                              ALU.subtract, ALU.mult).then_inc(S["rows_ready"], 1)

        gam = spread(colc[:, C_GAMMA:C_GAMMA + KB], [128, KB, RB])
        for b in range(NB + 1):
            if b < NB:
                dve.wait_ge(S["rows_t"], NB + b + 1)
                if b >= 2:
                    dve.wait_ge(S["xn_hi"], NB + b - 1)
                    dve.wait_ge(S["xn_lo"], NB + b - 1)
                dve.tensor_tensor(xg[:, b % 2, :, :], ps[:, b, 0:KB * RB].rearrange("p (k n) -> p k n", k=KB),
                                  gam, ALU.mult).then_inc(S["xg_ready"], 1)
            if b > 0:
                cut = slice((b - 1) * RB, b * RB)
                dve.wait_ge(S["xn_hi"], NB + b)
                lo(xn_l[:, :, cut], xg[:, (b - 1) % 2, :, :], xn_h[:, :, cut], "xn_lo")

        dve.wait_ge(S["wt_mm"], 1)
        for c, n in ((0, SC), (1, N - SC)):
            ins = dve.tensor_scalar(wt[:, c * SC:c * SC + n], ps[0:L, 2 + c, 0:n], rowc[:, 1:2], None, ALU.add)
            ins.then_inc(S["wt_ready"], 1)
        dve.wait_ge(S["wt_ready"], 2)
        dve.tensor_reduce(wtc[:, 0:1], wt[:, :], AX.X, ALU.max, negate=True).then_inc(S["wt2_max"], 1)
        dve.wait_ge(S["wt2_exp"], 1)
        link(dve.reciprocal(wtc[:, 2:3], wtc[:, 1:2]))
        dve.tensor_scalar(wt2[:, :], wt2[:, :], wtc[:, 2:3], 0.5 / L, ALU.mult, ALU.mult).then_inc(S["wt2_ready"], 1)
        dve.wait_ge(S["wt_t"], 1)
        wps = ps[0:RB, 4, 0:NB * L].rearrange("p (b l) -> p b l", b=NB)
        link(dve.tensor_reduce(rdev[:, :], wps, AX.X, ALU.max))
        dve.tensor_tensor(w[:, :, :], wps, spread(rdev[:, :], [RB, NB, L]), ALU.subtract).then_inc(S["w_sh"], 1)
        dve.wait_ge(S["w_exp"], 1)
        link(dve.tensor_reduce(rsum[:, :], w[:, :, :], AX.X, ALU.add))
        link(dve.reciprocal(rdev[:, :], rsum[:, :]))
        link(dve.tensor_tensor(w[:, :, :], w[:, :, :], spread(rdev[:, :], [RB, NB, L]), ALU.mult))
        dve.wait_ge(S["wt_t"], 2)
        dve.scalar_tensor_tensor(out=w[:, :, :], in0=w[:, :, :], scalar=0.5 / N,
                                 in1=ps[0:RB, 5, 0:NB * L].rearrange("p (b l) -> p b l", b=NB),
                                 op0=ALU.mult, op1=ALU.add).then_inc(S["w_ready"], 1)
        dve.wait_ge(S["lm_mm"], 1)
        dve.tensor_tensor(ct[:, :, :], ps[:, 7, 0:KB * L].rearrange("p (k l) -> p k l", k=KB),
                          spread(colc[:, C_GAMMA:C_GAMMA + KB], [128, KB, L]), ALU.mult).then_inc(S["ct_ready"], 1)
        dve.wait_ge(S["lm_mm"], 2)
        dve.tensor_copy(swb[:, :], ps[:, 6, 0:L]).then_inc(S["lm_ev"], 1)
        dve.tensor_copy(swc[:, :], ps[0:L, 6, 128:129]).then_inc(S["lm_ev"], 1)
        dve.wait_ge(S["lm_ev"], 2)
        for g in range(G):
            if g % 4 == 0:
                dve.wait_ge(S["kc_mm"], g // 4 + 1)
            ins = dve.scalar_tensor_tensor(out=kf[:, g, :], in0=swb[:, :], scalar=colc[:, C_BK + g:C_BK + g + 1],
                                           in1=ps[:, g // 4, (g % 4) * L:(g % 4 + 1) * L],
                                           op0=ALU.mult, op1=ALU.add)
        link(ins)
        dve.tensor_scalar(kf[:, :, :], kf[:, :, :], float(DK) ** -0.5, None, ALU.mult).then_inc(S["kf_ready"], 1)
        dve.wait_ge(S["vc_mm"], 1)
        dve.scalar_tensor_tensor(out=vf[:, :, :].rearrange("p g d -> p (g d)").rearrange("p (c n) -> p c n", c=2),
                                 in0=bvb[:, :].rearrange("p (c n) -> p c n", c=2), scalar=swc[:, 0:1],
                                 in1=ps[0:L, 2:4, :], op0=ALU.mult, op1=ALU.add).then_inc(S["vf_ready"], 1)
        dve.wait_ge(S["kc_hi"], 1)
        lo(kc[:, :, 1, :], kf[:, :, :], kc[:, :, 0, :], "kc_lo")
        dve.wait_ge(S["vc_hi"], 1)
        lo(vc_l[:, :, :], vf[:, :, :], vc_h[:, :, :], "vc_lo")
        dve.wait_ge(S["bq_mm"], 1)
        dve.tensor_copy(bq[:, :, :].rearrange("p (c g) l -> p c g l", c=2),
                        ps[0:HG, 4:6, 0:4 * L].rearrange("p c (g l) -> p c g l", g=4)).then_inc(S["bq_ready"], 1)
        for n in ("kc_lo", "vc_lo", "bq_ready"):
            dve.wait_ge(S[n], 1)
        dve.nop().then_inc(S["lm_done"], 1)

        def sum_p(v, kb):
            dve.wait_ge(S["p_second"], KB * v + kb + 1)
            if kb > 0 or not first(v):
                dve.wait_ge(S["p_lo"], KB * v + kb)
            dve.tensor_tensor(by_head(p_sum[:, :]), p_banks(v, kb, 0), by_head(p_second[:, :]), ALU.add)\
                .then_inc(S["p_sum"], 1)

        def lo_p(v, kb):
            dve.wait_ge(S["p_hi"], KB * v + kb + 1)
            lo(p_l[:, kb, :], p_sum[:, :], p_h[:, kb, :], "p_lo")

        for kb in range(KB):
            sum_p(0, kb)
            lo_p(0, kb)
        dve.wait_ge(S["bq_saved"], 16)
        dve.wait_ge(S["x1_saved"], 16)

        def add_h(v, n):
            f, c = n // 2, n % 2
            dve.wait_ge(S["h_mm"], HO * v + n + 1)
            a = acc[:, f, c * SC:(c + 1) * SC]
            dve.tensor_tensor(a, a, ps[:, 2 + n % 2, 0:SC], ALU.add).then_inc(S["h_acc"], 1)

        def unit_step(v, k):
            def softmax(j):
                q = NB * v + j
                pj = prob[:, j % SR, :].rearrange("p (h l) -> p h l", h=HU)
                if j >= SR:
                    dve.wait_ge(S["prob_t"], q + 1 - SR)
                elif not first(v):
                    dve.wait_ge(S["prob_t"], NB * v - {0: 1, 1: 0, 2: 2}[j])
                if j == 0:
                    dve.wait_ge(S["brow_in"], 16 * (v + 1))
                dve.wait_ge(S["score_mm"], q + 1)
                dve.tensor_tensor(prob[:, j % SR, :], ps[0:RB, j % 2, 0:UC], brow[:, :], ALU.add)\
                    .then_inc(S["biased"], 1)
                dve.wait_ge(S["biased"], q + 1)
                dve.tensor_reduce(smax[:, :], pj, AX.X, ALU.max).then_inc(S["max_ready"], 1)
                dve.wait_ge(S["max_ready"], q + 1)
                dve.tensor_tensor(pj, pj, spread(smax[:, :], [RB, HU, L]), ALU.subtract).then_inc(S["shifted"], 1)
                dve.wait_ge(S["exp_ready"], q + 1)
                dve.tensor_reduce(ssum[:, :], pj, AX.X, ALU.add).then_inc(S["sum_ready"], 1)
                dve.wait_ge(S["sum_ready"], q + 1)
                dve.reciprocal(srec[:, j % SR, :], ssum[:, :]).then_inc(S["rec_ready"], 1)

            def lo_att(j):
                dve.wait_ge(S["att_hi"], NB * v + j + 1)
                cut = slice(j * RB, (j + 1) * RB)
                lo(at_l[:, :, cut], ps[0:L, 6, 0:HU * RB].rearrange("p (h n) -> p h n", h=HU), at_h[:, :, cut],
                   "att_lo")

            def lo_z(h):
                dve.wait_ge(S["z_sq"], HU * v + h + 1)
                dve.scalar_tensor_tensor(out=z_l[k][:, h, :].rearrange("p (c n) -> p c n", c=2), in0=z_banks(h),
                                         scalar=g1u[:, h:h + 1],
                                         in1=z_h[k][:, h, :].rearrange("p (c n) -> p c n", c=2).bitcast(F32),
                                         op0=ALU.mult, op1=ALU.subtract).then_inc(S["z_lo"], 1)

            def add(n):
                if not first(v):
                    add_h(v - 1, n)

            more = not final(v, U - 1)
            softmax(0)
            add(0)
            softmax(1)
            add(1)
            add(2)
            lo_att(0)
            softmax(2)
            add(3)
            add(4)
            lo_att(1)
            softmax(3)
            add(5)
            lo_att(2)
            softmax(4)
            add(6)
            if more:
                sum_p(v + 1, 0)
            add(7)
            lo_att(3)
            if more:
                lo_p(v + 1, 0)
                sum_p(v + 1, 1)
            add(8)
            lo_att(4)
            if more:
                lo_p(v + 1, 1)
                sum_p(v + 1, 2)
            add(9)
            add(10)
            lo_z(0)
            if more:
                lo_p(v + 1, 2)
                sum_p(v + 1, 3)
            add(11)
            add(12)
            lo_z(1)
            if more:
                lo_p(v + 1, 3)
            add(13)
            lo_z(2)
            add(14)
            lo_z(3)
            add(15)

        dve.wait_ge(S["acc_zero"], 1)
        over_units(dve, unit_step)
        def lo_w2(f):
            dve.wait_ge(S["w2_hi"], f + 1)
            dve.scalar_tensor_tensor(out=w2_l[:, f, :], in0=w2_raw[:, f, :], scalar=colc[:, C_G2 + f:C_G2 + f + 1],
                                     in1=w2_h[:, f, :].bitcast(F32), op0=ALU.mult, op1=ALU.subtract)\
                .then_inc(S["w2_lo"], 1)

        def norms(c):
            cut = slice(c * (SPAD // 4), (c + 1) * (SPAD // 4))
            if c == 0:
                dve.wait_ge(S["n_sd"], 1)
            link(dve.tensor_scalar(znorm[:, cut], znorm[:, cut], L2_EPS, None, ALU.max))
            link(dve.reciprocal(znorm[:, cut], znorm[:, cut]))

        def scaled(f):
            dve.wait_ge(S["h_acc"], HO * (U - 1) + 2 * f + 2)
            dve.scalar_tensor_tensor(out=acc[:, f, :], in0=acc[:, f, :], scalar=float(G * HG * DK) ** 0.5,
                                     in1=znorm[:, :], op0=ALU.mult, op1=ALU.mult).then_inc(S["h_sh"], 1)

        def lo_h(f):
            dve.wait_ge(S["ht_hi"], f + 1)
            lo(ht_l[:, f, :], acc[:, f, :], ht_h[:, f, :], "ht_lo")

        for n in range(HO):
            add_h(U - 1, n)
            if n < 4:
                lo_w2(2 * n)
                lo_w2(2 * n + 1)
            elif n < 8:
                norms(n - 4)
                if n == 7:
                    scaled(0)
            elif n < HO - 2:
                scaled(n - 7)
                lo_h(n - 8)
        scaled(FB - 1)
        for f in range(6, FB):
            lo_h(f)
        dve.wait_ge(S["h1_sd"], 1)
        link(dve.tensor_scalar(hss[:, :], hsd[:, :], L2_EPS, None, ALU.max))
        link(dve.reciprocal(hrn[:, :], hss[:, :]))
        link(dve.tensor_scalar(hrn[:, :], hrn[:, :], float(F2) ** 0.5, None, ALU.mult))
        dve.wait_ge(S["fin_in"], 32)
        for b in range(NB):
            dve.wait_ge(S["o_mm"], b + 1)
            dve.scalar_tensor_tensor(out=o[:, b, :], in0=ps[0:RB, OB[b], :], scalar=hrn[:, b:b + 1],
                                     in1=b2b[:, :], op0=ALU.mult, op1=ALU.add).then_inc(S["o_sh"], 1)
        for b in range(NB):
            dve.wait_ge(S["o_act"], b + 1)
            dve.tensor_tensor(o[:, b, :], o[:, b, :], x1r[:, b, :], ALU.add).then_inc(S["o_ready"], 1)

    @block.tensor
    def _(pe):
        def three(dst, lh, ll, rh, rl, start, stop):
            pe.matmul(dst, lh, rh, start=start, stop=False)
            pe.matmul(dst, lh, rl, start=False, stop=False)
            return pe.matmul(dst, ll, rh, start=False, stop=stop)

        def transpose_rows(n):
            for b in range(NB):
                pe.wait_ge(S["rows_ready"], n * NB + b + 1)
                for k in range(KB):
                    mm = pe.transpose(ps[:, b, k * RB:(k + 1) * RB], rows[:, b, k * 128:(k + 1) * 128],
                                      ident[0:RB, 0:RB])
                mm.then_inc(S["rows_t"], 1)

        pe.wait_ge(S["consts"], 13)
        transpose_rows(0)

        def column_sums():
            pe.wait_ge(S["blocks_ready"], 1)
            for b in range(NB):
                for c in range(2):
                    dst = ps[0:ET, 5 + c, b * EP:(b + 1) * EP] if b < 4 else ps[0:ET, 7, c * EP:(c + 1) * EP]
                    mm = pe.matmul(dst, inb[:, b, c * ET:(c + 1) * ET], ones[0:EP, 0:EP], start=True, stop=True)
            mm.then_inc(S["cs_mm"], 1)

        def table(r, i, k):
            pe.wait_ge(S["wr_hi"], r + 1)
            pe.wait_ge(S["wr_lo"], r + 1)
            for b in range(NB):
                if first(r):
                    pe.wait_ge(S["xn_lo"], b + 1)
                else:
                    pe.wait_ge(S["hout_ready"], NB * (r - 1) + b + 1)
                cut = slice(b * RB, (b + 1) * RB)
                for kb in range(KB):
                    mm = three(ps[0:RB, b, :], xn_h[:, kb, cut], xn_l[:, kb, cut], wr_h[:, k, kb, :],
                               wr_l[:, k, kb, :], kb == 0, kb == KB - 1 and not final(r, R2))
                mm.then_inc(S["table_mm"], 1)
                if first(r) and b == 1:
                    column_sums()

        table(0, 0, 0)
        pe.wait_ge(S["cs_ready"], 3)
        for b in range(NB):
            q, at = (5, b) if b < 3 else (6, b - 3)
            dst = ps[0:EP, q, at * (MT + 1):(at + 1) * (MT + 1)]
            for c in range(2):
                pe.matmul(dst, cs[:, c, b, :], later_t[:, c, :], start=(c == 0), stop=False)
            mm = pe.matmul(dst[:, 0:MT], later_p[:, :], inb[:, b, :], start=False, stop=True)
        mm.then_inc(S["rank_mm"], 1)
        table(1, 0, 1)
        with pe.Fori(1, R2 // 2) as i:
            table(2 * i, i, 0)
            table(2 * i + 1, i, 1)
        table(R2, R2 // 2, 0)

        pe.wait_ge(S["slot_ready"], 2)

        def tile_blocks(t, n):
            return nc.values_load_multi_w_load_instructions(
                tile_block[0:1, bass.ds(t, n)], engines=[mybir.EngineType.PE], min_val=0, max_val=NB - 1,
                skip_runtime_bounds_check_because="the block is a sum of NB - 1 comparisons")[1]

        def segment(t, i, k, block_of):
            pe.wait_ge(S["hot_ready"], t + 1)
            pe.wait_ge(S["msg_lo"], t + 1)
            dst = ps[0:RB, bass.ds(block_of, 1), :].rearrange("p b d -> p (b d)")
            pe.matmul(dst, hot[:, k, 0:RB], msg_h[:, k, :], start=False, stop=False)
            pe.matmul(dst, hot[:, k, 0:RB], msg_l[:, k, :], start=False, stop=False).then_inc(S["seg_mm"], 1)

        def keys_weights():
            pe.wait_ge(S["lm_in"], 16 * (4 + G))
            pe.wait_ge(S["cols_in"], 16)
            for kb in range(KB):
                for g in range(G):
                    pe.matmul(ps[:, 7, kb * L:(kb + 1) * L], wkt[:, g, kb * 128:(kb + 1) * 128], a1w[:, g, :],
                              start=(g == 0), stop=(g == G - 1))
            for g in range(G):
                mm = pe.matmul(ps[0:L, 6, 0:1], a1w[:, g, :], colc[:, C_BK + g:C_BK + g + 1], start=(g == 0),
                               stop=(g == G - 1))
            mm.then_inc(S["a1_mm"], 1)

        def some(start, i, n):
            blocks = tile_blocks(start, n)
            for k in range(n):
                segment(start + k, i, k, blocks[k])

        some(0, 0, MR)
        with pe.Fori(1, PAUSE) as i:
            some(i * MR, i, MR)
        keys_weights()
        with pe.Fori(PAUSE, MS // MR) as i:
            some(i * MR, i, MR)
        some(MS - MS % MR, MS // MR, MS % MR)
        pe.wait_ge(S["bself_lo"], 1)
        for b in range(NB):
            pe.matmul(ps[0:RB, b, :], ones_r[:, :], bself_h[:, :], start=False, stop=False)
            pe.matmul(ps[0:RB, b, :], ones_r[:, :], bself_l[:, :], start=False, stop=True).then_inc(S["agg_mm"], 1)

        pe.wait_ge(S["x1_ready"], NB)
        transpose_rows(1)

        pe.wait_ge(S["a1_lo"], 1)
        for c in range(2):
            pe.wait_ge(S["xn_lo"], NB + (SC + RB - 1) // RB if c == 0 else 2 * NB)
            for kb in range(KB):
                cut = slice(c * SC, (c + 1) * SC)
                mm = three(ps[0:L, c, 0:SC], a1_h[:, kb, :], a1_l[:, kb, :], xn_h[:, kb, cut], xn_l[:, kb, cut],
                           kb == 0, kb == KB - 1)
        mm.then_inc(S["hid_mm"], 1)
        pe.wait_ge(S["hid_ready"], 1)
        for c in range(2):
            mm = pe.matmul(ps[0:L, 2 + c, 0:SC], a2w[:, :], hid[:, c * SC:(c + 1) * SC], start=True, stop=True)
        mm.then_inc(S["wt_mm"], 1)
        pe.wait_ge(S["wt_ready"], 2)
        for b in range(NB):
            mm = pe.transpose(ps[0:RB, 4, b * L:(b + 1) * L], wt[:, b * RB:(b + 1) * RB], ident[0:L, 0:L])
        mm.then_inc(S["wt_t"], 1)
        pe.wait_ge(S["wt2_ready"], 1)
        for b in range(NB):
            mm = pe.transpose(ps[0:RB, 5, b * L:(b + 1) * L], wt2[:, b * RB:(b + 1) * RB], ident[0:L, 0:L])
        mm.then_inc(S["wt_t"], 1)
        pe.wait_ge(S["w_ready"], 1)
        for kb in range(KB):
            for b in range(NB):
                mm = pe.matmul(ps[:, 7, kb * L:(kb + 1) * L], rows[:, b, kb * 128:(kb + 1) * 128], w[:, b, :],
                               start=(b == 0), stop=(b == NB - 1))
        mm.then_inc(S["lm_mm"], 1)
        for b in range(NB):
            pe.matmul(ps[:, 6, 0:L], ones[0:RB, :], w[:, b, :], start=(b == 0), stop=(b == NB - 1))
        for b in range(NB):
            mm = pe.matmul(ps[0:L, 6, 128:129], w[:, b, :], ones[0:RB, 0:1], start=(b == 0), stop=(b == NB - 1))
        mm.then_inc(S["lm_mm"], 1)
        pe.wait_ge(S["ct_ready"], 1)
        pe.wait_ge(S["kv_in"], 16 * (KB + 1))
        for g in range(G):
            for kb in range(KB):
                mm = pe.matmul(ps[:, g // 4, (g % 4) * L:(g % 4 + 1) * L], wkv[:, kb, g * DK:(g + 1) * DK],
                               ct[:, kb, :], start=(kb == 0), stop=(kb == KB - 1))
            if g % 4 == 3:
                mm.then_inc(S["kc_mm"], 1)
        for c in range(2):
            for kb in range(KB):
                mm = pe.matmul(ps[0:L, 2 + c, :], ct[:, kb, :], wkv[:, kb, G * DK + c * 512:G * DK + (c + 1) * 512],
                               start=(kb == 0), stop=(kb == KB - 1))
        mm.then_inc(S["vc_mm"], 1)
        pe.wait_ge(S["kf_ready"], 1)
        for g in range(G):
            mm = pe.matmul(ps[0:HG, 4 + g // 4, (g % 4) * L:(g % 4 + 1) * L],
                           colc[:, C_BQ + g * HG:C_BQ + (g + 1) * HG], kf[:, g, :], start=True, stop=True)
        mm.then_inc(S["bq_mm"], 1)

        def queries(v, kb):
            if kb == 0:
                pe.wait_ge(S["wq_lo"], HU * (v + 1))
            if kb >= 2 or not first(v):
                pe.wait_ge(S["p_sum"], KB * v + kb - (1 if first(v) else 0))
            g = v // UG
            cut = slice(kb * 128, (kb + 1) * 128)
            for h in range(HU):
                at = (2 * (kb % 2) if first(v) else 4) + h // 2
                dst = ps[:, at, (h % 2) * 2 * L:(h % 2 + 1) * 2 * L]
                both = kc[:, bass.ds(g, 1), :, :].rearrange("p g a l -> p (g a l)")
                pe.matmul(dst, wq_h[:, h, cut], both, start=True, stop=False)
                mm = pe.matmul(dst[:, 0:L], wq_l[:, h, cut],
                               kc[:, bass.ds(g, 1), 0, :].rearrange("p g l -> p (g l)"), start=False, stop=True)
            mm.then_inc(S["p_mm"], 1)

        pe.wait_ge(S["kc_lo"], 1)
        pe.wait_ge(S["vf_ready"], 1)
        for kb in range(KB):
            queries(0, kb)
        pe.wait_ge(S["lm_done"], 1)

        def hidden(v, k, n):
            f, c = n // 2, n % 2
            half, at = f // (FB // 2), f % (FB // 2)
            if n == 0:
                pe.wait_ge(S["z_lo"], HU * (v + 1))
            if n % HH == 0:
                pe.wait_ge(S["w1_lo"], HU * (2 * v + half + 1))
            if n == 0:
                if not first(v):
                    pe.wait_ge(S["h_acc"], HO * v)
            elif n > 1:
                pe.wait_ge(S["h_acc"], HO * v + n - 1)
            cut, cols = slice(c * SC, (c + 1) * SC), slice(at * 128, (at + 1) * 128)
            for h in range(HU):
                mm = three(ps[:, 2 + n % 2, 0:SC], w1_h[half][:, h, cols], w1_l[half][:, h, cols],
                           z_h[k][:, h, cut], z_l[k][:, h, cut], h == 0, h == HU - 1)
            mm.then_inc(S["h_mm"], 1)

        def unit_step(v, k):
            def scores(j):
                q = NB * v + j
                if j == 0:
                    pe.wait_ge(S["p_lo"], KB * (v + 1))
                if j >= 2:
                    pe.wait_ge(S["biased"], q - 1)
                elif not first(v):
                    pe.wait_ge(S["biased"], NB * v)
                dst = ps[0:RB, j % 2, 0:UC]
                cut = slice(j * RB, (j + 1) * RB)
                for kb in range(KB):
                    mm = three(dst, xn_h[:, kb, cut], xn_l[:, kb, cut], p_h[:, kb, :], p_l[:, kb, :], kb == 0,
                               kb == KB - 1)
                mm.then_inc(S["score_mm"], 1)

            def turn(j):
                q = NB * v + j
                pe.wait_ge(S["prob_ready"], q + 1)
                if j > 0 or not first(v):
                    pe.wait_ge(S["att_lo"], q)
                for h in range(HU):
                    mm = pe.transpose(ps[0:L, 6, h * RB:(h + 1) * RB], prob[:, j % SR, h * L:(h + 1) * L],
                                      ident[0:RB, 0:RB])
                mm.then_inc(S["prob_t"], 1)

            def values(h):
                q = HU * v + h
                if h == 0:
                    pe.wait_ge(S["att_lo"], NB * (v + 1))
                    pe.wait_ge(S["unit_cols"], 3 * (v + 1))
                if h == 1 and not final(v, U - 1):
                    pe.wait_ge(S["p_sum"], KB * (v + 2))
                if h >= 2:
                    pe.wait_ge(S["z_lo"], q - 1)
                    pe.wait_ge(S["z_sq"], q - 1)
                for c in range(2):
                    cut = slice(c * SC, (c + 1) * SC)
                    mm = three(z_banks(h)[:, c, :], vcu_h[:, :], vcu_l[:, :], at_h[:, h, cut], at_l[:, h, cut],
                               True, True)
                mm.then_inc(S["z_mm"], 1)

            def h1(n):
                if not first(v):
                    hidden(v - 1, 1 - k, n)

            def p(kb):
                if not final(v, U - 1):
                    queries(v + 1, kb)

            scores(0)
            h1(0)
            scores(1)
            h1(1)
            h1(2)
            turn(0)
            scores(2)
            h1(3)
            h1(4)
            turn(1)
            scores(3)
            h1(5)
            turn(2)
            scores(4)
            h1(6)
            p(0)
            h1(7)
            turn(3)
            p(1)
            h1(8)
            turn(4)
            p(2)
            h1(9)
            h1(10)
            values(0)
            p(3)
            h1(11)
            h1(12)
            values(1)
            h1(13)
            values(2)
            h1(14)
            values(3)
            h1(15)

        over_units(pe, unit_step)

        def outputs(f):
            pe.wait_ge(S["ht_lo"], f + 1)
            if f == 0:
                pe.wait_ge(S["w2_lo"], FB)
                pe.wait_ge(S["n_sd"], 1)
            for b in range(NB):
                cut = slice(b * RB, (b + 1) * RB)
                mm = three(ps[0:RB, OB[b], :], ht_h[:, f, cut], ht_l[:, f, cut], w2_h[:, f, :], w2_l[:, f, :],
                           f == 0, f == FB - 1)
                if f == FB - 1:
                    mm.then_inc(S["o_mm"], 1)

        for n in range(HO):
            hidden(U - 1, 1, n)
            if n == 1:
                pe.wait_ge(S["z_acc"], HU * U + 1)
                pe.wait_ge(S["biased"], NB * U)
                for c in range(2):
                    mm = pe.matmul(ps[:, c, 0:SC], ones[:, :], zacc[:, c * SC:(c + 1) * SC], start=True, stop=True)
                mm.then_inc(S["n_mm"], 1)
            if n in (11, 13):
                outputs((n - 11) // 2)
        for f in range(2, FB - 2):
            outputs(f)
        pe.wait_ge(S["h1_sum"], FB)
        for b in range(NB):
            mm = pe.matmul(ps[0:RB, 1, b:b + 1], zacc[:, b * RB:(b + 1) * RB], ones[:, 0:1], start=True, stop=True)
        mm.then_inc(S["ss_mm"], 1)
        outputs(FB - 2)
        outputs(FB - 1)

    ctx.close()


def kernel(**inputs):
    import numpy as np
    import concourse.bacc as bacc
    from concourse.bass_utils import run_bass_kernel_spmd

    a = {k: np.asarray(v) for k, v in inputs.items()}
    f = "L0_ffn_"

    def by_partition(m):
        return m.reshape(-1, 128, m.shape[-1]).transpose(1, 0, 2)

    def col(v):
        return v.reshape(-1, 128).T

    w_rel = np.concatenate([a["L0_gnn_W_rel"], a["L0_gnn_W_self"][None]], 0).transpose(0, 2, 1)
    data = {
        "x": a["x"], "src": a["src"], "dst": a["dst"], "etype": a["edge_type_8"],
        "w_rel_t": w_rel.reshape(R2 + 1, KB, 128, D).transpose(0, 2, 1, 3).reshape(R2 + 1, 128, KB * D),
        "b_rel": np.concatenate([a["L0_gnn_b_rel"], a["L0_gnn_b_self"][None]], 0),
        "cols": np.concatenate([col(a[f + "gamma_norm"]), col(a[f + "wz_g2"]), col(a[f + "Wkv_b"][:G * DK]),
                                col(a[f + "Wq_b"]), col(a[f + "wz_g1"]), col(a[f + "wz_b1"])], 1),
        "wk_t": by_partition(a[f + "Wkv_w"][:, :G * DK].T),
        "w_kv": by_partition(a[f + "Wkv_w"]),
        "aw1": by_partition(a[f + "aw1_w"]), "aw1_b": a[f + "aw1_b"][:, None],
        "aw2": a[f + "aw2_w"], "aw2_b": a[f + "aw2_b"][:, None],
        "b_v": a[f + "Wkv_b"][None, G * DK:],
        "wq_t": a[f + "Wq_w"].T.reshape(U, HU, 128, D).transpose(0, 2, 1, 3).reshape(U, 128, HU * D),
        "wz_w1": a[f + "wz_w1"].reshape(U, HU, 128, 2, FH).transpose(0, 3, 2, 1, 4).reshape(U, 2, 128, HU * FH),
        "w2": by_partition(a[f + "wz_w2"]), "b2": a[f + "wz_b2"][None],
    }
    nc = bacc.Bacc("TRN2", target_bir_lowering=False, num_devices=1)
    arrays, args = {}, []
    for name, v in data.items():
        v = np.ascontiguousarray(v)
        arrays[f"in_{name}"] = v
        args.append(nc.dram_tensor(f"in_{name}", v.shape, mybir.dt.from_np(v.dtype), kind="ExternalInput").ap())
    args.append(nc.dram_tensor("out", (N, D), F32, kind="ExternalOutput").ap())
    build_layer(nc, *args)
    r = run_bass_kernel_spmd(nc, [arrays], core_ids=[0])
    return r.results[0]["out"]
```
